# Optimizing a Trainium2 kernel written in Bass

```python
import numpy as np
import jax
import jax.numpy as jnp

def _softmax(x, axis=-1):
    return jax.nn.softmax(x, axis=axis)

def _gelu(x):
    return jax.nn.gelu(x, approximate=True)

def _silu(x):
    return jax.nn.silu(x)

def _sigmoid(x):
    return jax.nn.sigmoid(x)

def _layernorm(x, axis=-1, eps=1e-05):
    m = jnp.mean(x, axis=axis, keepdims=True)
    v = jnp.var(x, axis=axis, keepdims=True)
    return (x - m) / jnp.sqrt(v + eps)

def _scatter_add(tgt, idx, src, axis=0):
    return tgt.at[idx].add(src)

def _segment_sum(src, seg, n):
    return jax.ops.segment_sum(src, seg, n)
kernel_name = 'mk_hybrid_d1_jaxref_r8_73b810'

def setup_inputs(seed: int=0):
    np.random.seed(seed)
    _w = jnp.asarray

    def _L0_attn_a_setup():
        import math
        import jax, jax.numpy as jnp
        import numpy as np
        L, D, H, F = (4, 128, 16, 512)
        HD = D // H
        EPS = 1e-05

        def get_alibi_slopes(num_heads):
            closest = 2 ** math.floor(math.log2(num_heads))
            base = 2 ** (-2 ** (-(math.log2(closest) - 3)))
            slopes = base ** np.arange(1, closest + 1)
            if closest != num_heads:
                extra_base = 2 ** (-2 ** (-(math.log2(2 * closest) - 3)))
                extra = extra_base ** np.arange(1, 2 * (num_heads - closest) + 1, 2)
                slopes = np.concatenate([slopes, extra])
            return jnp.asarray(slopes, dtype=jnp.float32)

        def build_mask(num_heads, T):
            pos = jnp.arange(T)
            dist = pos[None, :] - pos[:, None]
            alibi = get_alibi_slopes(num_heads)[:, None, None] * dist[None]
            causal = jnp.where(dist > 0, -jnp.inf, 0.0).astype(jnp.float32)
            return causal[None] + alibi

        def layer_norm(x, w, b):
            mu = jnp.mean(x, axis=-1, keepdims=True)
            var = jnp.mean(jnp.square(x - mu), axis=-1, keepdims=True)
            return (x - mu) * jax.lax.rsqrt(var + EPS) * w + b

        def mha(x, mask, Wi, bi, Wo, bo):
            B, T, _ = x.shape
            qkv = x @ Wi.T + bi
            q, k, v = jnp.split(qkv, 3, axis=-1)
            q = q.reshape(B, T, H, HD).transpose(0, 2, 1, 3)
            k = k.reshape(B, T, H, HD).transpose(0, 2, 1, 3)
            v = v.reshape(B, T, H, HD).transpose(0, 2, 1, 3)
            scores = jnp.einsum('bhqd,bhkd->bhqk', q, k) / math.sqrt(HD)
            scores = scores + mask[None]
            attn = jax.nn.softmax(scores, axis=-1)
            out = jnp.einsum('bhqk,bhkd->bhqd', attn, v)
            out = out.transpose(0, 2, 1, 3).reshape(B, T, D)
            return out @ Wo.T + bo
        key = jax.random.key(seed)
        ks = jax.random.split(key, 13)
        s = 0.02
        inp = {'x': jax.random.normal(ks[0], (2, 256, D), dtype=jnp.float32), 'in_proj_w': jax.random.normal(ks[1], (L, 3 * D, D), dtype=jnp.float32) * s, 'in_proj_b': jnp.zeros((L, 3 * D), dtype=jnp.float32), 'out_proj_w': jax.random.normal(ks[2], (L, D, D), dtype=jnp.float32) * s, 'out_proj_b': jnp.zeros((L, D), dtype=jnp.float32), 'ffn1_w': jax.random.normal(ks[3], (L, F, D), dtype=jnp.float32) * s, 'ffn1_b': jnp.zeros((L, F), dtype=jnp.float32), 'ffn2_w': jax.random.normal(ks[4], (L, D, F), dtype=jnp.float32) * s, 'ffn2_b': jnp.zeros((L, D), dtype=jnp.float32), 'ln1_w': jnp.ones((L, D), dtype=jnp.float32), 'ln1_b': jnp.zeros((L, D), dtype=jnp.float32), 'ln2_w': jnp.ones((L, D), dtype=jnp.float32), 'ln2_b': jnp.zeros((L, D), dtype=jnp.float32), 'final_w': jnp.ones((D,), dtype=jnp.float32), 'final_b': jnp.zeros((D,), dtype=jnp.float32)}
        return inp
    _L0_attn_a_in = _L0_attn_a_setup()

    def _L0_attn_b_setup():
        import jax, jax.numpy as jnp
        import numpy as np
        D_MODEL = 128
        NUM_HEADS = 16
        D_K = D_MODEL // NUM_HEADS
        ROPE_THETA = 10000.0
        MAX_SEQ_LEN = 256

        def _rope_tables():
            dim_index = jnp.arange(D_K // 2, dtype=jnp.float32)
            pos = jnp.arange(MAX_SEQ_LEN, dtype=jnp.float32)
            theta_inv = ROPE_THETA ** (-2.0 * dim_index / D_K)
            ang = pos[:, None] * theta_inv[None, :]
            return (jnp.sin(ang), jnp.cos(ang))

        def _apply_rope(x, positions, sin, cos):
            s = sin[positions]
            c = cos[positions]
            x_even = x[..., ::2]
            x_odd = x[..., 1::2]
            y_even = x_even * c - x_odd * s
            y_odd = x_even * s + x_odd * c
            y = jnp.stack([y_even, y_odd], axis=-1)
            return y.reshape(x.shape)
        key = jax.random.key(seed)
        k0, k1, k2, k3, k4 = jax.random.split(key, 5)
        std = np.sqrt(2.0 / (D_MODEL + D_MODEL))
        in_features = jax.random.normal(k0, (2, 256, D_MODEL), dtype=jnp.float32)
        W_q = jax.random.normal(k1, (D_MODEL, D_MODEL), dtype=jnp.float32) * std
        W_k = jax.random.normal(k2, (D_MODEL, D_MODEL), dtype=jnp.float32) * std
        W_v = jax.random.normal(k3, (D_MODEL, D_MODEL), dtype=jnp.float32) * std
        W_o = jax.random.normal(k4, (D_MODEL, D_MODEL), dtype=jnp.float32) * std
        return {'in_features': in_features, 'W_q': W_q, 'W_k': W_k, 'W_v': W_v, 'W_o': W_o}
    _L0_attn_b_in = _L0_attn_b_setup()

    def _L0_ffn_setup():
        import jax, jax.numpy as jnp
        import numpy as np
        import math
        MAX_NORM = 0.95
        CURVATURE = 1.0
        TOP_K = 2
        EPS = 1e-07

        def _project_to_ball(x):
            norm = jnp.clip(jnp.linalg.norm(x, axis=-1, keepdims=True), EPS, None)
            scale = jnp.where(norm > MAX_NORM, MAX_NORM / norm, jnp.ones_like(norm))
            return x * scale
        key = jax.random.key(seed)
        ks = jax.random.split(key, 8)
        B, N, D, E, F = (2, 256, 128, 8, 512)
        x = jax.random.normal(ks[0], (B, N, D), dtype=jnp.float32)
        c = jax.random.normal(ks[1], (E, D), dtype=jnp.float32)
        centroids = c / jnp.linalg.norm(c, axis=-1, keepdims=True) * 0.5
        Wp = jax.random.normal(ks[2], (D, D), dtype=jnp.float32) * 0.02
        bp = jnp.zeros((D,), dtype=jnp.float32)
        W1 = jax.random.normal(ks[3], (E, D, F), dtype=jnp.float32) * 0.02
        b1 = jnp.zeros((E, F), dtype=jnp.float32)
        W2 = jax.random.normal(ks[4], (E, F, D), dtype=jnp.float32) * 0.02
        b2 = jnp.zeros((E, D), dtype=jnp.float32)
        return {'x': x, 'centroids': centroids, 'Wp': Wp, 'bp': bp, 'W1': W1, 'b1': b1, 'W2': W2, 'b2': b2}
    _L0_ffn_in = _L0_ffn_setup()
    _d = {'L0_attn_a_x': _L0_attn_a_in['x'], 'L0_attn_a_in_proj_w': _L0_attn_a_in['in_proj_w'], 'L0_attn_a_in_proj_b': _L0_attn_a_in['in_proj_b'], 'L0_attn_a_out_proj_w': _L0_attn_a_in['out_proj_w'], 'L0_attn_a_out_proj_b': _L0_attn_a_in['out_proj_b'], 'L0_attn_a_ffn1_w': _L0_attn_a_in['ffn1_w'], 'L0_attn_a_ffn1_b': _L0_attn_a_in['ffn1_b'], 'L0_attn_a_ffn2_w': _L0_attn_a_in['ffn2_w'], 'L0_attn_a_ffn2_b': _L0_attn_a_in['ffn2_b'], 'L0_attn_a_ln1_w': _L0_attn_a_in['ln1_w'], 'L0_attn_a_ln1_b': _L0_attn_a_in['ln1_b'], 'L0_attn_a_ln2_w': _L0_attn_a_in['ln2_w'], 'L0_attn_a_ln2_b': _L0_attn_a_in['ln2_b'], 'L0_attn_a_final_w': _L0_attn_a_in['final_w'], 'L0_attn_a_final_b': _L0_attn_a_in['final_b'], 'L0_attn_b_W_q': _L0_attn_b_in['W_q'], 'L0_attn_b_W_k': _L0_attn_b_in['W_k'], 'L0_attn_b_W_v': _L0_attn_b_in['W_v'], 'L0_attn_b_W_o': _L0_attn_b_in['W_o'], 'L0_ffn_centroids': _L0_ffn_in['centroids'], 'L0_ffn_Wp': _L0_ffn_in['Wp'], 'L0_ffn_bp': _L0_ffn_in['bp'], 'L0_ffn_W1': _L0_ffn_in['W1'], 'L0_ffn_b1': _L0_ffn_in['b1'], 'L0_ffn_W2': _L0_ffn_in['W2'], 'L0_ffn_b2': _L0_ffn_in['b2']}
    _x0 = _d['L0_attn_a_x']
    _d['L0_attn_a_x'] = jax.random.normal(jax.random.fold_in(jax.random.key(seed), 1), (8, 512, 128), dtype=_x0.dtype)
    del _x0
    return _d

def reference(L0_attn_a_x, L0_attn_a_in_proj_w, L0_attn_a_in_proj_b, L0_attn_a_out_proj_w, L0_attn_a_out_proj_b, L0_attn_a_ffn1_w, L0_attn_a_ffn1_b, L0_attn_a_ffn2_w, L0_attn_a_ffn2_b, L0_attn_a_ln1_w, L0_attn_a_ln1_b, L0_attn_a_ln2_w, L0_attn_a_ln2_b, L0_attn_a_final_w, L0_attn_a_final_b, L0_attn_b_W_q, L0_attn_b_W_k, L0_attn_b_W_v, L0_attn_b_W_o, L0_ffn_centroids, L0_ffn_Wp, L0_ffn_bp, L0_ffn_W1, L0_ffn_b1, L0_ffn_W2, L0_ffn_b2):

    def _L0_attn_a_ref(x, in_proj_w, in_proj_b, out_proj_w, out_proj_b, ffn1_w, ffn1_b, ffn2_w, ffn2_b, ln1_w, ln1_b, ln2_w, ln2_b, final_w, final_b):
        import math
        import jax, jax.numpy as jnp
        import numpy as np
        L, D, H, F = (4, 128, 16, 512)
        HD = D // H
        EPS = 1e-05

        def get_alibi_slopes(num_heads):
            closest = 2 ** math.floor(math.log2(num_heads))
            base = 2 ** (-2 ** (-(math.log2(closest) - 3)))
            slopes = base ** np.arange(1, closest + 1)
            if closest != num_heads:
                extra_base = 2 ** (-2 ** (-(math.log2(2 * closest) - 3)))
                extra = extra_base ** np.arange(1, 2 * (num_heads - closest) + 1, 2)
                slopes = np.concatenate([slopes, extra])
            return jnp.asarray(slopes, dtype=jnp.float32)

        def build_mask(num_heads, T):
            pos = jnp.arange(T)
            dist = pos[None, :] - pos[:, None]
            alibi = get_alibi_slopes(num_heads)[:, None, None] * dist[None]
            causal = jnp.where(dist > 0, -jnp.inf, 0.0).astype(jnp.float32)
            return causal[None] + alibi

        def layer_norm(x, w, b):
            mu = jnp.mean(x, axis=-1, keepdims=True)
            var = jnp.mean(jnp.square(x - mu), axis=-1, keepdims=True)
            return (x - mu) * jax.lax.rsqrt(var + EPS) * w + b

        def mha(x, mask, Wi, bi, Wo, bo):
            B, T, _ = x.shape
            qkv = x @ Wi.T + bi
            q, k, v = jnp.split(qkv, 3, axis=-1)
            q = q.reshape(B, T, H, HD).transpose(0, 2, 1, 3)
            k = k.reshape(B, T, H, HD).transpose(0, 2, 1, 3)
            v = v.reshape(B, T, H, HD).transpose(0, 2, 1, 3)
            scores = jnp.einsum('bhqd,bhkd->bhqk', q, k) / math.sqrt(HD)
            scores = scores + mask[None]
            attn = jax.nn.softmax(scores, axis=-1)
            out = jnp.einsum('bhqk,bhkd->bhqd', attn, v)
            out = out.transpose(0, 2, 1, 3).reshape(B, T, D)
            return out @ Wo.T + bo
        T = x.shape[1]
        mask = build_mask(H, T)
        for i in range(L):
            xn = layer_norm(x, ln1_w[i], ln1_b[i])
            x = x + mha(xn, mask, in_proj_w[i], in_proj_b[i], out_proj_w[i], out_proj_b[i])
            xn = layer_norm(x, ln2_w[i], ln2_b[i])
            h = jax.nn.gelu(xn @ ffn1_w[i].T + ffn1_b[i], approximate=False)
            x = x + (h @ ffn2_w[i].T + ffn2_b[i])
        return layer_norm(x, final_w, final_b)

    def _L0_attn_b_ref(in_features, W_q, W_k, W_v, W_o):
        import jax, jax.numpy as jnp
        import numpy as np
        D_MODEL = 128
        NUM_HEADS = 16
        D_K = D_MODEL // NUM_HEADS
        ROPE_THETA = 10000.0
        MAX_SEQ_LEN = 256

        def _rope_tables():
            dim_index = jnp.arange(D_K // 2, dtype=jnp.float32)
            pos = jnp.arange(MAX_SEQ_LEN, dtype=jnp.float32)
            theta_inv = ROPE_THETA ** (-2.0 * dim_index / D_K)
            ang = pos[:, None] * theta_inv[None, :]
            return (jnp.sin(ang), jnp.cos(ang))

        def _apply_rope(x, positions, sin, cos):
            s = sin[positions]
            c = cos[positions]
            x_even = x[..., ::2]
            x_odd = x[..., 1::2]
            y_even = x_even * c - x_odd * s
            y_odd = x_even * s + x_odd * c
            y = jnp.stack([y_even, y_odd], axis=-1)
            return y.reshape(x.shape)
        B, S, _ = in_features.shape
        sin, cos = _rope_tables()
        positions = jnp.arange(S)

        def proj(W):
            y = jnp.einsum('bsd,od->bso', in_features, W)
            return y.reshape(B, S, NUM_HEADS, D_K).transpose(0, 2, 1, 3)
        Q = _apply_rope(proj(W_q), positions, sin, cos)
        K = _apply_rope(proj(W_k), positions, sin, cos)
        V = proj(W_v)
        scores = jnp.einsum('bhnd,bhmd->bhnm', Q, K) / jnp.sqrt(jnp.float32(D_K))
        causal = jnp.tril(jnp.ones((S, S), dtype=bool))
        scores = jnp.where(causal[None, None], scores, -jnp.inf)
        attn = jax.nn.softmax(scores, axis=-1)
        head = jnp.einsum('bhnm,bhmd->bhnd', attn, V)
        head = head.transpose(0, 2, 1, 3).reshape(B, S, D_MODEL)
        return jnp.einsum('bso,do->bsd', head, W_o.T.T) if False else jnp.einsum('bsi,oi->bso', head, W_o)

    def _L0_ffn_ref(x, centroids, Wp, bp, W1, b1, W2, b2):
        import jax, jax.numpy as jnp
        import numpy as np
        import math
        MAX_NORM = 0.95
        CURVATURE = 1.0
        TOP_K = 2
        EPS = 1e-07

        def _project_to_ball(x):
            norm = jnp.clip(jnp.linalg.norm(x, axis=-1, keepdims=True), EPS, None)
            scale = jnp.where(norm > MAX_NORM, MAX_NORM / norm, jnp.ones_like(norm))
            return x * scale
        B, N, D = x.shape
        E = centroids.shape[0]
        x_hyper = _project_to_ball(x @ Wp + bp)
        c_proj = _project_to_ball(centroids)
        x_norm_sq = jnp.sum(x_hyper * x_hyper, axis=-1)
        c_norm_sq = jnp.sum(c_proj * c_proj, axis=-1)
        x_norm_sq = jnp.clip(x_norm_sq, None, 0.99)
        c_norm_sq = jnp.clip(c_norm_sq, None, 0.99)
        dot = jnp.einsum('bnd,ed->bne', x_hyper, c_proj)
        diff_sq = jnp.maximum(x_norm_sq[..., None] + c_norm_sq - 2.0 * dot, 0.0)
        denom = (1.0 - x_norm_sq)[..., None] * (1.0 - c_norm_sq) + EPS
        arg = jnp.clip(1.0 + 2.0 * diff_sq / denom, 1.0 + EPS, None)
        dist = jnp.arccosh(arg)
        routing_logits = -dist / math.sqrt(CURVATURE)
        top_v, top_i = jax.lax.top_k(routing_logits, TOP_K)
        top_w = jax.nn.softmax(top_v, axis=-1)
        comb = jnp.sum(jax.nn.one_hot(top_i, E, dtype=x.dtype) * top_w[..., None], axis=2)
        h = jax.nn.gelu(jnp.einsum('bnd,edf->bnef', x, W1) + b1, approximate=False)
        y = jnp.einsum('bnef,efd->bned', h, W2) + b2
        out = jnp.einsum('bne,bned->bnd', comb, y)
        return out
    x = L0_attn_a_x
    x = x + _L0_attn_a_ref(_layernorm(x, axis=-1), L0_attn_a_in_proj_w, L0_attn_a_in_proj_b, L0_attn_a_out_proj_w, L0_attn_a_out_proj_b, L0_attn_a_ffn1_w, L0_attn_a_ffn1_b, L0_attn_a_ffn2_w, L0_attn_a_ffn2_b, L0_attn_a_ln1_w, L0_attn_a_ln1_b, L0_attn_a_ln2_w, L0_attn_a_ln2_b, L0_attn_a_final_w, L0_attn_a_final_b)
    x = x + _L0_ffn_ref(_layernorm(x, axis=-1), L0_ffn_centroids, L0_ffn_Wp, L0_ffn_bp, L0_ffn_W1, L0_ffn_b1, L0_ffn_W2, L0_ffn_b2)
    x = x + _L0_attn_b_ref(_layernorm(x, axis=-1), L0_attn_b_W_q, L0_attn_b_W_k, L0_attn_b_W_v, L0_attn_b_W_o)
    x = x + _L0_ffn_ref(_layernorm(x, axis=-1), L0_ffn_centroids, L0_ffn_Wp, L0_ffn_bp, L0_ffn_W1, L0_ffn_b1, L0_ffn_W2, L0_ffn_b2)
    return x

_drawn_inputs = setup_inputs


def setup_inputs(seed=0):
    import zlib

    import numpy as np

    out = dict(_drawn_inputs(seed))
    spreads = {'L0_attn_a_in_proj_b': (0.0, 0.267),
     'L0_attn_a_out_proj_b': (0.0, 0.1),
     'L0_attn_a_ffn1_b': (0.0, 0.1),
     'L0_attn_a_ffn2_b': (0.0, 0.1),
     'L0_attn_a_ln1_w': (1.0, 0.6),
     'L0_attn_a_ln1_b': (0.0, 0.8),
     'L0_attn_a_ln2_w': (1.0, 0.6),
     'L0_attn_a_ln2_b': (0.0, 0.8),
     'L0_attn_a_final_w': (1.0, 0.2),
     'L0_attn_a_final_b': (0.0, 0.1),
     'L0_ffn_bp': (0.0, 0.1),
     'L0_ffn_b1': (0.0, 0.441),
     'L0_ffn_b2': (0.0, 0.1)}
    factors = {'L0_attn_a_in_proj_w': 2.745}
    for name, (base, spread) in spreads.items():
        noise = np.random.default_rng([zlib.crc32(name.encode()), seed]).standard_normal(out[name].shape)
        drawn = base * np.exp(spread * noise) if base else spread * noise
        out[name] = jnp.asarray(drawn.astype(out[name].dtype))
    for name, factor in factors.items():
        out[name] = (out[name] * factor).astype(out[name].dtype)
    return out
```

```python
import math
from contextlib import ExitStack

import numpy as np

import concourse.bass as bass
from concourse import mybir

F32 = mybir.dt.float32
BF16 = mybir.dt.bfloat16
ALU = mybir.AluOpType
ACT = mybir.ActivationFunctionType
AX = mybir.AxisListType

P = 128
D = 128
T = 512
TT = T // P
JOBS = 8
H, HD = 16, 8
LAYERS = 4
FT = 4
E = 8
EPS = 1e-5
NEG = -3.0e38

NPART = 3
ROW_ALIBI = NPART * NPART * HD
N_ALIBI = 12
ROW_MAX = 96
ROWS = ROW_MAX + NPART
LOADS = NPART + NPART * NPART
PAIRS = H // 2
QUADS = H // 4
CPP = 5
CHUNKS = PAIRS * CPP
CPQ = 2 * CPP
HCOLS = 1280
SKEW = 2 * CPP

AP_QKV, AP_WO, AP_BV, AP_BO, AP_COL, AP_N = 0, 384, 512, 640, 768, 772
FP_W1, FP_W2, FP_B2, FP_COL, FP_N = 0, 512, 1024, 1152, 1158
BP_N = 6 * D
MP_C, MP_WP, MP_BP, MP_B1, MP_N = 0, 8, 136, 137, 137 + 32


def _plain(eng):
    eng.get_value_cache().nocache = True


def hybrid_kernel(nc, x, apack, fpack, final, bpack, mpack, b2e, w1e, w2e,
                  alibi, rope, out, part_scr):
    ctx = ExitStack()
    with ctx:
        def sb(name, shape, dt=F32):
            return ctx.enter_context(nc.sbuf_tensor(name, shape, dt))

        def sem(name):
            return ctx.enter_context(nc.semaphore(name))

        xs = sb("xs", [P, JOBS * TT, D])
        ident = sb("ident", [P, P])
        ident_b = sb("ident_b", [P, P], BF16)
        mask_a = sb("mask_a", [P, P], BF16)
        mask_b = sb("mask_b", [P, P], BF16)
        half = sb("half", [P, TT])
        mhalf = sb("mhalf", [P, TT])
        ones = sb("ones", [P, P])
        tri = sb("tri", [P, E, E])
        ap_sb = sb("ap_sb", [P, AP_N])
        fp_sb = sb("fp_sb", [P, FP_N])
        fin_sb = sb("fin_sb", [P, 2 * D])
        bp_sb = sb("bp_sb", [P, BP_N])
        mp_sb = sb("mp_sb", [P, MP_N])
        b2_sb = sb("b2_sb", [E, D])
        rope_sb = sb("rope_sb", [P, 4, T])
        bqs = sb("bqs", [P, 1])
        stats = sb("stats", [P, TT, 6])
        mv = sb("mv", [P, TT, 2])
        veps = sb("veps", [P, TT])
        rstd = sb("rstd", [P, TT])
        xn = sb("xn", [P, TT, D])
        xnT = sb("xnT", [P, T])
        xnT2 = sb("xnT2", [P, T])
        qk = sb("qk", [P, 2, T])
        resid = sb("resid", [P, 2, T])
        rtmp = sb("rtmp", [P, 2, T])
        parts = sb("parts", [P, 2, NPART, T], BF16)
        QS = [sb(f"QS{i}", [P, H, T], BF16) for i in range(2)]
        KS = [sb(f"KS{i}", [P, H, T], BF16) for i in range(2)]
        V = [sb(f"V{i}", [P, TT, H, HD + 1]) for i in range(3)]
        big = sb("big", [P, 12288])
        Pq = [big[:, n * 4 * HCOLS:(n + 1) * 4 * HCOLS].rearrange("p (h c) -> p h c", h=4) for n in range(2)]
        W1 = big[:, 0:4096].rearrange("p (e f) -> p e f", e=E)
        W2 = big[:, 4096:8192].rearrange("p (e f d) -> p e f d", e=E, f=FT)
        hT = [big[:, 8192 + 2048 * n:8192 + 2048 * (n + 1)].rearrange("p (f t) -> p f t", f=FT) for n in range(2)]
        mx = sb("mx", [P, H, 10])
        mneg = sb("mneg", [P, TT, H])
        mres = sb("mres", [P, TT, H])
        mparts = sb("mparts", [P, TT, P], BF16)
        mT = sb("mT", [NPART * H, T], BF16)
        spare = sb("spare", [P, 4])
        OT = sb("OT", [P, QUADS, T])
        rl = sb("rl", [P, H])
        attn = sb("attn", [P, TT, D])
        attnT = sb("attnT", [P, T])
        xload = resid[:].rearrange("p k (t d) -> p k t d", t=TT)
        xpT, sqT = qk[:, 0, :], qk[:, 1, :]
        cproj = sb("cproj", [P, E])
        cn = sb("cn", [P, 3, E])
        R = sb("R", [P, TT, E + 1])
        s4 = sb("s4", [P, 12, TT])
        s8 = sb("s8", [P, 10, TT, E])
        s88 = OT[:, 0:2, :].rearrange("p g c -> p (g c)")[:, 0:3 * TT * E * E].rearrange(
            "p (i t e) -> p i t e", i=3, t=TT)
        comb = [sb(f"comb{n}", [P, TT, E]) for n in range(2)]
        combT = sb("combT", [E, T])

        bank = [ctx.enter_context(nc.psum_tensor(f"bank{i}", [P, T], F32)) for i in range(8)]
        bankA, bankB = bank[0:2], bank[2:5]
        bankPV, bankF, bankR = bank[5], bank[6], bank[7]
        mT_ps = bankR[:, 0:T // 2].bitcast(BF16)
        bankH, bankY = bank[0:4], bank[4:6]

        const_done = sem("const_done")
        const_zero = sem("const_zero")
        pv_clear = sem("pv_clear")
        load_const = sem("load_const")
        alibi_loaded = sem("alibi_loaded")
        alibi_cleared = sem("alibi_cleared")
        x_loaded = sem("x_loaded")
        xr_loaded = [sem(f"xr_loaded{n}") for n in range(2)]
        apack_free = sem("apack_free")
        fpack_free = sem("fpack_free")
        apack_loaded = sem("apack_loaded")
        fpack_loaded = sem("fpack_loaded")
        mw_loaded = sem("mw_loaded")
        bqs_ready = sem("bqs_ready")
        ln_step = sem("ln_step")
        rstd_ready = sem("rstd_ready")
        xn_ready = sem("xn_ready")
        xt_ready = sem("xt_ready")
        xnT_ready = sem("xnT_ready")
        init_step = sem("init_step")
        fin_step = sem("fin_step")
        proj_ready = sem("proj_ready")
        qk_ready = sem("qk_ready")
        rproj_ready = sem("rproj_ready")
        rproj_used = sem("rproj_used")
        rope_step = sem("rope_step")
        v_ready = sem("v_ready")
        p1_ready = sem("p1_ready")
        p2_ready = sem("p2_ready")
        r1_ready = sem("r1_ready")
        p3_ready = sem("p3_ready")
        parts_stored = sem("parts_stored")
        stack_loaded = [sem(f"stack_loaded{g}") for g in range(QUADS)]
        a_ready = sem("a_ready")
        a_used = sem("a_used")
        max_step = sem("max_step")
        mparts_ready = sem("mparts_ready")
        mT_made = sem("mT_made")
        mT_ready = sem("mT_ready")
        m_loaded = sem("m_loaded")
        b_ready = sem("b_ready")
        exp_done = sem("exp_done")
        pv_done = sem("pv_done")
        ot_done = sem("ot_done")
        otT_ready = sem("otT_ready")
        norm_step = sem("norm_step")
        norm_done = sem("norm_done")
        attnT_made = sem("attnT_made")
        attnT_ready = sem("attnT_ready")
        o_ready = sem("o_ready")
        x_added = sem("x_added")
        h_ready = sem("h_ready")
        gelu_done = sem("gelu_done")
        y_ready = sem("y_ready")
        f_added = sem("f_added")
        eh_ready = sem("eh_ready")
        egelu_done = sem("egelu_done")
        ey_ready = sem("ey_ready")
        ey_used = sem("ey_used")
        c_made = sem("c_made")
        c_step = sem("c_step")
        cproj_step = sem("cproj_step")
        cproj_pow = sem("cproj_pow")
        cproj_ready = sem("cproj_ready")
        xp_ready = sem("xp_ready")
        xpT_ready = sem("xpT_ready")
        r_ready = sem("r_ready")
        route_step = sem("route_step")
        route_pow = sem("route_pow")
        comb_ready = sem("comb_ready")
        combT_made = sem("combT_made")
        combT_ready = sem("combT_ready")
        b2_ready = sem("b2_ready")
        b2_added = sem("b2_added")
        out_ready = sem("out_ready")
        stored = sem("stored")

        block = ctx.enter_context(nc.Block())

        class Chain:
            def __init__(self, eng, s, n, each):
                self.eng, self.s, self.base, self.each, self.k = eng, s, n * each, each, 0

            def link(self, ins, wait=True):
                ins.then_inc(self.s, 1)
                self.k += 1
                assert self.k <= self.each
                if wait:
                    self.eng.wait_ge(self.s, self.base + self.k)

            def end(self):
                assert self.k == self.each, (self.k, self.each)

        def tiles(buf, J):
            if isinstance(J, int):
                return buf[:, J * TT:(J + 1) * TT, :]
            return buf[:, bass.ds(J * TT, TT), :]

        def tile1(buf, J, t):
            if isinstance(J, int):
                return buf[:, J * TT + t, :]
            return buf[:, bass.ds(J * TT + t, 1), :].rearrange("p a d -> p (a d)")

        A_CHUNKS = [[(0, 0, 3)], [(0, 0, 2), (0, 384, 0)], [(1, 0, 3)], [(1, 0, 2), (1, 384, 0)],
                    [(0, 0, 1), (1, 256, 1)]]
        B_CHUNKS = [[(0, 0, 0)], [(0, 0, 1), (0, 384, 3)], [(1, 0, 0)], [(1, 0, 1), (1, 384, 3)],
                    [(0, 0, 2), (1, 256, 2)]]
        KT_COL = [0, 512, 1024, 896]

        def iterations(base, job_a, job_b, extras):
            for i in range(-2, JOBS + 1):
                for pos in range(CHUNKS):
                    a_glob = (i + 1) * CHUNKS + pos + SKEW
                    ja, ca = divmod(a_glob, CHUNKS)
                    for what, rel, at in extras:
                        if at == (pos, 0) and 0 <= i + rel < JOBS:
                            what(base, i + rel)
                    if 0 <= ja < JOBS and job_a:
                        job_a(base, ja, ca)
                    if 0 <= i < JOBS and job_b:
                        job_b(base, i, pos)
                    for what, rel, at in extras:
                        if at == (pos, 1) and 0 <= i + rel < JOBS:
                            what(base, i + rel)

        ROPE_EACH = 4

        @block.tensor
        def _(pe):
            mm = nc.tensor.matmul

            def transposes(X, L):
                pe.wait_ge(xn_ready, L + 1)
                for t in range(TT):
                    last = nc.tensor.transpose(bankF[:, t * P:(t + 1) * P], xn[:, t, :], ident[:])
                last.then_inc(xt_ready, 1)

            def attention(base, X0, L0, rope_job):
                w = bp_sb if rope_job else ap_sb
                wq, wk, wv, wo = ([0, 256, 512, 640] if rope_job else [0, 128, 256, AP_WO])

                def xt(b, j):
                    if j >= 1:
                        pe.wait_ge(v_ready, b + j)
                    transposes(X0 + j, L0 + j)

                def project(b, j, k):
                    if k == 0:
                        pe.wait_ge(xnT_ready, X0 + j + 1)
                    else:
                        pe.wait_ge(qk_ready, 2 * (b + j) + 1)
                    mm(bankF[:], ap_sb[:, k * D:(k + 1) * D], xnT[:], start=True, stop=True).then_inc(proj_ready, 1)

                def project_rope(b, j, k):
                    if k == 0:
                        pe.wait_ge(xnT_ready, X0 + j + 1)
                    else:
                        pe.wait_ge(rproj_used, ROPE_EACH * j + k)
                    mm(bankF[:], bp_sb[:, k * D:(k + 1) * D], xnT[:], start=True, stop=True).then_inc(rproj_ready, 1)

                def project_v(b, j):
                    if rope_job:
                        pe.wait_ge(rproj_used, ROPE_EACH * (j + 1))
                        wv = bp_sb[:, 4 * D:5 * D]
                    else:
                        pe.wait_ge(qk_ready, 2 * (b + j) + 2)
                        wv = ap_sb[:, 2 * D:3 * D]
                    for t in range(TT):
                        last = mm(bankF[:, t * D:(t + 1) * D], xnT[:, t * P:(t + 1) * P], wv, start=True, stop=True)
                    last.then_inc(proj_ready, 1)

                def pass_a(b, j, c):
                    pair, k = divmod(c, CPP)
                    if c % CPQ == 0:
                        pe.wait_ge(stack_loaded[pair // 2], LOADS * 16 * (b + j + 1))
                    if j > 0 or c >= 2:
                        pe.wait_ge(a_used, CHUNKS * (b + j) + c - 1)
                    Q, K, bk = QS[j % 2], KS[j % 2], bankA[c % 2]
                    for n, (h, col, t) in enumerate(A_CHUNKS[k]):
                        hh, w = 2 * pair + h, (t + 1) * P
                        mm(bk[:, col:col + w], Q[0:ROW_MAX, hh, t * P:(t + 1) * P], K[0:ROW_MAX, hh, 0:w],
                           start=True, stop=False)
                        last = mm(bk[:, col + w - P:col + w], ident_b[:], mask_a[:], start=False, stop=True)
                    last.then_inc(a_ready, 1)

                def pass_b(b, j, c):
                    pair, k = divmod(c, CPP)
                    if c == 0:
                        pe.wait_ge(m_loaded, 48 * (b + j + 1))
                    if j > 0 or c >= 3:
                        pe.wait_ge(exp_done, CHUNKS * (b + j) + c - 2)
                    Q, K, bk = QS[j % 2], KS[j % 2], bankB[(CHUNKS * j + c) % 3]
                    for n, (h, col, t) in enumerate(B_CHUNKS[k]):
                        hh, w = 2 * pair + h, T - t * P
                        mm(bk[:, col:col + w], K[0:ROWS, hh, t * P:(t + 1) * P], Q[0:ROWS, hh, t * P:T],
                           start=True, stop=False)
                        last = mm(bk[:, col:col + P], ident_b[:], mask_b[:], start=False, stop=True)
                    last.then_inc(b_ready, 1)

                def pv(b, j, g):
                    pe.wait_ge(exp_done, CHUNKS * (b + j) + CPQ * (g + 1))
                    if g == 0:
                        pe.wait_ge(v_ready, b + j + 1)
                    if j > 0 or g > 0:
                        pe.wait_ge(ot_done, QUADS * (b + j) + g)
                    for kt in range(TT):
                        for h in range(4):
                            last = mm(bankPV[32 * h:32 * h + HD + 1, kt * P:T], V[j % 3][:, kt, 4 * g + h, :],
                                      Pq[g % 2][:, h, KT_COL[kt]:KT_COL[kt] + T - kt * P],
                                      start=(kt == 0), stop=(kt == TT - 1))
                    last.then_inc(pv_done, 1)

                def ot_transposes(b, j, t):
                    if t == 0:
                        pe.wait_ge(ot_done, QUADS * (b + j + 1))
                        if j + 1 < JOBS:
                            pe.wait_ge(mT_ready, b + j + 2)
                        else:
                            pe.wait_ge(x_added, 2 * (b + j) - 1)
                    else:
                        pe.wait_ge(norm_done, TT * (b + j) + t)
                    for g in range(QUADS):
                        last = nc.tensor.transpose(bankR[:, g * P:(g + 1) * P], OT[:, g, t * P:(t + 1) * P], ident[:])
                    last.then_inc(otT_ready, 1)

                def attn_transposes(b, j):
                    pe.wait_ge(norm_done, TT * (b + j + 1))
                    for t in range(TT):
                        last = nc.tensor.transpose(bankR[:, t * P:(t + 1) * P], attn[:, t, :], ident[:])
                    last.then_inc(attnT_made, 1)

                def out_project(b, j):
                    pe.wait_ge(attnT_ready, b + j + 1)
                    wo = bp_sb[:, 5 * D:6 * D] if rope_job else ap_sb[:, AP_WO:AP_WO + D]
                    for t in range(TT):
                        last = mm(bankR[:, t * D:(t + 1) * D], attnT[:, t * P:(t + 1) * P], wo, start=True, stop=True)
                    last.then_inc(o_ready, 1)

                def max_transposes(b, j):
                    pe.wait_ge(mparts_ready, b + j + 1)
                    if j >= 2:
                        pe.wait_ge(x_added, 2 * (b + j - 2) + 1)
                    elif j == 1:
                        pe.wait_ge(mT_ready, b + 1)
                    for t in range(TT):
                        last = nc.tensor.transpose(mT_ps[:, t * P:(t + 1) * P],
                                                   mparts[:, t, :], ident_b[:])
                    last.then_inc(mT_made, 1)

                extras = [(xt, 2, (0, 1))]
                if rope_job:
                    extras += [(lambda b, j, k=k: project_rope(b, j, k), 2, (3 + 2 * k, 1)) for k in range(4)]
                    extras += [(project_v, 2, (12, 1))]
                else:
                    extras += [(lambda b, j, k=k: project(b, j, k), 2, (3 + 3 * k, 1)) for k in range(2)]
                    extras += [(project_v, 2, (9, 1))]
                extras += [(lambda b, j: pv(b, j, 3), -1, (2, 1))]
                extras += [(lambda b, j, g=g: pv(b, j, g), 0, (10 * g + 12, 1)) for g in range(3)]
                extras += [(lambda b, j, t=t: ot_transposes(b, j, t), -1, (6 + 2 * t, 1)) for t in range(TT)]
                extras += [(attn_transposes, -1, (15, 1)), (out_project, -1, (18, 1)), (max_transposes, 1, (33, 1))]
                iterations(base, pass_a, pass_b, extras)

            def hidden(xT, w1, f, banks_free, ready):
                banks_free()
                for ft in range(FT):
                    last = mm(bankH[ft][:], w1(ft), xT[:], start=True, stop=True).then_inc(ready, 1)

            def ffn(L):
                F0 = L * JOBS
                X0, L0 = 16 * L + JOBS, 16 * L + 2 * JOBS

                def xt(j):
                    if j >= 1:
                        pe.wait_ge(xnT_ready, X0 + j)
                    transposes(X0 + j, L0 + j)

                def up(j):
                    pe.wait_ge(xnT_ready, X0 + j + 1)
                    if j == 0:
                        pe.wait_ge(fpack_loaded, 16 * (L + 1))
                    if j >= 1:
                        pe.wait_ge(gelu_done, FT * (F0 + j))
                    for ft in range(FT):
                        mm(bankH[ft][:], fp_sb[:, FP_W1 + ft * P:FP_W1 + (ft + 1) * P], xnT[:],
                           start=True, stop=True).then_inc(h_ready, 1)

                def down(j):
                    pe.wait_ge(gelu_done, FT * (F0 + j + 1))
                    if j >= 2:
                        pe.wait_ge(f_added, 2 * (F0 + j - 1) - 1)
                    for t in range(TT):
                        for ft in range(FT):
                            last = mm(bankY[j % 2][:, t * D:(t + 1) * D], hT[j % 2][:, ft, t * P:(t + 1) * P],
                                      fp_sb[:, FP_W2 + ft * D:FP_W2 + (ft + 1) * D],
                                      start=(ft == 0), stop=(ft == FT - 1))
                    last.then_inc(y_ready, 1)

                xt(0)
                for j in range(JOBS):
                    up(j)
                    if j + 1 < JOBS:
                        xt(j + 1)
                    if j >= 1:
                        down(j - 1)
                down(JOBS - 1)

            def experts(round_, X0, L0):
                def xt(M):
                    pe.wait_ge(xnT_ready, X0 + M)
                    pe.wait_ge(xn_ready, L0 + M + 1)
                    for t in range(TT):
                        last = nc.tensor.transpose(bankF[:, t * P:(t + 1) * P], xn[:, t, :], ident[:])
                    last.then_inc(xt_ready, 1)

                def up(M, xT, e):
                    EI = M * E + e
                    pe.wait_ge(egelu_done, FT * EI)
                    for ft in range(FT):
                        mm(bankH[ft][:], W1[:, e, ft * P:(ft + 1) * P], xT[:],
                           start=True, stop=True).then_inc(eh_ready, 1)

                def down(M, e, first):
                    EI = M * E + e
                    pe.wait_ge(egelu_done, FT * (EI + 1))
                    if not (first and e < 2):
                        pe.wait_ge(ey_used, EI - 1)
                    for t in range(TT):
                        for ft in range(FT):
                            last = mm(bankY[e % 2][:, t * D:(t + 1) * D], hT[e % 2][:, ft, t * P:(t + 1) * P],
                                      W2[:, e, ft, :], start=(ft == 0), stop=(ft == FT - 1))
                    last.then_inc(ey_ready, 1)

                def route(M, xT):
                    pe.wait_ge(b2_added, M)
                    mm(bankR[:], mp_sb[:, MP_WP:MP_WP + D], xT[:], start=True, stop=True).then_inc(xp_ready, 1)

                def route2(M):
                    pe.wait_ge(xpT_ready, 2 * (M + 1))
                    for t in range(TT):
                        mm(bankR[:, t * 16:t * 16 + E], xpT[:, t * P:(t + 1) * P], cproj[:], start=True, stop=True)
                        last = mm(bankR[:, t * 16 + E:t * 16 + E + 1], sqT[:, t * P:(t + 1) * P], ones[:, 0:1],
                                  start=True, stop=True)
                    last.then_inc(r_ready, 1)

                def bias1(M, p):
                    pe.wait_ge(comb_ready, M + 1)
                    for t in range(TT):
                        last = nc.tensor.transpose(bankR[0:E, t * P:(t + 1) * P], comb[p][:, t, :], ident[:])
                    last.then_inc(combT_made, 1)

                def bias2(M):
                    pe.wait_ge(combT_ready, M + 1)
                    for t in range(TT):
                        last = mm(bankR[:, t * D:(t + 1) * D], combT[:, t * P:(t + 1) * P], b2_sb[:],
                                  start=True, stop=True)
                    last.then_inc(b2_ready, 1)

                if round_ == 0:
                    pe.wait_ge(c_step, 1)
                    pe.wait_ge(xn_ready, L0 + 1)
                    mm(bankR[:, 0:E], ones[:], cn[:, 0, :], start=True, stop=True).then_inc(c_made, 1)
                    pe.wait_ge(cproj_ready, 1)
                pe.wait_ge(mw_loaded, 32 * (round_ + 1))
                M0 = round_ * JOBS
                xt(M0)

                def job(M, p, first, last):
                    xT = [xnT, xnT2][p]
                    pe.wait_ge(xnT_ready, X0 + M + 1)
                    route(M, xT)
                    up(M, xT, 0)
                    route2(M)
                    up(M, xT, 1)
                    down(M, 0, first)
                    up(M, xT, 2)
                    down(M, 1, first)
                    bias1(M, p)
                    up(M, xT, 3)
                    bias2(M)
                    down(M, 2, first)
                    for e in range(4, E):
                        up(M, xT, e)
                        down(M, e - 1, first)
                        if e == 5 and not last:
                            xt(M + 1)
                    down(M, E - 1, first)

                job(M0, 0, round_ == 0, False)
                job(M0 + 1, 1, False, False)
                with pe.Fori(0, 2) as it:
                    _plain(pe)
                    job(M0 + 2 + it * 2, 0, False, False)
                    job(M0 + 3 + it * 2, 1, False, False)
                job(M0 + 6, 0, False, False)
                job(M0 + 7, 1, False, True)

            pe.wait_ge(const_done, 11)
            pe.wait_ge(pv_clear, 1)
            pe.wait_ge(load_const, 16 * 6)
            with pe.Fori(0, LAYERS) as L:
                _plain(pe)
                pe.wait_ge(apack_loaded, 16 * (L + 1))
                attention(L * JOBS, 16 * L, 16 * L + JOBS, False)
                ffn(L)
            experts(0, 64, 80)
            attention(32, 72, 88, True)
            experts(1, 72, 88)

        @block.scalar
        def _(act):
            A = nc.scalar.activation

            def evac_x(X, dst):
                act.wait_ge(xt_ready, X + 1)
                A(dst[:], bankF[:], ACT.Copy).then_inc(xnT_ready, 1)

            def attention(base, X0, rope_job):
                def xnt(b, j):
                    act.wait_ge(xt_ready, X0 + j + 1)
                    if rope_job:
                        A(xnT[:], bankF[:], ACT.Copy).then_inc(xnT_ready, 1)
                    else:
                        A(xnT[:], bankF[:], ACT.Identity, bias=ap_sb[:, AP_COL + 1:AP_COL + 2],
                          scale=ap_sb[:, AP_COL:AP_COL + 1]).then_inc(xnT_ready, 1)

                def evac_qk(b, j, k):
                    act.wait_ge(proj_ready, 3 * (b + j) + k + 1)
                    if k == 0 and j >= 1:
                        act.wait_ge(p3_ready, 2 * (b + j))
                    if k == 0:
                        A(qk[:, 0, :], bankF[:], ACT.Identity, bias=bqs[:], scale=1.0 / math.sqrt(HD)).then_inc(qk_ready, 1)
                    else:
                        A(qk[:, 1, :], bankF[:], ACT.Identity,
                          bias=ap_sb[:, AP_COL + 3:AP_COL + 4]).then_inc(qk_ready, 1)

                def exps(b, j, c):
                    pair, k = divmod(c, CPP)
                    g = pair // 2
                    if c % CPQ == 0 and (j > 0 or g >= 2):
                        act.wait_ge(pv_done, QUADS * (b + j) + g - 1)
                    act.wait_ge(b_ready, CHUNKS * (b + j) + c + 1)
                    bk = bankB[(CHUNKS * j + c) % 3]
                    h0 = 2 * (pair % 2)
                    if k < 4:
                        dst = Pq[g % 2][:, h0 + k // 2, (k % 2) * T:(k % 2) * T + T]
                        src = bk[:]
                    else:
                        dst = Pq[g % 2][:, h0:h0 + 2, 2 * T:HCOLS]
                        src = bk[:].rearrange("p (h c) -> p h c", h=2)
                    A(dst, src, ACT.Exp).then_inc(exp_done, 1)

                def evac_ot(b, j, g):
                    act.wait_ge(pv_done, QUADS * (b + j) + g + 1)
                    if g == 0 and j > 0:
                        act.wait_ge(otT_ready, TT * (b + j))
                    A(OT[:, g, :], bankPV[:], ACT.Copy).then_inc(ot_done, 1)

                def evac_attn(b, j):
                    act.wait_ge(attnT_made, b + j + 1)
                    A(attnT[:], bankR[:], ACT.Copy).then_inc(attnT_ready, 1)

                extras = [(xnt, 2, (1, 1))]
                if not rope_job:
                    extras += [(lambda b, j, k=k: evac_qk(b, j, k), 2, (4 + 3 * k, 1)) for k in range(2)]
                extras += [(lambda b, j: evac_ot(b, j, 3), -1, (4, 1))]
                extras += [(lambda b, j, g=g: evac_ot(b, j, g), 0, (10 * g + 14, 1)) for g in range(3)]
                extras += [(evac_attn, -1, (16, 1))]
                iterations(base, None, exps, extras)

            act.wait_ge(const_done, 11)
            act.wait_ge(load_const, 16 * 6)
            with act.Fori(0, LAYERS) as L:
                _plain(act)
                act.wait_ge(apack_loaded, 16 * (L + 1))
                A(bqs[:], ap_sb[:, AP_COL + 2:AP_COL + 3], ACT.Copy, scale=1.0 / math.sqrt(HD)).then_inc(bqs_ready, 1)
                act.wait_ge(bqs_ready, L + 1)
                attention(L * JOBS, 16 * L, False)

                F0, X0 = L * JOBS, 16 * L + JOBS

                def ffn_x(j):
                    act.wait_ge(xt_ready, X0 + j + 1)
                    if j == 0:
                        act.wait_ge(fpack_loaded, 16 * (L + 1))
                    else:
                        act.wait_ge(h_ready, FT * (F0 + j))
                    A(xnT[:], bankF[:], ACT.Identity, bias=fp_sb[:, FP_COL + 1:FP_COL + 2],
                      scale=fp_sb[:, FP_COL:FP_COL + 1]).then_inc(xnT_ready, 1)

                def ffn_gelu(j):
                    if j >= 2:
                        act.wait_ge(y_ready, F0 + j - 1)
                    for ft in range(FT):
                        act.wait_ge(h_ready, FT * (F0 + j) + ft + 1)
                        A(hT[j % 2][:, ft, :], bankH[ft][:], ACT.Gelu,
                          bias=fp_sb[:, FP_COL + 2 + ft:FP_COL + 3 + ft]).then_inc(gelu_done, 1)

                ffn_x(0)
                for j in range(JOBS):
                    ffn_gelu(j)
                    if j + 1 < JOBS:
                        ffn_x(j + 1)

            def experts(round_, X0):
                def job(M, p, first, last):
                    act.wait_ge(xp_ready, M + 1)
                    A(xpT, bankR[:], ACT.Identity, bias=mp_sb[:, MP_BP:MP_BP + 1]).then_inc(xpT_ready, 1)
                    A(sqT, bankR[:], ACT.Square, bias=mp_sb[:, MP_BP:MP_BP + 1]).then_inc(xpT_ready, 1)
                    for e in range(E):
                        EI = M * E + e
                        if not (first and e < 2):
                            act.wait_ge(ey_ready, EI - 1)
                        for ft in range(FT):
                            act.wait_ge(eh_ready, FT * EI + ft + 1)
                            A(hT[e % 2][:, ft, :], bankH[ft][:], ACT.Gelu,
                              bias=mp_sb[:, MP_B1 + e * FT + ft:MP_B1 + e * FT + ft + 1]).then_inc(egelu_done, 1)
                        if e == 2:
                            act.wait_ge(combT_made, M + 1)
                            A(combT[:], bankR[0:E, :], ACT.Copy).then_inc(combT_ready, 1)
                        if e == 5 and not last:
                            evac_x(X0 + M + 1, [xnT2, xnT][p])

                M0 = round_ * JOBS
                evac_x(X0 + M0, xnT)
                job(M0, 0, round_ == 0, False)
                job(M0 + 1, 1, False, False)
                with act.Fori(0, 2) as it:
                    _plain(act)
                    job(M0 + 2 + it * 2, 0, False, False)
                    job(M0 + 3 + it * 2, 1, False, False)
                job(M0 + 6, 0, False, False)
                job(M0 + 7, 1, False, True)

            experts(0, 64)
            attention(32, 72, True)
            experts(1, 72)

        @block.vector
        def _(dve):
            v = nc.vector

            def ln_stats(n, J, src=None):
                ch = Chain(dve, ln_step, n, 3)
                rows = tiles(xs, J) if src is None else src
                for t in range(TT):
                    row = tile1(xs, J, t) if src is None else src[:, t, :]
                    last = v.bn_stats(stats[:, t, :], row)
                ch.link(last)
                v.tensor_copy(spare[:, 0:1], half[:, 0:1])
                for t in range(TT):
                    last = v.bn_aggr(mv[:, t, :], stats[:, t, :])
                ch.link(last)
                ch.link(v.tensor_scalar(veps[:], mv[:, :, 1], EPS, None, ALU.add), wait=False)
                ch.end()

            def ln_apply(n, J, src=None, dst=None):
                dve.wait_ge(rstd_ready, n + 1)
                for t in range(TT):
                    row = tile1(xs, J, t) if src is None else src[:, t, :]
                    to = xn[:, t, :] if dst is None else dst[:, t, :]
                    last = v.tensor_scalar(to, row, mv[:, t, 0:1], rstd[:, t:t + 1], ALU.subtract, ALU.mult)
                last.then_inc(xn_ready, 1)

            def attention(base, X0, L0, j0_stream, rope_job):
                def lns(b, j):
                    ln_stats(L0 + j, j)

                def lna(b, j):
                    if j >= 1:
                        dve.wait_ge(xt_ready, X0 + j)
                    ln_apply(L0 + j, j)

                def split1(b, j, k):
                    dve.wait_ge(qk_ready, 2 * (b + j) + k + 1)
                    if j >= 1:
                        dve.wait_ge(parts_stored, 96 * (b + j))
                    v.tensor_copy(parts[:, k, 0, :], qk[:, k, :]).then_inc(p1_ready, 1)

                def split2(b, j, k):
                    dve.wait_ge(r1_ready, 2 * (b + j) + k + 1)
                    v.tensor_copy(parts[:, k, 1, :], resid[:, k, :]).then_inc(p2_ready, 1)

                def rotate(b, j, n):
                    k = n // 2
                    dve.wait_ge(rproj_ready, ROPE_EACH * j + n + 1)
                    if n % 2 == 0:
                        if k == 0 and j >= 1:
                            dve.wait_ge(p3_ready, 2 * (b + j))
                        v.tensor_tensor(qk[:, k, :], bankF[:], rope_sb[:, 2 * k, :], ALU.mult).then_inc(rproj_used, 1)
                    else:
                        v.tensor_tensor(rtmp[:, k, :], bankF[:], rope_sb[:, 2 * k + 1, :],
                                        ALU.mult).then_inc(rproj_used, 1)
                        dve.wait_ge(rproj_used, ROPE_EACH * j + n + 1)
                        v.tensor_tensor(qk[:, k, :], qk[:, k, :], rtmp[:, k, :], ALU.add).then_inc(qk_ready, 1)
                        split1(b, j, k)

                def take_v(b, j):
                    dve.wait_ge(proj_ready, (96 + j + 1) if rope_job else 3 * (b + j) + 3)
                    dst = V[j % 3][:, :, :, 0:HD]
                    src = bankF[:].rearrange("p (t h d) -> p t h d", t=TT, h=H)
                    if j >= 3:
                        dve.wait_ge(pv_done, QUADS * (b + j - 2))
                    if rope_job:
                        v.tensor_copy(dst, src).then_inc(v_ready, 1)
                    else:
                        bias = ap_sb[:, AP_BV:AP_BV + D].rearrange("p (h d) -> p h d", h=H)
                        v.tensor_tensor(dst, src, bias.unsqueeze(1).broadcast_to([P, TT, H, HD]),
                                        ALU.add).then_inc(v_ready, 1)

                def maxima(b, j, c):
                    pair, k = divmod(c, CPP)
                    dve.wait_ge(a_ready, CHUNKS * (b + j) + c + 1)
                    bk = bankA[c % 2]
                    if k < 4:
                        h = 2 * pair + k // 2
                        dst = mx[:, h, 4 * (k % 2):4 * (k % 2) + 4]
                        src = bk[:].rearrange("p (n c) -> p n c", n=4)
                    else:
                        dst = mx[:, 2 * pair:2 * pair + 2, 8:10]
                        src = bk[:].rearrange("p (h n c) -> p h n c", h=2, n=2)
                    v.tensor_reduce(dst, src, axis=AX.X, op=ALU.max).then_inc(a_used, 1)

                def negate_split(b, j):
                    ch = Chain(dve, max_step, b + j, 4)
                    dve.wait_ge(a_used, CHUNKS * (b + j + 1))
                    for t, (lo, n) in enumerate([(7, 1), (8, 2), (4, 3), (0, 4)]):
                        last = v.tensor_reduce(mneg[:, t, :], mx[:, :, lo:lo + n], axis=AX.X, op=ALU.max, negate=True)
                    ch.link(last)
                    if j >= 1:
                        dve.wait_ge(mT_made, b + j)
                    ch.link(v.tensor_copy(mparts[:, :, 0 * H:1 * H], mneg[:]))
                    ch.link(v.tensor_tensor(mres[:], mneg[:], mparts[:, :, 0 * H:1 * H], ALU.subtract))
                    ch.link(v.tensor_copy(mparts[:, :, 1 * H:2 * H], mres[:]))
                    ch.end()
                    v.tensor_tensor(mparts[:, :, 2 * H:3 * H], mres[:], mparts[:, :, 1 * H:2 * H],
                                    ALU.subtract).then_inc(mparts_ready, 1)

                def evac_max(b, j):
                    dve.wait_ge(mT_made, b + j + 1)
                    if j >= 1:
                        dve.wait_ge(m_loaded, 48 * (b + j))
                    v.tensor_copy(mT[:], mT_ps[0:NPART * H, :]).then_inc(mT_ready, 1)

                def normalise(b, j, t):
                    dve.wait_ge(otT_ready, TT * (b + j) + t + 1)
                    heads = bankR[:].rearrange("p (h c) -> p h c", h=H)
                    ch = Chain(dve, norm_step, TT * (b + j) + t, 1)
                    ch.link(v.reciprocal(rl[:], heads[:, :, HD]))
                    ch.end()
                    if t == 0 and j > 0:
                        dve.wait_ge(attnT_made, b + j)
                    v.tensor_tensor(attn[:, t, :].rearrange("p (h d) -> p h d", h=H), heads[:, :, 0:HD],
                                    rl[:].unsqueeze(2).broadcast_to([P, H, HD]), ALU.mult).then_inc(norm_done, 1)

                def add_x(b, j):
                    dve.wait_ge(o_ready, b + j + 1)
                    rows = tiles(xs, j)
                    o = bankR[:].rearrange("p (t d) -> p t d", t=TT)
                    v.tensor_tensor(rows, rows, o, ALU.add).then_inc(x_added, 1)
                    dve.wait_ge(x_added, 2 * (b + j) + 1)
                    if rope_job:
                        v.tensor_copy(spare[:, 0:1], half[:, 0:1]).then_inc(x_added, 1)
                    else:
                        bo = ap_sb[:, AP_BO:AP_BO + D].unsqueeze(1).broadcast_to([P, TT, D])
                        v.tensor_tensor(rows, rows, bo, ALU.add).then_inc(x_added, 1)

                extras = []
                if rope_job:
                    extras += [(lambda b, j, n=n: rotate(b, j, n), 2, (4 + 2 * n, 1)) for n in range(4)]
                    extras += [(lambda b, j: split2(b, j, 0), 2, (11, 1)), (take_v, 2, (13, 1)),
                               (lambda b, j: split2(b, j, 1), 2, (15, 1))]
                else:
                    extras += [(lambda b, j: split1(b, j, 0), 2, (5, 1)), (lambda b, j: split1(b, j, 1), 2, (8, 1)),
                               (lambda b, j: split2(b, j, 0), 2, (9, 1)), (take_v, 2, (10, 1)),
                               (lambda b, j: split2(b, j, 1), 2, (12, 1))]
                extras += [(lambda b, j, t=t: normalise(b, j, t), -1, (7 + 2 * t, 1)) for t in range(TT)]
                extras += [(add_x, -1, (19, 1)), (negate_split, 1, (29, 1)), (evac_max, 1, (34, 1)),
                           (lns, 3, (35, 1)), (lna, 3, (38, 1))]
                lns(base, 0)
                lna(base, 0)
                iterations(base, maxima, None, extras)

            def ffn(L):
                F0, X0, L0 = L * JOBS, 16 * L + JOBS, 16 * L + 2 * JOBS

                def ln(j):
                    ln_stats(L0 + j, j)
                    dve.wait_ge(xt_ready, X0 + j)
                    ln_apply(L0 + j, j)

                def add(j):
                    dve.wait_ge(y_ready, F0 + j + 1)
                    rows = tiles(xs, j)
                    y = bankY[j % 2][:].rearrange("p (t d) -> p t d", t=TT)
                    v.tensor_tensor(rows, rows, y, ALU.add).then_inc(f_added, 1)
                    dve.wait_ge(f_added, 2 * (F0 + j) + 1)
                    b2 = fp_sb[:, FP_B2:FP_B2 + D].unsqueeze(1).broadcast_to([P, TT, D])
                    v.tensor_tensor(rows, rows, b2, ALU.add).then_inc(f_added, 1)

                dve.wait_ge(x_added, 2 * (F0 + JOBS))
                dve.wait_ge(fpack_loaded, 16 * (L + 1))
                ln(0)
                for j in range(JOBS):
                    if j + 1 < JOBS:
                        ln(j + 1)
                    if j >= 1:
                        add(j - 1)
                add(JOBS - 1)
                dve.wait_ge(f_added, 2 * (F0 + JOBS))

            def experts(round_, X0, L0):
                ROUTE = 22
                cnb = cn[:, 2, :]

                def route(M, p):
                    ch = Chain(dve, route_step, M, ROUTE)
                    n2, nrm, sc, xn2, omx, mn, ws = (s4[:, i, :] for i in range(7))
                    dot, t1, a, ap1, s, root, tt_, w, den, sel = (s8[:, i, :, :] for i in range(10))
                    lt, eq, rk = (s88[:, i, :, :] for i in range(3))

                    def b8(x):
                        return x.unsqueeze(2).broadcast_to([P, TT, E])

                    def row8(x):
                        return x.unsqueeze(1).broadcast_to([P, TT, E])

                    dve.wait_ge(r_ready, M + 1)
                    ch.link(v.tensor_copy(R[:], bankR[:, 0:64].rearrange("p (t c) -> p t c", t=TT)[:, :, 0:E + 1]))
                    ch.link(v.tensor_copy(n2, R[:, :, E]), wait=False)
                    dve.wait_ge(route_pow, 2 * M + 1)
                    ch.link(v.tensor_scalar(nrm, nrm, 1e-7, None, ALU.max))
                    ch.link(v.reciprocal(sc, nrm))
                    ch.link(v.tensor_scalar(sc, sc, 0.95, 1.0, ALU.mult, ALU.min))
                    ch.link(v.tensor_tensor(xn2, n2, sc, ALU.mult))
                    ch.link(v.tensor_tensor(xn2, xn2, sc, ALU.mult))
                    ch.link(v.tensor_scalar(xn2, xn2, 0.99, None, ALU.min))
                    ch.link(v.tensor_tensor(dot, R[:, :, 0:E], b8(sc), ALU.mult))
                    ch.link(v.tensor_scalar(t1, dot, -2.0, None, ALU.mult))
                    ch.link(v.tensor_tensor(t1, t1, row8(cnb), ALU.add))
                    ch.link(v.tensor_tensor(t1, t1, b8(xn2), ALU.add))
                    v.tensor_scalar(omx, xn2, -1.0, 1.0, ALU.mult, ALU.add)
                    ch.link(v.tensor_scalar(t1, t1, 0.0, 2.0, ALU.max, ALU.mult))
                    ch.link(v.tensor_tensor(den, b8(omx), row8(cn[:, 1, :]), ALU.mult))
                    ch.link(v.tensor_scalar(den, den, 1e-7, None, ALU.add))
                    ch.link(v.reciprocal(den, den))
                    ch.link(v.tensor_tensor(a, t1, den, ALU.mult))
                    ch.link(v.tensor_scalar(a, a, 1.0, 1.0 + 1e-7, ALU.add, ALU.max))
                    v.tensor_scalar(ap1, a, 1.0, None, ALU.add)
                    ch.link(v.tensor_scalar(root, a, -1.0, None, ALU.add))
                    ch.link(v.tensor_tensor(s, root, ap1, ALU.mult), wait=False)
                    ae = a.unsqueeze(3).broadcast_to([P, TT, E, E])
                    aj = a.unsqueeze(2).broadcast_to([P, TT, E, E])

                    def e88(x):
                        return x.rearrange("p t (e j) -> p t e j", e=E)

                    v.tensor_tensor(e88(lt), aj, ae, ALU.is_lt)
                    ch.link(v.tensor_tensor(e88(eq), aj, ae, ALU.is_equal))
                    trib = tri[:].rearrange("p e j -> p (e j)").unsqueeze(1).broadcast_to([P, TT, E * E])
                    ch.link(v.tensor_tensor(rk, eq, trib, ALU.mult))
                    ch.end()
                    return lt, eq, rk, sel, a, root, tt_, w, mn, ws

                def route2(M, p, vals):
                    lt, eq, rk, sel, a, root, tt_, w, mn, ws = vals
                    ch = Chain(dve, c_step, M, 11)
                    ch.base = ch.base + 4

                    def b8(x):
                        return x.unsqueeze(2).broadcast_to([P, TT, E])

                    ch.link(v.tensor_tensor(lt, lt, rk, ALU.add))
                    ch.link(v.tensor_reduce(sel, lt.rearrange("p t (e j) -> p t e j", e=E), axis=AX.X, op=ALU.add))
                    ch.link(v.tensor_scalar(sel, sel, 1.5, None, ALU.is_lt))
                    dve.wait_ge(route_pow, 2 * M + 2)
                    ch.link(v.tensor_tensor(tt_, a, root, ALU.add))
                    ch.link(v.tensor_reduce(mn, tt_, axis=AX.X, op=ALU.min))
                    ch.link(v.reciprocal(w, tt_))
                    ch.link(v.tensor_tensor(w, w, b8(mn), ALU.mult))
                    ch.link(v.tensor_tensor(w, w, sel, ALU.mult))
                    ch.link(v.tensor_reduce(ws, w, axis=AX.X, op=ALU.add))
                    ch.link(v.reciprocal(ws, ws))
                    ch.link(v.tensor_tensor(comb[p][:], w, b8(ws), ALU.mult))
                    ch.end()
                    v.tensor_copy(ws, mn).then_inc(comb_ready, 1)

                def ln(M, J):
                    ln_stats(L0 + M, J)
                    dve.wait_ge(xt_ready, X0 + M)
                    ln_apply(L0 + M, J)

                def job(M, J, p, last):
                    vals = route(M, p)
                    route2(M, p, vals)
                    for e in range(E):
                        EI = M * E + e
                        if e == 1:
                            dve.wait_ge(b2_ready, M + 1)
                            rows = tiles(xs, J)
                            v.tensor_tensor(rows, rows, bankR[:].rearrange("p (t d) -> p t d", t=TT),
                                            ALU.add).then_inc(b2_added, 1)
                            dve.wait_ge(b2_added, M + 1)
                        dve.wait_ge(ey_ready, EI + 1)
                        for t in range(TT):
                            row = tile1(xs, J, t)
                            ins = v.scalar_tensor_tensor(out=row, in0=bankY[e % 2][:, t * D:(t + 1) * D],
                                                         scalar=comb[p][:, t, e:e + 1], in1=row,
                                                         op0=ALU.mult, op1=ALU.add)
                        ins.then_inc(ey_used, 1)
                        dve.wait_ge(ey_used, EI + 1)
                        if e == 3 and not last:
                            ln(M + 1, J + 1)
                    if round_ == 1:
                        v.tensor_copy(spare[:, 0:1], half[:, 0:1]).then_inc(out_ready, 1)

                M0 = round_ * JOBS
                ln(M0, 0)
                if round_ == 0:
                    n = [0]

                    def step(ins):
                        n[0] += 1
                        ins.then_inc(cproj_step, 1)
                        dve.wait_ge(cproj_step, n[0])
                    c = mp_sb[:, MP_C:MP_C + E]
                    v.tensor_tensor(cn[:, 0, :], c, c, ALU.mult).then_inc(c_step, 1)
                    dve.wait_ge(c_made, 1)
                    ch = Chain(dve, c_step, 0, 4)
                    ch.k = 1
                    ch.link(v.tensor_copy(cn[:, 2, :], bankR[:, 0:E]), wait=False)
                    dve.wait_ge(cproj_pow, 1)
                    step(v.tensor_scalar(cn[:, 1, :], cn[:, 1, :], 1e-7, None, ALU.max))
                    step(v.reciprocal(cn[:, 1, :], cn[:, 1, :]))
                    step(v.tensor_scalar(cn[:, 1, :], cn[:, 1, :], 0.95, 1.0, ALU.mult, ALU.min))
                    step(v.tensor_tensor(cproj[:], c, cn[:, 1, :], ALU.mult))
                    step(v.tensor_tensor(cn[:, 2, :], cn[:, 2, :], cn[:, 1, :], ALU.mult))
                    step(v.tensor_tensor(cn[:, 2, :], cn[:, 2, :], cn[:, 1, :], ALU.mult))
                    step(v.tensor_scalar(cn[:, 2, :], cn[:, 2, :], 0.99, None, ALU.min))
                    ch.link(v.tensor_scalar(cn[:, 1, :], cn[:, 2, :], -1.0, 1.0, ALU.mult, ALU.add))
                    ch.link(v.tensor_copy(cn[:, 0, :], cn[:, 2, :]))
                    v.tensor_copy(spare[:, 0:1], half[:, 0:1]).then_inc(cproj_ready, 1)
                job(M0, 0, 0, False)
                job(M0 + 1, 1, 1, False)
                with dve.Fori(0, 2) as it:
                    _plain(dve)
                    job(M0 + 2 + it * 2, 2 + it * 2, 0, False)
                    job(M0 + 3 + it * 2, 3 + it * 2, 1, False)
                job(M0 + 6, 6, 0, False)
                job(M0 + 7, 7, 1, True)

            v.memset(bankPV[:], 0.0).then_inc(pv_clear, 1)
            dve.wait_ge(const_done, 11)
            dve.wait_ge(load_const, 16 * 6)
            dve.wait_ge(x_loaded, 16)
            v.tensor_copy(spare[:, 1:2], half[:, 0:1]).then_inc(apack_free, 1)
            v.tensor_copy(spare[:, 2:3], half[:, 0:1]).then_inc(fpack_free, 1)
            for j in range(JOBS):
                ln_stats(j, j)
                ln_apply(j, j, dst=tiles(xs, j))
                dve.wait_ge(xn_ready, j + 1)
            with dve.Fori(0, LAYERS) as L:
                _plain(dve)
                dve.wait_ge(apack_loaded, 16 * (L + 1))
                attention(L * JOBS, 16 * L, 16 * L + JOBS, 0, False)
                dve.wait_ge(x_added, 2 * JOBS * (L + 1))
                v.tensor_copy(spare[:, 1:2], half[:, 0:1]).then_inc(apack_free, 1)
                ffn(L)
                v.tensor_copy(spare[:, 2:3], half[:, 0:1]).then_inc(fpack_free, 1)
            for j in range(JOBS):
                rows = tiles(xs, j)
                ln_stats(72 + j, j)
                ln_apply(72 + j, j, dst=rows)
                dve.wait_ge(xn_ready, 73 + j)
                ch = Chain(dve, fin_step, j, 3)
                fw = fin_sb[:, 0:D].unsqueeze(1).broadcast_to([P, TT, D])
                fb = fin_sb[:, D:2 * D].unsqueeze(1).broadcast_to([P, TT, D])
                ch.link(v.tensor_tensor(rows, rows, fw, ALU.mult))
                ch.link(v.tensor_tensor(rows, rows, fb, ALU.add))
                dve.wait_ge(xr_loaded[j % 2], 16 * (j // 2 + 1))
                ch.link(v.tensor_tensor(rows, rows, xload[:, j % 2, :, :], ALU.add))
                ch.end()
            experts(0, 64, 80)
            attention(32, 72, 88, 0, True)
            dve.wait_ge(x_added, 80)
            experts(1, 72, 88)

        @block.gpsimd
        def _(pool):
            g = nc.gpsimd
            g.memset(ident[:], 0.0).then_inc(const_zero, 1)
            g.memset(ident_b[:], 0.0).then_inc(const_zero, 1)
            g.memset(mask_a[:], 0.0).then_inc(const_zero, 1)
            g.memset(mask_b[:], 0.0).then_inc(const_zero, 1)
            g.memset(tri[:], 1.0).then_inc(const_zero, 1)
            pool.wait_ge(const_zero, 5)
            for m in (ident, ident_b):
                g.affine_select(out=m[:], in_=m[:], compare_op=ALU.not_equal, fill=1.0, base=0,
                                pattern=[[-1, P]], channel_multiplier=1).then_inc(const_done, 1)
            g.affine_select(out=mask_a[:], in_=mask_a[:], compare_op=ALU.is_ge, fill=NEG, base=0,
                            pattern=[[-1, P]], channel_multiplier=1).then_inc(const_done, 1)
            g.affine_select(out=mask_b[:], in_=mask_b[:], compare_op=ALU.is_ge, fill=NEG, base=0,
                            pattern=[[1, P]], channel_multiplier=-1).then_inc(const_done, 1)
            g.affine_select(out=tri[:], in_=tri[:], compare_op=ALU.is_gt, fill=0.0, base=0,
                            pattern=[[1, E], [-1, E]], channel_multiplier=0).then_inc(const_done, 1)
            g.memset(half[:], 0.5).then_inc(const_done, 1)
            g.memset(mhalf[:], -0.5).then_inc(const_done, 1)
            g.memset(ones[:], 1.0).then_inc(const_done, 1)
            pool.wait_ge(const_done, 8)
            for i in range(2):
                g.memset(QS[i][64:P, :, :], 0.0).then_inc(const_zero, 1)
                g.memset(KS[i][64:P, :, :], 0.0).then_inc(const_zero, 1)
            pool.wait_ge(const_zero, 9)
            for i in range(2):
                last = g.memset(KS[i][ROW_MAX:ROWS, :, :], 1.0)
            last.then_inc(const_done, 1)
            pool.wait_ge(const_done, 9)
            g.memset(mparts[:], 0.0)
            for i in range(3):
                last = g.memset(V[i][:], 1.0)
            last.then_inc(const_done, 1)
            g.memset(big[:, 0:1], 0.0).then_inc(const_done, 1)
            for i in range(2):
                g.dma_start(QS[i][ROW_ALIBI:ROW_ALIBI + N_ALIBI, :, :], alibi[0]).then_inc(alibi_loaded, 16)
                g.dma_start(KS[i][ROW_ALIBI:ROW_ALIBI + N_ALIBI, :, :], alibi[1]).then_inc(alibi_loaded, 16)

            def rsqrt(n, ex=None):
                pool.wait_ge(ln_step, 3 * n + 3)
                g.tensor_tensor(rstd[:], veps[:], mhalf[:], ALU.pow).then_inc(rstd_ready, 1)

            def attention(base, L0):
                def split(b, j, k):
                    n = 2 * (b + j) + k
                    pool.wait_ge(p1_ready, n + 1)
                    g.tensor_tensor(resid[:, k, :], qk[:, k, :], parts[:, k, 0, :], ALU.subtract).then_inc(r1_ready, 1)

                def split3(b, j, k):
                    n = 2 * (b + j) + k
                    pool.wait_ge(p2_ready, n + 1)
                    g.tensor_tensor(parts[:, k, 2, :], resid[:, k, :], parts[:, k, 1, :],
                                    ALU.subtract).then_inc(p3_ready, 1)

                extras = [(lambda b, j: split(b, j, 0), 2, (5, 1)), (lambda b, j: split(b, j, 1), 2, (8, 1)),
                          (lambda b, j: split3(b, j, 0), 2, (10, 1)), (lambda b, j: split3(b, j, 1), 2, (13, 1)),
                          (lambda b, j: rsqrt(L0 + j), 3, (36, 1))]
                rsqrt(L0)
                iterations(base, None, None, extras)

            def experts(round_, L0):
                def job(M, last):
                    pool.wait_ge(route_step, 22 * M + 2)
                    g.tensor_tensor(s4[:, 1, :], s4[:, 0, :], half[:], ALU.pow).then_inc(route_pow, 1)
                    pool.wait_ge(route_step, 22 * M + 20)
                    g.tensor_tensor(s8[:, 5, :, :], s8[:, 4, :, :],
                                    half[:].unsqueeze(2).broadcast_to([P, TT, E]), ALU.pow).then_inc(route_pow, 1)
                    if not last:
                        rsqrt(L0 + M + 1)
                M0 = round_ * JOBS
                rsqrt(L0 + M0)
                if round_ == 0:
                    pool.wait_ge(c_step, 2)
                    g.tensor_tensor(cn[:, 1, :], cn[:, 2, :], half[:, 0:1].broadcast_to([P, E]),
                                    ALU.pow).then_inc(cproj_pow, 1)
                job(M0, False)
                job(M0 + 1, False)
                with pool.Fori(0, 2) as it:
                    _plain(pool)
                    job(M0 + 2 + it * 2, False)
                    job(M0 + 3 + it * 2, False)
                job(M0 + 6, False)
                job(M0 + 7, True)

            for j in range(JOBS):
                rsqrt(j)
            with pool.Fori(0, LAYERS) as L:
                _plain(pool)
                attention(L * JOBS, 16 * L + JOBS)
                for j in range(JOBS):
                    rsqrt(16 * L + 2 * JOBS + j)
            for j in range(JOBS):
                rsqrt(72 + j)
            pool.wait_ge(x_added, 2 * LAYERS * JOBS)
            for i in range(2):
                g.dma_start(QS[i][ROW_ALIBI:ROW_ALIBI + N_ALIBI, :, :], alibi[2]).then_inc(alibi_cleared, 16)
            experts(0, 80)
            attention(32, 88)
            experts(1, 88)

        @block.sync
        def _(sp):
            xv = x.rearrange("b (t p) d -> p (b t) d", p=P)
            ov = out.rearrange("b (t p) d -> p (b t) d", p=P)
            sp.dma_start(xs[:], xv).then_inc(x_loaded, 16)
            for dst, src in ((fin_sb, final), (bp_sb, bpack), (mp_sb, mpack), (b2_sb, b2e)):
                sp.dma_start(dst[:], src).then_inc(load_const, 16)
            sp.dma_start(rope_sb[:, 0:2, :], rope[:, 0:2, :]).then_inc(load_const, 16)
            sp.dma_start(rope_sb[:, 2:4, :], rope[:, 2:4, :]).then_inc(load_const, 16)

            def attention(base):
                def store(b, j):
                    for k in range(2):
                        sp.wait_ge(p3_ready, 2 * (b + j) + k + 1)
                        for a in range(NPART):
                            sp.dma_start(part_scr[j % 2, k, a], parts[:, k, a, :]).then_inc(parts_stored, 16)

                def load(b, j, q):
                    if q == 0:
                        sp.wait_ge(parts_stored, 96 * (b + j + 1))
                    if j >= 2:
                        sp.wait_ge(b_ready, CHUNKS * (b + j - 2) + CPQ * (q + 1))
                    for a in range(NPART):
                        for k, S in ((0, QS), (1, KS)):
                            src = part_scr[j % 2, k, a].rearrange("(d h) t -> d (h t)", d=HD)
                            src = src[:, q * 4 * T:(q + 1) * 4 * T]
                            if k == 0:
                                s3 = src.unsqueeze(0).broadcast_to([NPART, HD, 4 * T])
                                dst = S[j % 2][a * 24:(a + 1) * 24, 4 * q:4 * q + 4, :]
                                sp.dma_start(dst, s3).then_inc(stack_loaded[q], 16)
                            else:
                                for r in range(NPART):
                                    dst = S[j % 2][r * 24 + a * 8:r * 24 + a * 8 + 8, 4 * q:4 * q + 4, :]
                                    sp.dma_start(dst, src).then_inc(stack_loaded[q], 16)

                def load_max(b, j):
                    sp.wait_ge(mT_ready, b + j + 1)
                    for a in range(NPART):
                        sp.dma_start(QS[j % 2][ROW_MAX + a:ROW_MAX + a + 1, :, :],
                                     mT[a * H:(a + 1) * H, :]).then_inc(m_loaded, 16)

                extras = [(store, 2, (14, 1)), (lambda b, j: load(b, j, 0), 2, (15, 1)),
                          (lambda b, j: load(b, j, 1), 2, (20, 1)), (lambda b, j: load(b, j, 2), 2, (30, 1)),
                          (load_max, 1, (35, 1)), (lambda b, j: load(b, j, 3), 2, (39, 1))]
                iterations(base, None, None, extras)

            with sp.Fori(0, LAYERS) as L:
                _plain(sp)
                sp.wait_ge(apack_free, L + 1)
                sp.dma_start(ap_sb[:], apack[bass.ds(L, 1)].rearrange("a p n -> p (a n)")).then_inc(apack_loaded, 16)
                sp.wait_ge(fpack_free, L + 1)
                sp.dma_start(fp_sb[:], fpack[bass.ds(L, 1)].rearrange("a p n -> p (a n)")).then_inc(fpack_loaded, 16)
                sp.wait_ge(alibi_loaded, 64)
                attention(L * JOBS)
            sp.wait_ge(x_added, 2 * LAYERS * JOBS)
            for j in range(JOBS):
                if j >= 2:
                    sp.wait_ge(fin_step, 3 * (j - 1))
                sp.dma_start(xload[:, j % 2, :, :], xv[:, j * TT:(j + 1) * TT, :]).then_inc(xr_loaded[j % 2], 16)

            def load_experts():
                sp.dma_start(big[:, 0:4096], w1e).then_inc(mw_loaded, 16)
                sp.dma_start(big[:, 4096:8192], w2e).then_inc(mw_loaded, 16)

            load_experts()
            sp.wait_ge(alibi_cleared, 32)
            attention(32)
            sp.wait_ge(x_added, 80)
            load_experts()
            for j in range(JOBS):
                sp.wait_ge(out_ready, j + 1)
                sp.dma_start(ov[:, j * TT:(j + 1) * TT, :], xs[:, j * TT:(j + 1) * TT, :]).then_inc(stored, 16)
            sp.wait_ge(stored, 16 * JOBS)


def kernel(**inputs):
    import concourse.bacc as _bacc
    from concourse.bass_utils import run_bass_kernel_spmd as _run

    a = {k[3:] if k.startswith("L0_") else k: np.asarray(v) for k, v in inputs.items()}
    f = np.float32
    dh = np.arange(D).reshape(H, HD).T.reshape(-1)
    swap = (np.arange(D) ^ 1)[dh]

    def rep(v):
        return np.broadcast_to(v[..., None, :], (*v.shape[:-1], P, v.shape[-1]))

    wi = a["attn_a_in_proj_w"].reshape(LAYERS, 3, D, D)
    bi = a["attn_a_in_proj_b"].reshape(LAYERS, 3, D)
    T21 = (0, 2, 1)
    apack = np.concatenate([
        wi[:, 0][:, dh].transpose(T21), wi[:, 1][:, dh].transpose(T21), wi[:, 2].transpose(T21),
        a["attn_a_out_proj_w"].transpose(T21), rep(bi[:, 2]), rep(a["attn_a_out_proj_b"]),
        a["attn_a_ln1_w"][:, :, None], a["attn_a_ln1_b"][:, :, None],
        bi[:, 0][:, dh][:, :, None], bi[:, 1][:, dh][:, :, None]], axis=2)
    fpack = np.concatenate([
        a["attn_a_ffn1_w"].transpose(T21),
        a["attn_a_ffn2_w"].reshape(LAYERS, D, FT, P).transpose(0, 3, 2, 1).reshape(LAYERS, P, FT * D),
        rep(a["attn_a_ffn2_b"]), a["attn_a_ln2_w"][:, :, None], a["attn_a_ln2_b"][:, :, None],
        a["attn_a_ffn1_b"].reshape(LAYERS, FT, P).transpose(T21)], axis=2)
    final = np.concatenate([rep(a["attn_a_final_w"]), rep(a["attn_a_final_b"])], axis=1)
    wq, wk = a["attn_b_W_q"], a["attn_b_W_k"]
    bpack = np.concatenate([wq[dh].T, wq[swap].T, wk[dh].T, wk[swap].T, a["attn_b_W_v"].T, a["attn_b_W_o"].T], axis=1)
    mpack = np.concatenate([a["ffn_centroids"].T, a["ffn_Wp"], a["ffn_bp"][:, None],
                            a["ffn_b1"].reshape(E, FT, P).transpose(2, 0, 1).reshape(P, E * FT)], axis=1)
    w1e = a["ffn_W1"].transpose(1, 0, 2).reshape(P, E * T)
    w2e = a["ffn_W2"].reshape(E, FT, P, D).transpose(2, 0, 1, 3).reshape(P, E * FT * D)

    def part(v):
        return (v.view(np.uint32) & np.uint32(0xFFFF0000)).view(f)
    slopes = ((2.0 ** -0.5) ** np.arange(1, H + 1)).astype(f)
    s1 = part(slopes)
    s2 = part(slopes - s1)
    s3 = slopes - s1 - s2
    pos = np.arange(T)
    hi, lo = (pos // 8 * 8).astype(f), (pos % 8).astype(f)
    alibi = np.zeros((3, N_ALIBI, H, T), f)
    for n, s in enumerate((s1, s2, s3)):
        for m, p in enumerate((hi, lo)):
            r = 2 * n + m
            alibi[0, r], alibi[1, r] = s[:, None], p[None]
            alibi[0, 6 + r], alibi[1, 6 + r] = p[None], -s[:, None]
    at = np.minimum(pos, 255).astype(f)
    theta = (10000.0 ** (-2.0 * np.arange(HD // 2, dtype=f) / HD)).astype(f)
    ang = at[None, :] * theta[:, None]
    cos, sin = np.cos(ang).astype(f), np.sin(ang).astype(f)
    dim = np.repeat(np.arange(HD), H)
    C, S = cos[dim // 2], sin[dim // 2] * np.where(dim % 2 == 0, -1, 1)[:, None].astype(f)
    r8 = f(1.0 / math.sqrt(HD))
    rope = np.stack([C * r8, S * r8, C, S], axis=1).astype(f)

    arrays = dict(x=a["attn_a_x"], apack=apack, fpack=fpack, final=final, bpack=bpack, mpack=mpack,
                  b2e=a["ffn_b2"], w1e=w1e, w2e=w2e, alibi=alibi, rope=rope)
    arrays = {f"in_{k}": np.ascontiguousarray(v) for k, v in arrays.items()}
    nc = _bacc.Bacc("TRN2", target_bir_lowering=False, num_devices=1)
    args = [nc.dram_tensor(k, v.shape, F32, kind="ExternalInput").ap() for k, v in arrays.items()]
    out = nc.dram_tensor("out_x", [JOBS, T, D], F32, kind="ExternalOutput").ap()
    part_scr = nc.dram_tensor("part_scr", [2, 2, NPART, P, T], BF16, kind="Internal").ap()
    hybrid_kernel(nc, *args, out, part_scr)
    r = _run(nc, [arrays], core_ids=[0])
    return r.results[0]["out_x"]
```

```python
import math
from contextlib import ExitStack

import numpy as np

import concourse.bass as bass
from concourse import mybir

F32 = mybir.dt.float32
BF16 = mybir.dt.bfloat16
ALU = mybir.AluOpType
ACT = mybir.ActivationFunctionType
AX = mybir.AxisListType

P = 128
D = 128
T = 512
TT = T // P
JOBS = 8
H, HD = 16, 8
LAYERS = 4
FT = 4
E = 8
EPS = 1e-5
NEG = -3.0e38

NPART = 3
ROW_ALIBI = NPART * NPART * HD
N_ALIBI = 12
ROW_MAX = 96
ROWS = ROW_MAX + NPART
LOADS = NPART + NPART * NPART
PAIRS = H // 2
QUADS = H // 4
CPP = 5
CHUNKS = PAIRS * CPP
CPQ = 2 * CPP
HCOLS = 1280
SKEW = 2 * CPP

AP_QKV, AP_BV, AP_COL, AP_N = 0, 384, 512, 516
FP_W1, FP_W2, FP_B2, FP_WO, FP_BO, FP_COL, FP_N = 0, 512, 1024, 1152, 1280, 1408, 1414
BP_N = 6 * D
MP_C, MP_WP, MP_BP, MP_B1, MP_N = 0, 8, 136, 137, 137 + 32


def _plain(eng):
    eng.get_value_cache().nocache = True


def hybrid_kernel(nc, x, apack, fpack, final, bpack, mpack, b2e, w1e, w2e,
                  alibi, rope, out, part_scr):
    ctx = ExitStack()
    with ctx:
        def sb(name, shape, dt=F32):
            return ctx.enter_context(nc.sbuf_tensor(name, shape, dt))

        def sem(name):
            return ctx.enter_context(nc.semaphore(name))

        xs = sb("xs", [P, JOBS * TT, D])
        ident = sb("ident", [P, P])
        ident_b = sb("ident_b", [P, P], BF16)
        mask_a = sb("mask_a", [P, P], BF16)
        mask_b = sb("mask_b", [P, P], BF16)
        half = sb("half", [P, TT])
        mhalf = sb("mhalf", [P, TT])
        ones = sb("ones", [P, P])
        tri = sb("tri", [P, E, E])
        ap_sb = sb("ap_sb", [P, AP_N])
        fp_sb = sb("fp_sb", [P, FP_N])
        fin_sb = sb("fin_sb", [P, 2 * D])
        bp_sb = sb("bp_sb", [P, BP_N])
        mp_sb = sb("mp_sb", [P, MP_N])
        b2_sb = sb("b2_sb", [E, D])
        bqs = sb("bqs", [P, 1])
        stats = sb("stats", [P, TT, 6])
        mv = sb("mv", [P, TT, 2])
        veps = sb("veps", [P, TT])
        rstd = sb("rstd", [P, TT])
        xn = sb("xn", [P, TT, D])
        xnT = sb("xnT", [P, T])
        xnT2 = sb("xnT2", [P, T])
        qk = sb("qk", [P, 2, T])
        resid = sb("resid", [P, 2, T])
        rtmp = sb("rtmp", [P, 2, T])
        parts = sb("parts", [P, 2, NPART, T], BF16)
        QS = [sb(f"QS{i}", [P, H, T], BF16) for i in range(2)]
        KS = [sb(f"KS{i}", [P, H, T], BF16) for i in range(2)]
        V = [sb(f"V{i}", [P, TT, H, HD + 1]) for i in range(4)]
        big = sb("big", [P, 12288])
        Pq = [big[:, n * 4 * HCOLS:(n + 1) * 4 * HCOLS].rearrange("p (h c) -> p h c", h=4) for n in range(2)]
        W1 = big[:, 0:4096].rearrange("p (e f) -> p e f", e=E)
        W2 = big[:, 4096:8192].rearrange("p (e f d) -> p e f d", e=E, f=FT)
        fhT = big[:, 8 * HCOLS:12288].rearrange("p (f t) -> p f t", f=FT)
        rope_sb = big[:, 8 * HCOLS:12288].rearrange("p (n t) -> p n t", n=4)
        hT = [big[:, 8192 + 2048 * n:8192 + 2048 * (n + 1)].rearrange("p (f t) -> p f t", f=FT) for n in range(2)]
        mx = sb("mx", [P, H, 10])
        mneg = sb("mneg", [P, TT, H])
        mres = sb("mres", [P, TT, H])
        mparts = sb("mparts", [P, TT, P], BF16)
        mT = sb("mT", [NPART * H, T], BF16)
        spare = sb("spare", [P, 4])
        OT = sb("OT", [P, QUADS, T])
        rl = sb("rl", [P, H])
        attn = sb("attn", [P, TT, D])
        attnT = sb("attnT", [P, T])
        xload = resid[:].rearrange("p k (t d) -> p k t d", t=TT)
        xpT, sqT = qk[:, 0, :], qk[:, 1, :]
        cproj = sb("cproj", [P, E])
        cn = sb("cn", [P, 3, E])
        R = sb("R", [P, TT, E + 1])
        s4 = sb("s4", [P, 12, TT])
        s8 = sb("s8", [P, 10, TT, E])
        s88 = OT[:, 0:2, :].rearrange("p g c -> p (g c)")[:, 0:3 * TT * E * E].rearrange(
            "p (i t e) -> p i t e", i=3, t=TT)
        comb = [sb(f"comb{n}", [P, TT, E]) for n in range(2)]
        combT = sb("combT", [E, T])

        bank = [ctx.enter_context(nc.psum_tensor(f"bank{i}", [P, T], F32)) for i in range(8)]
        bankA, bankB = bank[0:2], bank[2:5]
        bankPV, bankF, bankR = bank[5], bank[6], bank[7]
        mT_ps = bankR[:, 0:T // 2].bitcast(BF16)
        bankH, bankY = bank[0:4], bank[4:6]
        bankG = [bankF, bankR, bankPV, bankF]

        const_done = sem("const_done")
        const_zero = sem("const_zero")
        pv_clear = sem("pv_clear")
        load_const = sem("load_const")
        alibi_loaded = sem("alibi_loaded")
        alibi_cleared = sem("alibi_cleared")
        x_loaded = sem("x_loaded")
        xr_loaded = [sem(f"xr_loaded{n}") for n in range(2)]
        rope_loaded = sem("rope_loaded")
        fln_step = sem("fln_step")
        frstd_ready = sem("frstd_ready")
        fxn_ready = sem("fxn_ready")
        fxt_ready = sem("fxt_ready")
        fxnT_ready = sem("fxnT_ready")
        apack_loaded = sem("apack_loaded")
        fpack_loaded = sem("fpack_loaded")
        mw_loaded = sem("mw_loaded")
        bqs_ready = sem("bqs_ready")
        ln_step = sem("ln_step")
        rstd_ready = sem("rstd_ready")
        xn_ready = sem("xn_ready")
        xt_ready = sem("xt_ready")
        xnT_ready = sem("xnT_ready")
        init_step = sem("init_step")
        fin_step = sem("fin_step")
        proj_ready = sem("proj_ready")
        qk_ready = sem("qk_ready")
        rproj_ready = sem("rproj_ready")
        rproj_used = sem("rproj_used")
        rope_step = sem("rope_step")
        v_ready = sem("v_ready")
        p1_ready = sem("p1_ready")
        p2_ready = sem("p2_ready")
        r1_ready = sem("r1_ready")
        p3_ready = sem("p3_ready")
        parts_stored = sem("parts_stored")
        stack_loaded = [sem(f"stack_loaded{g}") for g in range(QUADS)]
        a_ready = sem("a_ready")
        a_used = sem("a_used")
        max_step = sem("max_step")
        mparts_ready = sem("mparts_ready")
        mT_made = sem("mT_made")
        mT_ready = sem("mT_ready")
        m_loaded = sem("m_loaded")
        b_ready = sem("b_ready")
        exp_done = sem("exp_done")
        pv_done = sem("pv_done")
        ot_done = sem("ot_done")
        otT_ready = sem("otT_ready")
        norm_step = sem("norm_step")
        norm_done = sem("norm_done")
        attnT_made = sem("attnT_made")
        attnT_ready = sem("attnT_ready")
        o_ready = sem("o_ready")
        x_added = sem("x_added")
        h_ready = sem("h_ready")
        gelu_done = sem("gelu_done")
        y_ready = sem("y_ready")
        f_added = sem("f_added")
        eh_ready = sem("eh_ready")
        egelu_done = sem("egelu_done")
        ey_ready = sem("ey_ready")
        ey_used = sem("ey_used")
        c_made = sem("c_made")
        c_step = sem("c_step")
        cproj_step = sem("cproj_step")
        cproj_pow = sem("cproj_pow")
        cproj_ready = sem("cproj_ready")
        xp_ready = sem("xp_ready")
        xpT_ready = sem("xpT_ready")
        r_ready = sem("r_ready")
        route_step = sem("route_step")
        route_pow = sem("route_pow")
        comb_ready = sem("comb_ready")
        combT_made = sem("combT_made")
        combT_ready = sem("combT_ready")
        b2_ready = sem("b2_ready")
        b2_added = sem("b2_added")
        out_ready = sem("out_ready")
        stored = sem("stored")

        block = ctx.enter_context(nc.Block())

        class Chain:
            def __init__(self, eng, s, n, each):
                self.eng, self.s, self.base, self.each, self.k = eng, s, n * each, each, 0

            def link(self, ins, wait=True):
                ins.then_inc(self.s, 1)
                self.k += 1
                assert self.k <= self.each
                if wait:
                    self.eng.wait_ge(self.s, self.base + self.k)

            def end(self):
                assert self.k == self.each, (self.k, self.each)

        def tiles(buf, J):
            if isinstance(J, int):
                return buf[:, J * TT:(J + 1) * TT, :]
            return buf[:, bass.ds(J * TT, TT), :]

        def tile1(buf, J, t):
            if isinstance(J, int):
                return buf[:, J * TT + t, :]
            return buf[:, bass.ds(J * TT + t, 1), :].rearrange("p a d -> p (a d)")

        A_CHUNKS = [[(0, 0, 3)], [(0, 0, 2), (0, 384, 0)], [(1, 0, 3)], [(1, 0, 2), (1, 384, 0)],
                    [(0, 0, 1), (1, 256, 1)]]
        B_CHUNKS = [[(0, 0, 0)], [(0, 0, 1), (0, 384, 3)], [(1, 0, 0)], [(1, 0, 1), (1, 384, 3)],
                    [(0, 0, 2), (1, 256, 2)]]
        KT_COL = [0, 512, 1024, 896]

        def iteration(b, i, jobs, job_a, job_b, extras):
            for pos in range(CHUNKS):
                ja, ca = divmod((i + 1) * CHUNKS + pos + SKEW, CHUNKS)
                for what, rel, at in extras:
                    if at == (pos, 0) and 0 <= i + rel < jobs:
                        what(b, i + rel)
                if 0 <= ja < jobs and job_a:
                    job_a(b, ja, ca)
                if 0 <= i < jobs and job_b:
                    job_b(b, i, pos)
                for what, rel, at in extras:
                    if at == (pos, 1) and 0 <= i + rel < jobs:
                        what(b, i + rel)

        def iterations(eng, base, jobs, job_a, job_b, extras):
            first, last = 2, jobs - 6
            if jobs > JOBS:
                for i in range(-2, first):
                    iteration(base, i, jobs, job_a, job_b, extras)
                with eng.Fori(0, last - first, 4) as at:
                    _plain(eng)
                    for i in range(first + 4, first + 8):
                        iteration(at - 4, i, jobs, job_a, job_b, extras)
                for i in range(last, jobs + 1):
                    iteration(base, i, jobs, job_a, job_b, extras)
            else:
                for i in range(-2, jobs + 1):
                    iteration(base, i, jobs, job_a, job_b, extras)

        ROPE_EACH = 4

        ENC = LAYERS * JOBS

        def ln_init(j):
            return 0 if j == 0 else j + 1

        def ln_index(b, j):
            if isinstance(b, int):
                if b == ENC:
                    return LN_B + j
                if b + j == 0:
                    return 1
            return b + j + JOBS

        LN_B = JOBS + ENC + 2 * JOBS
        XT_B = ENC + JOBS

        def ln_final(M):
            return JOBS + ENC + 2 * M

        def ln_exp(round_, M):
            return JOBS + ENC + 2 * M + 1 if round_ == 0 else LN_B + M

        def xt_exp(round_, M):
            return ENC + M if round_ == 0 else XT_B + M

        @block.tensor
        def _(pe):
            mm = nc.tensor.matmul

            def transposes(rows_ready, n, made):
                pe.wait_ge(rows_ready, n + 1)
                for t in range(TT):
                    last = nc.tensor.transpose(bankF[:, t * P:(t + 1) * P], xn[:, t, :], ident[:])
                last.then_inc(made, 1)

            def attention(base, jobs, X0, L0, rope_job):
                def xt(b, j):
                    if j >= 1:
                        pe.wait_ge(v_ready, b + j)
                    transposes(xn_ready, ln_index(b, j), xt_ready)

                def project(b, j, k):
                    if k == 0:
                        pe.wait_ge(xnT_ready, b + j + 1)
                        if j % 4 == 0:
                            pe.wait_ge(apack_loaded, 4 * (b + j) + 16)
                    else:
                        pe.wait_ge(qk_ready, 2 * (b + j) + 1)
                    mm(bankF[:], ap_sb[:, k * D:(k + 1) * D], xnT[:], start=True, stop=True).then_inc(proj_ready, 1)

                def project_rope(b, j, k):
                    if k == 0:
                        pe.wait_ge(xnT_ready, XT_B + j + 1)
                    else:
                        pe.wait_ge(rproj_used, ROPE_EACH * j + k)
                    mm(bankF[:], bp_sb[:, k * D:(k + 1) * D], xnT[:], start=True, stop=True).then_inc(rproj_ready, 1)

                def project_v(b, j):
                    if rope_job:
                        pe.wait_ge(rproj_used, ROPE_EACH * (j + 1))
                        wv = bp_sb[:, 4 * D:5 * D]
                    else:
                        pe.wait_ge(qk_ready, 2 * (b + j) + 2)
                        wv = ap_sb[:, 2 * D:3 * D]
                    for t in range(TT):
                        last = mm(bankF[:, t * D:(t + 1) * D], xnT[:, t * P:(t + 1) * P], wv, start=True, stop=True)
                    last.then_inc(proj_ready, 1)

                def pass_a(b, j, c):
                    pair, k = divmod(c, CPP)
                    if c % CPQ == 0:
                        pe.wait_ge(stack_loaded[pair // 2], LOADS * 16 * (b + j + 1))
                    if j > 0 or c >= 2:
                        pe.wait_ge(a_used, CHUNKS * (b + j) + c - 1)
                    Q, K, bk = QS[j % 2], KS[j % 2], bankA[c % 2]
                    for n, (h, col, t) in enumerate(A_CHUNKS[k]):
                        hh, w = 2 * pair + h, (t + 1) * P
                        mm(bk[:, col:col + w], Q[0:ROW_MAX, hh, t * P:(t + 1) * P], K[0:ROW_MAX, hh, 0:w],
                           start=True, stop=False)
                        last = mm(bk[:, col + w - P:col + w], ident_b[:], mask_a[:], start=False, stop=True)
                    last.then_inc(a_ready, 1)

                def pass_b(b, j, c):
                    pair, k = divmod(c, CPP)
                    if c == 0:
                        pe.wait_ge(m_loaded, 48 * (b + j + 1))
                    if c == 0:
                        if j > 0:
                            pe.wait_ge(exp_done, CHUNKS * (b + j))
                    elif j > 0 or c >= 3:
                        pe.wait_ge(exp_done, CHUNKS * (b + j) + c - 2)
                    Q, K, bk = QS[j % 2], KS[j % 2], bankB[c % 3]
                    for n, (h, col, t) in enumerate(B_CHUNKS[k]):
                        hh, w = 2 * pair + h, T - t * P
                        mm(bk[:, col:col + w], K[0:ROWS, hh, t * P:(t + 1) * P], Q[0:ROWS, hh, t * P:T],
                           start=True, stop=False)
                        last = mm(bk[:, col:col + P], ident_b[:], mask_b[:], start=False, stop=True)
                    last.then_inc(b_ready, 1)

                def pv(b, j, g):
                    pe.wait_ge(exp_done, CHUNKS * (b + j) + CPQ * (g + 1))
                    if g == 0:
                        pe.wait_ge(v_ready, b + j + 1)
                    if j > 0 or g > 0:
                        pe.wait_ge(ot_done, QUADS * (b + j) + g)
                    for kt in range(TT):
                        for h in range(4):
                            last = mm(bankPV[32 * h:32 * h + HD + 1, kt * P:T], V[j % 4][:, kt, 4 * g + h, :],
                                      Pq[g % 2][:, h, KT_COL[kt]:KT_COL[kt] + T - kt * P],
                                      start=(kt == 0), stop=(kt == TT - 1))
                    last.then_inc(pv_done, 1)

                def ot_transposes(b, j, t):
                    if t == 0:
                        pe.wait_ge(ot_done, QUADS * (b + j + 1))
                        if j + 1 < jobs:
                            pe.wait_ge(mT_ready, b + j + 2)
                        elif rope_job:
                            pe.wait_ge(x_added, 2 * (b + j) - 1)
                        else:
                            pe.wait_ge(f_added, 2 * (b + j) - 1)
                    else:
                        pe.wait_ge(norm_done, TT * (b + j) + t)
                    for g in range(QUADS):
                        last = nc.tensor.transpose(bankR[:, g * P:(g + 1) * P], OT[:, g, t * P:(t + 1) * P], ident[:])
                    last.then_inc(otT_ready, 1)

                def attn_transposes(b, j):
                    pe.wait_ge(norm_done, TT * (b + j + 1))
                    for t in range(TT):
                        last = nc.tensor.transpose(bankR[:, t * P:(t + 1) * P], attn[:, t, :], ident[:])
                    last.then_inc(attnT_made, 1)

                def out_project(b, j):
                    pe.wait_ge(attnT_ready, b + j + 1)
                    if not rope_job and j % 4 == 0:
                        pe.wait_ge(fpack_loaded, 4 * (b + j) + 16)
                    wo = bp_sb[:, 5 * D:6 * D] if rope_job else fp_sb[:, FP_WO:FP_WO + D]
                    for t in range(TT):
                        last = mm(bankR[:, t * D:(t + 1) * D], attnT[:, t * P:(t + 1) * P], wo, start=True, stop=True)
                    last.then_inc(o_ready, 1)

                def max_transposes(b, j):
                    pe.wait_ge(mparts_ready, b + j + 1)
                    if j >= 2:
                        pe.wait_ge(x_added if rope_job else f_added, 2 * (b + j - 2) + 1)
                    elif j == 1:
                        pe.wait_ge(mT_ready, b + 1)
                    for t in range(TT):
                        last = nc.tensor.transpose(mT_ps[:, t * P:(t + 1) * P],
                                                   mparts[:, t, :], ident_b[:])
                    last.then_inc(mT_made, 1)

                def ffn_xt(b, j):
                    transposes(fxn_ready, b + j, fxt_ready)

                def ffn_up(b, j, ft):
                    if ft == 0:
                        pe.wait_ge(fxnT_ready, b + j + 1)
                    if ft == 2 and j + 1 < jobs:
                        pe.wait_ge(ot_done, QUADS * (b + j + 1) + 2)
                    if ft == 3:
                        pe.wait_ge(gelu_done, FT * (b + j) + 1)
                    mm(bankG[ft][:], fp_sb[:, FP_W1 + ft * P:FP_W1 + (ft + 1) * P], xnT[:],
                       start=True, stop=True).then_inc(h_ready, 1)

                def ffn_down(b, j, t):
                    if t == 0:
                        pe.wait_ge(gelu_done, FT * (b + j + 1))
                    for ft in range(FT):
                        last = mm(bankR[:, t * D:(t + 1) * D], fhT[:, ft, t * P:(t + 1) * P],
                                  fp_sb[:, FP_W2 + ft * D:FP_W2 + (ft + 1) * D],
                                  start=(ft == 0), stop=(ft == FT - 1))
                    if t == TT - 1:
                        last.then_inc(y_ready, 1)

                extras = [(xt, 2, (0, 1))]
                if rope_job:
                    extras += [(lambda b, j, k=k: project_rope(b, j, k), 2, (3 + 2 * k, 1)) for k in range(4)]
                    extras += [(project_v, 2, (12, 1))]
                else:
                    extras += [(lambda b, j, k=k: project(b, j, k), 2, (3 + 3 * k, 1)) for k in range(2)]
                    extras += [(project_v, 2, (9, 1))]
                extras += [(lambda b, j: pv(b, j, 3), -1, (2, 1))]
                extras += [(lambda b, j, g=g: pv(b, j, g), 0, (10 * g + 12, 1)) for g in range(3)]
                extras += [(lambda b, j, t=t: ot_transposes(b, j, t), -1, (6 + 2 * t, 1)) for t in range(TT)]
                extras += [(attn_transposes, -1, (15, 1)), (out_project, -1, (18, 1)), (max_transposes, 1, (33, 1))]
                if not rope_job:
                    extras += [(ffn_xt, -1, (23, 1))]
                    extras += [(lambda b, j, ft=ft: ffn_up(b, j, ft), -1, (25 + ft // 3, 1)) for ft in range(FT)]
                    extras += [(lambda b, j, t=t: ffn_down(b, j, t), -1, (28 + t, 0)) for t in range(TT)]
                iterations(pe, base, jobs, pass_a, pass_b, extras)

            def experts(round_):
                def xt(M):
                    pe.wait_ge(xnT_ready, xt_exp(round_, M))
                    transposes(xn_ready, ln_exp(round_, M), xt_ready)

                def up(M, xT, e):
                    EI = M * E + e
                    pe.wait_ge(egelu_done, FT * EI)
                    for ft in range(FT):
                        mm(bankH[ft][:], W1[:, e, ft * P:(ft + 1) * P], xT[:],
                           start=True, stop=True).then_inc(eh_ready, 1)

                def down(M, e, first):
                    EI = M * E + e
                    pe.wait_ge(egelu_done, FT * (EI + 1))
                    if not (first and e < 2):
                        pe.wait_ge(ey_used, EI - 1)
                    for t in range(TT):
                        for ft in range(FT):
                            last = mm(bankY[e % 2][:, t * D:(t + 1) * D], hT[e % 2][:, ft, t * P:(t + 1) * P],
                                      W2[:, e, ft, :], start=(ft == 0), stop=(ft == FT - 1))
                    last.then_inc(ey_ready, 1)

                def route(M, xT):
                    pe.wait_ge(b2_added, M)
                    mm(bankR[:], mp_sb[:, MP_WP:MP_WP + D], xT[:], start=True, stop=True).then_inc(xp_ready, 1)

                def route2(M):
                    pe.wait_ge(xpT_ready, 2 * (M + 1))
                    for t in range(TT):
                        mm(bankR[:, t * 16:t * 16 + E], xpT[:, t * P:(t + 1) * P], cproj[:], start=True, stop=True)
                        last = mm(bankR[:, t * 16 + E:t * 16 + E + 1], sqT[:, t * P:(t + 1) * P], ones[:, 0:1],
                                  start=True, stop=True)
                    last.then_inc(r_ready, 1)

                def bias1(M, p):
                    pe.wait_ge(comb_ready, M + 1)
                    for t in range(TT):
                        last = nc.tensor.transpose(bankR[0:E, t * P:(t + 1) * P], comb[p][:, t, :], ident[:])
                    last.then_inc(combT_made, 1)

                def bias2(M):
                    pe.wait_ge(combT_ready, M + 1)
                    for t in range(TT):
                        last = mm(bankR[:, t * D:(t + 1) * D], combT[:, t * P:(t + 1) * P], b2_sb[:],
                                  start=True, stop=True)
                    last.then_inc(b2_ready, 1)

                if round_ == 0:
                    pe.wait_ge(c_step, 1)
                    pe.wait_ge(xn_ready, ln_exp(0, 0) + 1)
                    mm(bankR[:, 0:E], ones[:], cn[:, 0, :], start=True, stop=True).then_inc(c_made, 1)
                    pe.wait_ge(cproj_ready, 1)
                pe.wait_ge(mw_loaded, 32 * (round_ + 1))
                M0 = round_ * JOBS
                xt(M0)

                def job(M, p, first, last):
                    xT = [xnT, xnT2][p]
                    pe.wait_ge(xnT_ready, xt_exp(round_, M) + 1)
                    route(M, xT)
                    up(M, xT, 0)
                    route2(M)
                    up(M, xT, 1)
                    down(M, 0, first)
                    up(M, xT, 2)
                    down(M, 1, first)
                    bias1(M, p)
                    up(M, xT, 3)
                    bias2(M)
                    down(M, 2, first)
                    for e in range(4, E):
                        up(M, xT, e)
                        down(M, e - 1, first)
                        if e == 5 and not last:
                            xt(M + 1)
                    down(M, E - 1, first)

                job(M0, 0, round_ == 0, False)
                job(M0 + 1, 1, False, False)
                with pe.Fori(0, 2) as it:
                    _plain(pe)
                    job(M0 + 2 + it * 2, 0, False, False)
                    job(M0 + 3 + it * 2, 1, False, False)
                job(M0 + 6, 0, False, False)
                job(M0 + 7, 1, False, True)

            pe.wait_ge(const_done, 11)
            pe.wait_ge(pv_clear, 1)
            pe.wait_ge(load_const, 16 * 4)
            attention(0, ENC, 0, JOBS, False)
            experts(0)
            attention(ENC, JOBS, 0, 0, True)
            experts(1)

        @block.scalar
        def _(act):
            A = nc.scalar.activation

            def evac_x(X, dst):
                act.wait_ge(xt_ready, X + 1)
                A(dst[:], bankF[:], ACT.Copy).then_inc(xnT_ready, 1)

            def attention(base, jobs, rope_job):
                def xnt(b, j):
                    act.wait_ge(xt_ready, (XT_B + j if rope_job else b + j) + 1)
                    if not rope_job and j % 4 == 0:
                        act.wait_ge(apack_loaded, 4 * (b + j) + 16)
                    if rope_job:
                        A(xnT[:], bankF[:], ACT.Copy).then_inc(xnT_ready, 1)
                    else:
                        A(xnT[:], bankF[:], ACT.Identity, bias=ap_sb[:, AP_COL + 1:AP_COL + 2],
                          scale=ap_sb[:, AP_COL:AP_COL + 1]).then_inc(xnT_ready, 1)

                def evac_qk(b, j, k):
                    if k == 0 and j % 4 == 0:
                        A(bqs[:], ap_sb[:, AP_COL + 2:AP_COL + 3], ACT.Copy, scale=1.0 / math.sqrt(HD)).then_inc(bqs_ready, 4)
                        act.wait_ge(bqs_ready, b + j + 4)
                    act.wait_ge(proj_ready, 3 * (b + j) + k + 1)
                    if k == 0 and j >= 1:
                        act.wait_ge(p3_ready, 2 * (b + j))
                    if k == 0:
                        A(qk[:, 0, :], bankF[:], ACT.Identity, bias=bqs[:], scale=1.0 / math.sqrt(HD)).then_inc(qk_ready, 1)
                    else:
                        A(qk[:, 1, :], bankF[:], ACT.Identity,
                          bias=ap_sb[:, AP_COL + 3:AP_COL + 4]).then_inc(qk_ready, 1)

                def exps(b, j, c):
                    pair, k = divmod(c, CPP)
                    g = pair // 2
                    if c % CPQ == 0 and (j > 0 or g >= 2):
                        act.wait_ge(pv_done, QUADS * (b + j) + g - 1)
                    act.wait_ge(b_ready, CHUNKS * (b + j) + c + 1)
                    bk = bankB[c % 3]
                    h0 = 2 * (pair % 2)
                    if k < 4:
                        dst = Pq[g % 2][:, h0 + k // 2, (k % 2) * T:(k % 2) * T + T]
                        src = bk[:]
                    else:
                        dst = Pq[g % 2][:, h0:h0 + 2, 2 * T:HCOLS]
                        src = bk[:].rearrange("p (h c) -> p h c", h=2)
                    A(dst, src, ACT.Exp).then_inc(exp_done, 1)

                def evac_ot(b, j, g):
                    act.wait_ge(pv_done, QUADS * (b + j) + g + 1)
                    if g == 0 and j > 0:
                        act.wait_ge(otT_ready, TT * (b + j))
                    A(OT[:, g, :], bankPV[:], ACT.Copy).then_inc(ot_done, 1)

                def evac_attn(b, j):
                    act.wait_ge(attnT_made, b + j + 1)
                    A(attnT[:], bankR[:], ACT.Copy).then_inc(attnT_ready, 1)

                extras = [(xnt, 2, (1, 1))]
                if not rope_job:
                    extras += [(lambda b, j, k=k: evac_qk(b, j, k), 2, (4 + 3 * k, 1)) for k in range(2)]
                extras += [(lambda b, j: evac_ot(b, j, 3), -1, (4, 1))]
                extras += [(lambda b, j, g=g: evac_ot(b, j, g), 0, (10 * g + 14, 1)) for g in range(3)]
                extras += [(evac_attn, -1, (16, 1))]

                def ffn_x(b, j):
                    act.wait_ge(fxt_ready, b + j + 1)
                    A(xnT[:], bankF[:], ACT.Identity, bias=fp_sb[:, FP_COL + 1:FP_COL + 2],
                      scale=fp_sb[:, FP_COL:FP_COL + 1]).then_inc(fxnT_ready, 1)

                def ffn_gelu(b, j):
                    if j >= 1:
                        act.wait_ge(y_ready, b + j)
                    for ft in range(FT):
                        act.wait_ge(h_ready, FT * (b + j) + ft + 1)
                        A(fhT[:, ft, :], bankG[ft][:], ACT.Gelu,
                          bias=fp_sb[:, FP_COL + 2 + ft:FP_COL + 3 + ft]).then_inc(gelu_done, 1)

                if not rope_job:
                    extras += [(ffn_x, -1, (24, 1)), (ffn_gelu, -1, (26, 1))]
                iterations(act, base, jobs, None, exps, extras)

            act.wait_ge(const_done, 11)
            act.wait_ge(load_const, 16 * 4)
            attention(0, ENC, False)

            def experts(round_):
                def job(M, p, first, last):
                    act.wait_ge(xp_ready, M + 1)
                    A(xpT, bankR[:], ACT.Identity, bias=mp_sb[:, MP_BP:MP_BP + 1]).then_inc(xpT_ready, 1)
                    A(sqT, bankR[:], ACT.Square, bias=mp_sb[:, MP_BP:MP_BP + 1]).then_inc(xpT_ready, 1)
                    for e in range(E):
                        EI = M * E + e
                        if not (first and e < 2):
                            act.wait_ge(ey_ready, EI - 1)
                        for ft in range(FT):
                            act.wait_ge(eh_ready, FT * EI + ft + 1)
                            A(hT[e % 2][:, ft, :], bankH[ft][:], ACT.Gelu,
                              bias=mp_sb[:, MP_B1 + e * FT + ft:MP_B1 + e * FT + ft + 1]).then_inc(egelu_done, 1)
                        if e == 2:
                            act.wait_ge(combT_made, M + 1)
                            A(combT[:], bankR[0:E, :], ACT.Copy).then_inc(combT_ready, 1)
                        if e == 5 and not last:
                            evac_x(xt_exp(round_, M) + 1, [xnT2, xnT][p])

                M0 = round_ * JOBS
                evac_x(xt_exp(round_, M0), xnT)
                job(M0, 0, round_ == 0, False)
                job(M0 + 1, 1, False, False)
                with act.Fori(0, 2) as it:
                    _plain(act)
                    job(M0 + 2 + it * 2, 0, False, False)
                    job(M0 + 3 + it * 2, 1, False, False)
                job(M0 + 6, 0, False, False)
                job(M0 + 7, 1, False, True)

            experts(0)
            attention(ENC, JOBS, True)
            experts(1)

        @block.vector
        def _(dve):
            v = nc.vector

            def ln_stats(n, J, steps=ln_step):
                ch = Chain(dve, steps, n, 3)
                for t in range(TT):
                    last = v.bn_stats(stats[:, t, :], tile1(xs, J, t))
                ch.link(last)
                v.tensor_copy(spare[:, 0:1], half[:, 0:1])
                for t in range(TT):
                    last = v.bn_aggr(mv[:, t, :], stats[:, t, :])
                ch.link(last)
                ch.link(v.tensor_scalar(veps[:], mv[:, :, 1], EPS, None, ALU.add), wait=False)
                ch.end()

            def ln_apply(n, J, power=rstd_ready, done=xn_ready, in_place=False):
                dve.wait_ge(power, n + 1)
                for t in range(TT):
                    row = tile1(xs, J, t)
                    last = v.tensor_scalar(row if in_place else xn[:, t, :], row, mv[:, t, 0:1], rstd[:, t:t + 1],
                                           ALU.subtract, ALU.mult)
                last.then_inc(done, 1)

            def attention(base, jobs, rope_job):
                def stream(b, j):
                    if isinstance(b, int):
                        return j % JOBS
                    return (b + j) & (JOBS - 1)

                def lns(b, j):
                    ln_stats(ln_index(b, j), stream(b, j))

                def lna(b, j):
                    if j >= 1:
                        dve.wait_ge(xt_ready, (XT_B if rope_job else b) + j)
                    if j >= 4 and not rope_job:
                        dve.wait_ge(fxt_ready, b + j - 3)
                    ln_apply(ln_index(b, j), stream(b, j))

                def first_ln(b, j, k):
                    if b == 0 and j == 0 if isinstance(b, int) else False:
                        dve.wait_ge(x_loaded, 16)
                        ln_stats(ln_init(k), k)
                        ln_apply(ln_init(k), k, in_place=True)
                        dve.wait_ge(xn_ready, ln_init(k) + 1)

                def split1(b, j, k):
                    dve.wait_ge(qk_ready, 2 * (b + j) + k + 1)
                    if j >= 1:
                        dve.wait_ge(parts_stored, 96 * (b + j))
                    v.tensor_copy(parts[:, k, 0, :], qk[:, k, :]).then_inc(p1_ready, 1)

                def split2(b, j, k):
                    dve.wait_ge(r1_ready, 2 * (b + j) + k + 1)
                    v.tensor_copy(parts[:, k, 1, :], resid[:, k, :]).then_inc(p2_ready, 1)

                def rotate(b, j, n):
                    k = n // 2
                    if j == 0 and n == 0:
                        dve.wait_ge(rope_loaded, 16)
                    dve.wait_ge(rproj_ready, ROPE_EACH * j + n + 1)
                    if n % 2 == 0:
                        if k == 0 and j >= 1:
                            dve.wait_ge(p3_ready, 2 * (b + j))
                        v.tensor_tensor(qk[:, k, :], bankF[:], rope_sb[:, 2 * k, :], ALU.mult).then_inc(rproj_used, 1)
                    else:
                        v.tensor_tensor(rtmp[:, k, :], bankF[:], rope_sb[:, 2 * k + 1, :],
                                        ALU.mult).then_inc(rproj_used, 1)
                        dve.wait_ge(rproj_used, ROPE_EACH * j + n + 1)
                        v.tensor_tensor(qk[:, k, :], qk[:, k, :], rtmp[:, k, :], ALU.add).then_inc(qk_ready, 1)
                        split1(b, j, k)

                def take_v(b, j):
                    dve.wait_ge(proj_ready, (3 * ENC + j + 1) if rope_job else 3 * (b + j) + 3)
                    dst = V[j % 4][:, :, :, 0:HD]
                    src = bankF[:].rearrange("p (t h d) -> p t h d", t=TT, h=H)
                    if j >= 4:
                        dve.wait_ge(pv_done, QUADS * (b + j - 3))
                    if rope_job:
                        v.tensor_copy(dst, src).then_inc(v_ready, 1)
                    else:
                        bias = ap_sb[:, AP_BV:AP_BV + D].rearrange("p (h d) -> p h d", h=H)
                        v.tensor_tensor(dst, src, bias.unsqueeze(1).broadcast_to([P, TT, H, HD]),
                                        ALU.add).then_inc(v_ready, 1)

                def maxima(b, j, c):
                    pair, k = divmod(c, CPP)
                    dve.wait_ge(a_ready, CHUNKS * (b + j) + c + 1)
                    bk = bankA[c % 2]
                    if k < 4:
                        h = 2 * pair + k // 2
                        dst = mx[:, h, 4 * (k % 2):4 * (k % 2) + 4]
                        src = bk[:].rearrange("p (n c) -> p n c", n=4)
                    else:
                        dst = mx[:, 2 * pair:2 * pair + 2, 8:10]
                        src = bk[:].rearrange("p (h n c) -> p h n c", h=2, n=2)
                    v.tensor_reduce(dst, src, axis=AX.X, op=ALU.max).then_inc(a_used, 1)

                def negate_split(b, j):
                    ch = Chain(dve, max_step, b + j, 4)
                    dve.wait_ge(a_used, CHUNKS * (b + j + 1))
                    for t, (lo, n) in enumerate([(7, 1), (8, 2), (4, 3), (0, 4)]):
                        last = v.tensor_reduce(mneg[:, t, :], mx[:, :, lo:lo + n], axis=AX.X, op=ALU.max, negate=True)
                    ch.link(last)
                    if j >= 1:
                        dve.wait_ge(mT_made, b + j)
                    ch.link(v.tensor_copy(mparts[:, :, 0 * H:1 * H], mneg[:]))
                    ch.link(v.tensor_tensor(mres[:], mneg[:], mparts[:, :, 0 * H:1 * H], ALU.subtract))
                    ch.link(v.tensor_copy(mparts[:, :, 1 * H:2 * H], mres[:]))
                    ch.end()
                    v.tensor_tensor(mparts[:, :, 2 * H:3 * H], mres[:], mparts[:, :, 1 * H:2 * H],
                                    ALU.subtract).then_inc(mparts_ready, 1)

                def evac_max(b, j):
                    dve.wait_ge(mT_made, b + j + 1)
                    if j >= 1:
                        dve.wait_ge(m_loaded, 48 * (b + j))
                    v.tensor_copy(mT[:], mT_ps[0:NPART * H, :]).then_inc(mT_ready, 1)

                def normalise(b, j, t):
                    dve.wait_ge(otT_ready, TT * (b + j) + t + 1)
                    heads = bankR[:].rearrange("p (h c) -> p h c", h=H)
                    ch = Chain(dve, norm_step, TT * (b + j) + t, 1)
                    ch.link(v.reciprocal(rl[:], heads[:, :, HD]))
                    ch.end()
                    if t == 0 and j > 0:
                        dve.wait_ge(attnT_made, b + j)
                    v.tensor_tensor(attn[:, t, :].rearrange("p (h d) -> p h d", h=H), heads[:, :, 0:HD],
                                    rl[:].unsqueeze(2).broadcast_to([P, H, HD]), ALU.mult).then_inc(norm_done, 1)

                def add_x(b, j):
                    dve.wait_ge(o_ready, b + j + 1)
                    rows = tiles(xs, stream(b, j))
                    o = bankR[:].rearrange("p (t d) -> p t d", t=TT)
                    v.tensor_tensor(rows, rows, o, ALU.add).then_inc(x_added, 1)
                    dve.wait_ge(x_added, 2 * (b + j) + 1)
                    if rope_job:
                        v.tensor_copy(spare[:, 0:1], half[:, 0:1]).then_inc(x_added, 1)
                    else:
                        bo = fp_sb[:, FP_BO:FP_BO + D].unsqueeze(1).broadcast_to([P, TT, D])
                        v.tensor_tensor(rows, rows, bo, ALU.add).then_inc(x_added, 1)

                def ffn_lns(b, j):
                    dve.wait_ge(x_added, 2 * (b + j + 1))
                    ln_stats(b + j, stream(b, j), fln_step)

                def ffn_lna(b, j):
                    ln_apply(b + j, stream(b, j), frstd_ready, fxn_ready)

                def ffn_add(b, j):
                    dve.wait_ge(y_ready, b + j + 1)
                    rows = tiles(xs, stream(b, j))
                    y = bankR[:].rearrange("p (t d) -> p t d", t=TT)
                    v.tensor_tensor(rows, rows, y, ALU.add).then_inc(f_added, 1)
                    dve.wait_ge(f_added, 2 * (b + j) + 1)
                    b2 = fp_sb[:, FP_B2:FP_B2 + D].unsqueeze(1).broadcast_to([P, TT, D])
                    v.tensor_tensor(rows, rows, b2, ALU.add).then_inc(f_added, 1)

                extras = []
                if rope_job:
                    extras += [(lambda b, j, n=n: rotate(b, j, n), 2, (4 + 2 * n, 1)) for n in range(4)]
                    extras += [(lambda b, j: split2(b, j, 0), 2, (11, 1)), (take_v, 2, (13, 1)),
                               (lambda b, j: split2(b, j, 1), 2, (15, 1))]
                else:
                    extras += [(lambda b, j: split1(b, j, 0), 2, (5, 1)), (lambda b, j: split1(b, j, 1), 2, (8, 1)),
                               (lambda b, j: split2(b, j, 0), 2, (9, 1)), (take_v, 2, (10, 1)),
                               (lambda b, j: split2(b, j, 1), 2, (12, 1))]
                extras += [(lambda b, j, t=t: normalise(b, j, t), -1, (7 + 2 * t, 1)) for t in range(TT)]
                extras += [(add_x, -1, (19, 1)), (negate_split, 1, (29, 1)), (evac_max, 1, (34, 1)),
                           (lns, 3, (35, 1)), (lna, 3, (38, 1))]
                if not rope_job:
                    extras += [(ffn_lns, -1, (20, 1)), (ffn_lna, -1, (22, 1)), (ffn_add, -1, (32, 1))]
                    extras += [(lambda b, j, k=k: first_ln(b, j, k), 2, (13 + k, 1)) for k in range(1, JOBS)]
                    first_ln(0, 0, 0)
                lns(base, 0)
                lna(base, 0)
                iterations(dve, base, jobs, maxima, None, extras)

            def experts(round_):
                ROUTE = 22
                cnb = cn[:, 2, :]

                def route(M, p):
                    ch = Chain(dve, route_step, M, ROUTE)
                    n2, nrm, sc, xn2, omx, mn, ws = (s4[:, i, :] for i in range(7))
                    dot, t1, a, ap1, s, root, tt_, w, den, sel = (s8[:, i, :, :] for i in range(10))
                    lt, eq, rk = (s88[:, i, :, :] for i in range(3))

                    def b8(x):
                        return x.unsqueeze(2).broadcast_to([P, TT, E])

                    def row8(x):
                        return x.unsqueeze(1).broadcast_to([P, TT, E])

                    dve.wait_ge(r_ready, M + 1)
                    ch.link(v.tensor_copy(R[:], bankR[:, 0:64].rearrange("p (t c) -> p t c", t=TT)[:, :, 0:E + 1]))
                    ch.link(v.tensor_copy(n2, R[:, :, E]), wait=False)
                    dve.wait_ge(route_pow, 2 * M + 1)
                    ch.link(v.tensor_scalar(nrm, nrm, 1e-7, None, ALU.max))
                    ch.link(v.reciprocal(sc, nrm))
                    ch.link(v.tensor_scalar(sc, sc, 0.95, 1.0, ALU.mult, ALU.min))
                    ch.link(v.tensor_tensor(xn2, n2, sc, ALU.mult))
                    ch.link(v.tensor_tensor(xn2, xn2, sc, ALU.mult))
                    ch.link(v.tensor_scalar(xn2, xn2, 0.99, None, ALU.min))
                    ch.link(v.tensor_tensor(dot, R[:, :, 0:E], b8(sc), ALU.mult))
                    ch.link(v.tensor_scalar(t1, dot, -2.0, None, ALU.mult))
                    ch.link(v.tensor_tensor(t1, t1, row8(cnb), ALU.add))
                    ch.link(v.tensor_tensor(t1, t1, b8(xn2), ALU.add))
                    v.tensor_scalar(omx, xn2, -1.0, 1.0, ALU.mult, ALU.add)
                    ch.link(v.tensor_scalar(t1, t1, 0.0, 2.0, ALU.max, ALU.mult))
                    ch.link(v.tensor_tensor(den, b8(omx), row8(cn[:, 1, :]), ALU.mult))
                    ch.link(v.tensor_scalar(den, den, 1e-7, None, ALU.add))
                    ch.link(v.reciprocal(den, den))
                    ch.link(v.tensor_tensor(a, t1, den, ALU.mult))
                    ch.link(v.tensor_scalar(a, a, 1.0, 1.0 + 1e-7, ALU.add, ALU.max))
                    v.tensor_scalar(ap1, a, 1.0, None, ALU.add)
                    ch.link(v.tensor_scalar(root, a, -1.0, None, ALU.add))
                    ch.link(v.tensor_tensor(s, root, ap1, ALU.mult), wait=False)
                    ae = a.unsqueeze(3).broadcast_to([P, TT, E, E])
                    aj = a.unsqueeze(2).broadcast_to([P, TT, E, E])

                    def e88(x):
                        return x.rearrange("p t (e j) -> p t e j", e=E)

                    v.tensor_tensor(e88(lt), aj, ae, ALU.is_lt)
                    ch.link(v.tensor_tensor(e88(eq), aj, ae, ALU.is_equal))
                    trib = tri[:].rearrange("p e j -> p (e j)").unsqueeze(1).broadcast_to([P, TT, E * E])
                    ch.link(v.tensor_tensor(rk, eq, trib, ALU.mult))
                    ch.end()
                    return lt, eq, rk, sel, a, root, tt_, w, mn, ws

                def route2(M, p, vals):
                    lt, eq, rk, sel, a, root, tt_, w, mn, ws = vals
                    ch = Chain(dve, c_step, M, 11)
                    ch.base = ch.base + 4

                    def b8(x):
                        return x.unsqueeze(2).broadcast_to([P, TT, E])

                    ch.link(v.tensor_tensor(lt, lt, rk, ALU.add))
                    ch.link(v.tensor_reduce(sel, lt.rearrange("p t (e j) -> p t e j", e=E), axis=AX.X, op=ALU.add))
                    ch.link(v.tensor_scalar(sel, sel, 1.5, None, ALU.is_lt))
                    dve.wait_ge(route_pow, 2 * M + 2)
                    ch.link(v.tensor_tensor(tt_, a, root, ALU.add))
                    ch.link(v.tensor_reduce(mn, tt_, axis=AX.X, op=ALU.min))
                    ch.link(v.reciprocal(w, tt_))
                    ch.link(v.tensor_tensor(w, w, b8(mn), ALU.mult))
                    ch.link(v.tensor_tensor(w, w, sel, ALU.mult))
                    ch.link(v.tensor_reduce(ws, w, axis=AX.X, op=ALU.add))
                    ch.link(v.reciprocal(ws, ws))
                    ch.link(v.tensor_tensor(comb[p][:], w, b8(ws), ALU.mult))
                    ch.end()
                    v.tensor_copy(ws, mn).then_inc(comb_ready, 1)

                def ln(M, J, p):
                    if round_ == 0:
                        rows = tiles(xs, J)
                        ln_stats(ln_final(M), J)
                        ln_apply(ln_final(M), J, in_place=True)
                        dve.wait_ge(xn_ready, ln_final(M) + 1)
                        ch = Chain(dve, fin_step, M, 3)
                        fw = fin_sb[:, 0:D].unsqueeze(1).broadcast_to([P, TT, D])
                        fb = fin_sb[:, D:2 * D].unsqueeze(1).broadcast_to([P, TT, D])
                        ch.link(v.tensor_tensor(rows, rows, fw, ALU.mult))
                        ch.link(v.tensor_tensor(rows, rows, fb, ALU.add))
                        dve.wait_ge(xr_loaded[p], 8 * M + 16 - 8 * p)
                        ch.link(v.tensor_tensor(rows, rows, xload[:, p, :, :], ALU.add))
                        ch.end()
                    ln_stats(ln_exp(round_, M), J)
                    dve.wait_ge(xt_ready, xt_exp(round_, M))
                    ln_apply(ln_exp(round_, M), J)

                def job(M, J, p, last):
                    vals = route(M, p)
                    route2(M, p, vals)
                    for e in range(E):
                        EI = M * E + e
                        if e == 1:
                            dve.wait_ge(b2_ready, M + 1)
                            rows = tiles(xs, J)
                            v.tensor_tensor(rows, rows, bankR[:].rearrange("p (t d) -> p t d", t=TT),
                                            ALU.add).then_inc(b2_added, 1)
                            dve.wait_ge(b2_added, M + 1)
                        dve.wait_ge(ey_ready, EI + 1)
                        for t in range(TT):
                            row = tile1(xs, J, t)
                            ins = v.scalar_tensor_tensor(out=row, in0=bankY[e % 2][:, t * D:(t + 1) * D],
                                                         scalar=comb[p][:, t, e:e + 1], in1=row,
                                                         op0=ALU.mult, op1=ALU.add)
                        ins.then_inc(ey_used, 1)
                        dve.wait_ge(ey_used, EI + 1)
                        if e == 3 and not last:
                            ln(M + 1, J + 1, 1 - p)
                    if round_ == 1:
                        v.tensor_copy(spare[:, 0:1], half[:, 0:1]).then_inc(out_ready, 1)

                M0 = round_ * JOBS
                ln(M0, 0, 0)
                if round_ == 0:
                    n = [0]

                    def step(ins):
                        n[0] += 1
                        ins.then_inc(cproj_step, 1)
                        dve.wait_ge(cproj_step, n[0])
                    c = mp_sb[:, MP_C:MP_C + E]
                    v.tensor_tensor(cn[:, 0, :], c, c, ALU.mult).then_inc(c_step, 1)
                    dve.wait_ge(c_made, 1)
                    ch = Chain(dve, c_step, 0, 4)
                    ch.k = 1
                    ch.link(v.tensor_copy(cn[:, 2, :], bankR[:, 0:E]), wait=False)
                    dve.wait_ge(cproj_pow, 1)
                    step(v.tensor_scalar(cn[:, 1, :], cn[:, 1, :], 1e-7, None, ALU.max))
                    step(v.reciprocal(cn[:, 1, :], cn[:, 1, :]))
                    step(v.tensor_scalar(cn[:, 1, :], cn[:, 1, :], 0.95, 1.0, ALU.mult, ALU.min))
                    step(v.tensor_tensor(cproj[:], c, cn[:, 1, :], ALU.mult))
                    step(v.tensor_tensor(cn[:, 2, :], cn[:, 2, :], cn[:, 1, :], ALU.mult))
                    step(v.tensor_tensor(cn[:, 2, :], cn[:, 2, :], cn[:, 1, :], ALU.mult))
                    step(v.tensor_scalar(cn[:, 2, :], cn[:, 2, :], 0.99, None, ALU.min))
                    ch.link(v.tensor_scalar(cn[:, 1, :], cn[:, 2, :], -1.0, 1.0, ALU.mult, ALU.add))
                    ch.link(v.tensor_copy(cn[:, 0, :], cn[:, 2, :]))
                    v.tensor_copy(spare[:, 0:1], half[:, 0:1]).then_inc(cproj_ready, 1)
                job(M0, 0, 0, False)
                job(M0 + 1, 1, 1, False)
                with dve.Fori(0, 2) as it:
                    _plain(dve)
                    job(M0 + 2 + it * 2, 2 + it * 2, 0, False)
                    job(M0 + 3 + it * 2, 3 + it * 2, 1, False)
                job(M0 + 6, 6, 0, False)
                job(M0 + 7, 7, 1, True)

            v.memset(bankPV[:], 0.0).then_inc(pv_clear, 1)
            dve.wait_ge(const_done, 11)
            dve.wait_ge(load_const, 16 * 4)
            attention(0, ENC, False)
            dve.wait_ge(f_added, 2 * ENC)
            experts(0)
            attention(ENC, JOBS, True)
            dve.wait_ge(x_added, 2 * (ENC + JOBS))
            experts(1)

        @block.gpsimd
        def _(pool):
            g = nc.gpsimd
            g.memset(ident[:], 0.0).then_inc(const_zero, 1)
            g.memset(ident_b[:], 0.0).then_inc(const_zero, 1)
            g.memset(mask_a[:], 0.0).then_inc(const_zero, 1)
            g.memset(mask_b[:], 0.0).then_inc(const_zero, 1)
            g.memset(tri[:], 1.0).then_inc(const_zero, 1)
            pool.wait_ge(const_zero, 5)
            for m in (ident, ident_b):
                g.affine_select(out=m[:], in_=m[:], compare_op=ALU.not_equal, fill=1.0, base=0,
                                pattern=[[-1, P]], channel_multiplier=1).then_inc(const_done, 1)
            g.affine_select(out=mask_a[:], in_=mask_a[:], compare_op=ALU.is_ge, fill=NEG, base=0,
                            pattern=[[-1, P]], channel_multiplier=1).then_inc(const_done, 1)
            g.affine_select(out=mask_b[:], in_=mask_b[:], compare_op=ALU.is_ge, fill=NEG, base=0,
                            pattern=[[1, P]], channel_multiplier=-1).then_inc(const_done, 1)
            g.affine_select(out=tri[:], in_=tri[:], compare_op=ALU.is_gt, fill=0.0, base=0,
                            pattern=[[1, E], [-1, E]], channel_multiplier=0).then_inc(const_done, 1)
            g.memset(half[:], 0.5).then_inc(const_done, 1)
            g.memset(mhalf[:], -0.5).then_inc(const_done, 1)
            g.memset(ones[:], 1.0).then_inc(const_done, 1)
            pool.wait_ge(const_done, 8)
            for i in range(2):
                g.memset(QS[i][64:P, :, :], 0.0).then_inc(const_zero, 1)
                g.memset(KS[i][64:P, :, :], 0.0).then_inc(const_zero, 1)
            pool.wait_ge(const_zero, 9)
            for i in range(2):
                last = g.memset(KS[i][ROW_MAX:ROWS, :, :], 1.0)
            last.then_inc(const_done, 1)
            pool.wait_ge(const_done, 9)
            g.memset(mparts[:], 0.0)
            for i in range(len(V)):
                last = g.memset(V[i][:], 1.0)
            last.then_inc(const_done, 1)
            g.memset(big[:, 0:1], 0.0).then_inc(const_done, 1)
            for i in range(2):
                g.dma_start(QS[i][ROW_ALIBI:ROW_ALIBI + N_ALIBI, :, :], alibi[0]).then_inc(alibi_loaded, 16)
                g.dma_start(KS[i][ROW_ALIBI:ROW_ALIBI + N_ALIBI, :, :], alibi[1]).then_inc(alibi_loaded, 16)

            def rsqrt(n, steps=ln_step, done=rstd_ready):
                pool.wait_ge(steps, 3 * n + 3)
                g.tensor_tensor(rstd[:], veps[:], mhalf[:], ALU.pow).then_inc(done, 1)

            def first_ln(b, j, k):
                if b == 0 and j == 0 if isinstance(b, int) else False:
                    rsqrt(ln_init(k))

            def attention(base, jobs, rope_job):
                def split(b, j, k):
                    n = 2 * (b + j) + k
                    pool.wait_ge(p1_ready, n + 1)
                    g.tensor_tensor(resid[:, k, :], qk[:, k, :], parts[:, k, 0, :], ALU.subtract).then_inc(r1_ready, 1)

                def split3(b, j, k):
                    n = 2 * (b + j) + k
                    pool.wait_ge(p2_ready, n + 1)
                    g.tensor_tensor(parts[:, k, 2, :], resid[:, k, :], parts[:, k, 1, :],
                                    ALU.subtract).then_inc(p3_ready, 1)

                extras = [(lambda b, j: split(b, j, 0), 2, (5, 1)), (lambda b, j: split(b, j, 1), 2, (8, 1)),
                          (lambda b, j: split3(b, j, 0), 2, (10, 1)), (lambda b, j: split3(b, j, 1), 2, (13, 1)),
                          (lambda b, j: rsqrt(ln_index(b, j)), 3, (36, 1))]
                if not rope_job:
                    extras += [(lambda b, j: rsqrt(b + j, fln_step, frstd_ready), -1, (21, 1))]
                    extras += [(lambda b, j, k=k: first_ln(b, j, k), 2, (13 + k, 1)) for k in range(1, JOBS)]
                    rsqrt(0)
                rsqrt(ln_index(base, 0))
                iterations(pool, base, jobs, None, None, extras)

            def experts(round_):
                def rows(M):
                    if round_ == 0:
                        rsqrt(ln_final(M))
                    rsqrt(ln_exp(round_, M))

                def job(M, last):
                    pool.wait_ge(route_step, 22 * M + 2)
                    g.tensor_tensor(s4[:, 1, :], s4[:, 0, :], half[:], ALU.pow).then_inc(route_pow, 1)
                    pool.wait_ge(route_step, 22 * M + 20)
                    g.tensor_tensor(s8[:, 5, :, :], s8[:, 4, :, :],
                                    half[:].unsqueeze(2).broadcast_to([P, TT, E]), ALU.pow).then_inc(route_pow, 1)
                    if not last:
                        rows(M + 1)
                M0 = round_ * JOBS
                rows(M0)
                if round_ == 0:
                    pool.wait_ge(c_step, 2)
                    g.tensor_tensor(cn[:, 1, :], cn[:, 2, :], half[:, 0:1].broadcast_to([P, E]),
                                    ALU.pow).then_inc(cproj_pow, 1)
                job(M0, False)
                job(M0 + 1, False)
                with pool.Fori(0, 2) as it:
                    _plain(pool)
                    job(M0 + 2 + it * 2, False)
                    job(M0 + 3 + it * 2, False)
                job(M0 + 6, False)
                job(M0 + 7, True)

            attention(0, ENC, False)
            pool.wait_ge(x_added, 2 * ENC)
            for i in range(2):
                g.dma_start(QS[i][ROW_ALIBI:ROW_ALIBI + N_ALIBI, :, :], alibi[2]).then_inc(alibi_cleared, 16)
            experts(0)
            attention(ENC, JOBS, True)
            experts(1)

        @block.sync
        def _(sp):
            xv = x.rearrange("b (t p) d -> p (b t) d", p=P)
            ov = out.rearrange("b (t p) d -> p (b t) d", p=P)
            sp.dma_start(xs[:], xv).then_inc(x_loaded, 16)
            for dst, src in ((ap_sb, apack[0]), (fp_sb, fpack[0])):
                sp.dma_start(dst[:], src).then_inc(apack_loaded if dst is ap_sb else fpack_loaded, 16)
            for dst, src in ((fin_sb, final), (bp_sb, bpack), (mp_sb, mpack), (b2_sb, b2e)):
                sp.dma_start(dst[:], src).then_inc(load_const, 16)

            def attention(base, jobs, rope_job):
                def layer(b, j):
                    return (b + j) // JOBS if isinstance(b, int) else ((b + j) >> 3) & (LAYERS - 1)

                def load_front(b, j):
                    if j % 4 == 0:
                        sp.wait_ge(v_ready, b + j)
                        src = apack[bass.ds(layer(b, j), 1)].rearrange("a p n -> p (a n)")
                        sp.dma_start(ap_sb[:], src).then_inc(apack_loaded, 16)

                def load_rear(b, j):
                    if j % 4 == 0 and j > 0:
                        sp.wait_ge(f_added, 2 * (b + j))
                        src = fpack[bass.ds(layer(b, j), 1)].rearrange("a p n -> p (a n)")
                        sp.dma_start(fp_sb[:], src).then_inc(fpack_loaded, 16)

                def store(b, j):
                    for k in range(2):
                        sp.wait_ge(p3_ready, 2 * (b + j) + k + 1)
                        for a in range(NPART):
                            sp.dma_start(part_scr[j % 2, k, a], parts[:, k, a, :]).then_inc(parts_stored, 16)

                def load(b, j, q):
                    if q == 0:
                        sp.wait_ge(parts_stored, 96 * (b + j + 1))
                    if j >= 2:
                        sp.wait_ge(b_ready, CHUNKS * (b + j - 2) + CPQ * (q + 1))
                    for a in range(NPART):
                        for k, S in ((0, QS), (1, KS)):
                            src = part_scr[j % 2, k, a].rearrange("(d h) t -> d (h t)", d=HD)
                            src = src[:, q * 4 * T:(q + 1) * 4 * T]
                            if k == 0:
                                s3 = src.unsqueeze(0).broadcast_to([NPART, HD, 4 * T])
                                dst = S[j % 2][a * 24:(a + 1) * 24, 4 * q:4 * q + 4, :]
                                sp.dma_start(dst, s3).then_inc(stack_loaded[q], 16)
                            else:
                                for r in range(NPART):
                                    dst = S[j % 2][r * 24 + a * 8:r * 24 + a * 8 + 8, 4 * q:4 * q + 4, :]
                                    sp.dma_start(dst, src).then_inc(stack_loaded[q], 16)

                def load_max(b, j):
                    sp.wait_ge(mT_ready, b + j + 1)
                    for a in range(NPART):
                        sp.dma_start(QS[j % 2][ROW_MAX + a:ROW_MAX + a + 1, :, :],
                                     mT[a * H:(a + 1) * H, :]).then_inc(m_loaded, 16)

                extras = [(store, 2, (14, 1)), (lambda b, j: load(b, j, 0), 2, (15, 1)),
                          (lambda b, j: load(b, j, 1), 2, (20, 1)), (lambda b, j: load(b, j, 2), 2, (30, 1)),
                          (load_max, 1, (35, 1)), (lambda b, j: load(b, j, 3), 2, (39, 1))]
                if not rope_job:
                    extras += [(load_front, 3, (16, 1)), (load_rear, 0, (36, 1))]
                iterations(sp, base, jobs, None, None, extras)

            sp.wait_ge(alibi_loaded, 64)
            attention(0, ENC, False)
            sp.wait_ge(f_added, 2 * ENC)

            def load_experts():
                sp.dma_start(big[:, 0:4096], w1e).then_inc(mw_loaded, 16)
                sp.dma_start(big[:, 4096:8192], w2e).then_inc(mw_loaded, 16)

            load_experts()
            for j in range(JOBS):
                if j >= 2:
                    sp.wait_ge(fin_step, 3 * (j - 1))
                sp.dma_start(xload[:, j % 2, :, :], xv[:, j * TT:(j + 1) * TT, :]).then_inc(xr_loaded[j % 2], 16)
            sp.wait_ge(ey_used, E * JOBS)
            sp.dma_start(rope_sb, rope).then_inc(rope_loaded, 16)
            sp.wait_ge(alibi_cleared, 32)
            attention(ENC, JOBS, True)
            sp.wait_ge(x_added, 80)
            load_experts()
            for j in range(JOBS):
                sp.wait_ge(out_ready, j + 1)
                sp.dma_start(ov[:, j * TT:(j + 1) * TT, :], xs[:, j * TT:(j + 1) * TT, :]).then_inc(stored, 16)
            sp.wait_ge(stored, 16 * JOBS)


def kernel(**inputs):
    import concourse.bacc as _bacc
    from concourse.bass_utils import run_bass_kernel_spmd as _run

    a = {k[3:] if k.startswith("L0_") else k: np.asarray(v) for k, v in inputs.items()}
    f = np.float32
    dh = np.arange(D).reshape(H, HD).T.reshape(-1)
    swap = (np.arange(D) ^ 1)[dh]

    def rep(v):
        return np.broadcast_to(v[..., None, :], (*v.shape[:-1], P, v.shape[-1]))

    wi = a["attn_a_in_proj_w"].reshape(LAYERS, 3, D, D)
    bi = a["attn_a_in_proj_b"].reshape(LAYERS, 3, D)
    T21 = (0, 2, 1)
    apack = np.concatenate([
        wi[:, 0][:, dh].transpose(T21), wi[:, 1][:, dh].transpose(T21), wi[:, 2].transpose(T21),
        rep(bi[:, 2]), a["attn_a_ln1_w"][:, :, None], a["attn_a_ln1_b"][:, :, None],
        bi[:, 0][:, dh][:, :, None], bi[:, 1][:, dh][:, :, None]], axis=2)
    fpack = np.concatenate([
        a["attn_a_ffn1_w"].transpose(T21),
        a["attn_a_ffn2_w"].reshape(LAYERS, D, FT, P).transpose(0, 3, 2, 1).reshape(LAYERS, P, FT * D),
        rep(a["attn_a_ffn2_b"]), a["attn_a_out_proj_w"].transpose(T21), rep(a["attn_a_out_proj_b"]),
        a["attn_a_ln2_w"][:, :, None], a["attn_a_ln2_b"][:, :, None],
        a["attn_a_ffn1_b"].reshape(LAYERS, FT, P).transpose(T21)], axis=2)
    final = np.concatenate([rep(a["attn_a_final_w"]), rep(a["attn_a_final_b"])], axis=1)
    wq, wk = a["attn_b_W_q"], a["attn_b_W_k"]
    bpack = np.concatenate([wq[dh].T, wq[swap].T, wk[dh].T, wk[swap].T, a["attn_b_W_v"].T, a["attn_b_W_o"].T], axis=1)
    mpack = np.concatenate([a["ffn_centroids"].T, a["ffn_Wp"], a["ffn_bp"][:, None],
                            a["ffn_b1"].reshape(E, FT, P).transpose(2, 0, 1).reshape(P, E * FT)], axis=1)
    w1e = a["ffn_W1"].transpose(1, 0, 2).reshape(P, E * T)
    w2e = a["ffn_W2"].reshape(E, FT, P, D).transpose(2, 0, 1, 3).reshape(P, E * FT * D)

    def part(v):
        return (v.view(np.uint32) & np.uint32(0xFFFF0000)).view(f)
    slopes = ((2.0 ** -0.5) ** np.arange(1, H + 1)).astype(f)
    s1 = part(slopes)
    s2 = part(slopes - s1)
    s3 = slopes - s1 - s2
    pos = np.arange(T)
    hi, lo = (pos // 8 * 8).astype(f), (pos % 8).astype(f)
    alibi = np.zeros((3, N_ALIBI, H, T), f)
    for n, s in enumerate((s1, s2, s3)):
        for m, p in enumerate((hi, lo)):
            r = 2 * n + m
            alibi[0, r], alibi[1, r] = s[:, None], p[None]
            alibi[0, 6 + r], alibi[1, 6 + r] = p[None], -s[:, None]
    at = np.minimum(pos, 255).astype(f)
    theta = (10000.0 ** (-2.0 * np.arange(HD // 2, dtype=f) / HD)).astype(f)
    ang = at[None, :] * theta[:, None]
    cos, sin = np.cos(ang).astype(f), np.sin(ang).astype(f)
    dim = np.repeat(np.arange(HD), H)
    C, S = cos[dim // 2], sin[dim // 2] * np.where(dim % 2 == 0, -1, 1)[:, None].astype(f)
    r8 = f(1.0 / math.sqrt(HD))
    rope = np.stack([C * r8, S * r8, C, S], axis=1).astype(f)

    arrays = dict(x=a["attn_a_x"], apack=apack, fpack=fpack, final=final, bpack=bpack, mpack=mpack,
                  b2e=a["ffn_b2"], w1e=w1e, w2e=w2e, alibi=alibi, rope=rope)
    arrays = {f"in_{k}": np.ascontiguousarray(v) for k, v in arrays.items()}
    nc = _bacc.Bacc("TRN2", target_bir_lowering=False, num_devices=1)
    args = [nc.dram_tensor(k, v.shape, F32, kind="ExternalInput").ap() for k, v in arrays.items()]
    out = nc.dram_tensor("out_x", [JOBS, T, D], F32, kind="ExternalOutput").ap()
    part_scr = nc.dram_tensor("part_scr", [2, 2, NPART, P, T], BF16, kind="Internal").ap()
    hybrid_kernel(nc, *args, out, part_scr)
    r = _run(nc, [arrays], core_ids=[0])
    return r.results[0]["out_x"]
```

```python
import math
from contextlib import ExitStack

import numpy as np

import concourse.bass as bass
from concourse import mybir

F32 = mybir.dt.float32
BF16 = mybir.dt.bfloat16
ALU = mybir.AluOpType
ACT = mybir.ActivationFunctionType
AX = mybir.AxisListType

P = 128
D = 128
T = 512
TT = T // P
JOBS = 8
H, HD = 16, 8
LAYERS = 4
FT = 4
E = 8
EPS = 1e-5
NEG = -3.0e38

N_CONST = 13
ONES_PAIR = float(np.array([0x3F803F80], np.uint32).view(np.float32)[0])
NPART = 3
ROW_ALIBI = NPART * NPART * HD
N_ALIBI = 12
ROW_MAX = 96
ROWS = ROW_MAX + NPART
LOADS = 2 * NPART
PAIRS = H // 2
QUADS = H // 4
CPP = 5
CHUNKS = PAIRS * CPP
CPQ = 2 * CPP
HCOLS = 1280
SKEW = 2 * CPP

AP_QKV, AP_BV, AP_COL, AP_N = 0, 384, 512, 516
FP_W1, FP_W2, FP_B2, FP_WO, FP_BO, FP_COL, FP_N = 0, 512, 1024, 1152, 1280, 1408, 1414
BP_N = 6 * D
MP_C, MP_WP, MP_BP, MP_B1, MP_N = 0, 8, 136, 137, 137 + 32


def _plain(eng):
    eng.get_value_cache().nocache = True


def hybrid_kernel(nc, x, apack, fpack, final, bpack, mpack, b2e, w1e, w2e,
                  alibi, rope, out, part_scr):
    ctx = ExitStack()
    with ctx:
        def sb(name, shape, dt=F32):
            return ctx.enter_context(nc.sbuf_tensor(name, shape, dt))

        def sem(name):
            return ctx.enter_context(nc.semaphore(name))

        xs = sb("xs", [P, JOBS * TT, D])
        ident = sb("ident", [P, P])
        ident_b = sb("ident_b", [P, P], BF16)
        mask_a = sb("mask_a", [P, P], BF16)
        mask_b = sb("mask_b", [P, P], BF16)
        half = sb("half", [P, TT])
        mhalf = sb("mhalf", [P, TT])
        ones = sb("ones", [P, P])
        tri = sb("tri", [P, E, E])
        ap_sb = sb("ap_sb", [P, AP_N])
        fp_sb = sb("fp_sb", [P, FP_N])
        fin_sb = sb("fin_sb", [P, 2 * D])
        bp_sb = sb("bp_sb", [P, BP_N])
        mp_sb = sb("mp_sb", [P, MP_N])
        b2_sb = sb("b2_sb", [E, D])
        bqs = sb("bqs", [P, 1])
        stats = sb("stats", [P, TT, 6])
        mv = sb("mv", [P, TT, 2])
        veps = sb("veps", [P, TT])
        rstd = sb("rstd", [P, TT])
        xn = sb("xn", [P, TT, D])
        xnT = sb("xnT", [P, T])
        xnT2 = sb("xnT2", [P, T])
        qk = sb("qk", [P, 2, T])
        resid = sb("resid", [P, 2, T])
        rtmp = sb("rtmp", [P, 2, T])
        parts = sb("parts", [P, 2, NPART, T], BF16)
        QS = [sb(f"QS{i}", [P, H, T], BF16) for i in range(2)]
        KS = [sb(f"KS{i}", [P, H, T], BF16) for i in range(2)]
        V = [sb(f"V{i}", [P, TT, H, HD + 1]) for i in range(4)]
        big = sb("big", [P, 12288])
        Pq = [big[:, n * 4 * HCOLS:(n + 1) * 4 * HCOLS].rearrange("p (h c) -> p h c", h=4) for n in range(2)]
        W1 = big[:, 0:4096].rearrange("p (e f) -> p e f", e=E)
        W2 = big[:, 4096:8192].rearrange("p (e f d) -> p e f d", e=E, f=FT)
        fhT = big[:, 8 * HCOLS:12288].rearrange("p (f t) -> p f t", f=FT)
        rope_sb = big[:, 8 * HCOLS:12288].rearrange("p (n t) -> p n t", n=4)
        hT = [big[:, 8192 + 2048 * n:8192 + 2048 * (n + 1)].rearrange("p (f t) -> p f t", f=FT) for n in range(2)]
        mx = sb("mx", [P, H, 10])
        mneg = sb("mneg", [P, TT, H])
        mres = sb("mres", [P, TT, H])
        mparts = sb("mparts", [P, TT, P], BF16)
        mT = sb("mT", [NPART * H, T], BF16)
        spare = sb("spare", [P, 4])
        OT = sb("OT", [P, QUADS, T])
        rl = sb("rl", [P, H])
        attn = sb("attn", [P, TT, D])
        attnT = sb("attnT", [P, T])
        xload = resid[:].rearrange("p k (t d) -> p k t d", t=TT)
        xpT, sqT = qk[:, 0, :], qk[:, 1, :]
        cproj = sb("cproj", [P, E])
        cn = sb("cn", [P, 3, E])
        R = sb("R", [P, TT, E + 1])
        s4 = sb("s4", [P, 12, TT])
        s8 = sb("s8", [P, 10, TT, E])
        s88 = OT[:, 0:2, :].rearrange("p g c -> p (g c)")[:, 0:3 * TT * E * E].rearrange(
            "p (i t e) -> p i t e", i=3, t=TT)
        comb = [sb(f"comb{n}", [P, TT, E]) for n in range(2)]
        combT = sb("combT", [E, T])

        bank = [ctx.enter_context(nc.psum_tensor(f"bank{i}", [P, T], F32)) for i in range(8)]
        bankA, bankB = bank[0:3], bank[3:5]
        bankPV, bankF, bankR = bank[5], bank[6], bank[7]
        mT_ps = bankF[:, 0:T // 2].bitcast(BF16)
        bankH, bankY = bank[0:4], bank[4:6]
        bankG = [bankF, bankR, bankPV, bankF]

        const_done = sem("const_done")
        const_zero = sem("const_zero")
        pv_clear = sem("pv_clear")
        load_const = sem("load_const")
        alibi_loaded = [sem(f"alibi_loaded{n}") for n in range(2)]
        alibi_cleared = sem("alibi_cleared")
        x_loaded = [sem(f"x_loaded{n}") for n in range(2)]
        xr_loaded = [sem(f"xr_loaded{n}") for n in range(2)]
        rope_loaded = sem("rope_loaded")
        fln_step = sem("fln_step")
        frstd_ready = sem("frstd_ready")
        fxn_ready = sem("fxn_ready")
        fxt_ready = sem("fxt_ready")
        fxnT_ready = sem("fxnT_ready")
        apack_loaded = sem("apack_loaded")
        fpack_loaded = sem("fpack_loaded")
        mw_loaded = [sem(f"mw_loaded{n}") for n in range(2)]
        bqs_ready = sem("bqs_ready")
        ln_step = sem("ln_step")
        rstd_ready = sem("rstd_ready")
        xn_ready = sem("xn_ready")
        xt_ready = sem("xt_ready")
        xnT_ready = sem("xnT_ready")
        fin_step = sem("fin_step")
        proj_ready = sem("proj_ready")
        qk_ready = sem("qk_ready")
        rproj_ready = sem("rproj_ready")
        rproj_used = sem("rproj_used")
        v_ready = sem("v_ready")
        p1_ready = sem("p1_ready")
        p2_ready = sem("p2_ready")
        r1_ready = sem("r1_ready")
        p3_ready = sem("p3_ready")
        parts_stored = sem("parts_stored")
        stack_loaded = [sem(f"stack_loaded{g}") for g in range(QUADS)]
        a_ready = sem("a_ready")
        a_used = sem("a_used")
        max_step = sem("max_step")
        mparts_ready = sem("mparts_ready")
        mT_made = sem("mT_made")
        mT_ready = sem("mT_ready")
        m_loaded = sem("m_loaded")
        b_ready = sem("b_ready")
        exp_done = sem("exp_done")
        pv_done = sem("pv_done")
        ot_done = sem("ot_done")
        otT_ready = sem("otT_ready")
        norm_step = sem("norm_step")
        norm_done = sem("norm_done")
        attnT_made = sem("attnT_made")
        attnT_ready = sem("attnT_ready")
        o_ready = sem("o_ready")
        x_added = sem("x_added")
        h_ready = sem("h_ready")
        gelu_done = sem("gelu_done")
        y_ready = sem("y_ready")
        f_added = sem("f_added")
        eh_ready = sem("eh_ready")
        egelu_done = sem("egelu_done")
        ey_ready = sem("ey_ready")
        ey_used = sem("ey_used")
        c_made = sem("c_made")
        c_step = sem("c_step")
        cproj_step = sem("cproj_step")
        cproj_pow = sem("cproj_pow")
        cproj_ready = sem("cproj_ready")
        xp_ready = sem("xp_ready")
        xpT_ready = sem("xpT_ready")
        r_ready = sem("r_ready")
        route_step = sem("route_step")
        route_pow = sem("route_pow")
        comb_ready = sem("comb_ready")
        combT_made = sem("combT_made")
        combT_ready = sem("combT_ready")
        b2_ready = sem("b2_ready")
        b2_added = sem("b2_added")
        out_ready = sem("out_ready")
        stored = sem("stored")

        block = ctx.enter_context(nc.Block())

        class Chain:
            def __init__(self, eng, s, n, each):
                self.eng, self.s, self.base, self.each, self.k = eng, s, n * each, each, 0

            def link(self, ins, wait=True):
                ins.then_inc(self.s, 1)
                self.k += 1
                assert self.k <= self.each
                if wait:
                    self.eng.wait_ge(self.s, self.base + self.k)

            def end(self):
                assert self.k == self.each, (self.k, self.each)

        def tiles(buf, J):
            if isinstance(J, int):
                return buf[:, J * TT:(J + 1) * TT, :]
            return buf[:, bass.ds(J * TT, TT), :]

        def tile1(buf, J, t):
            if isinstance(J, int):
                return buf[:, J * TT + t, :]
            return buf[:, bass.ds(J * TT + t, 1), :].rearrange("p a d -> p (a d)")

        A_CHUNKS = [[(0, 0, 3)], [(0, 0, 2), (0, 384, 0)], [(1, 0, 3)], [(1, 0, 2), (1, 384, 0)],
                    [(0, 0, 1), (1, 256, 1)]]
        B_CHUNKS = [[(0, 0, 0)], [(0, 0, 1), (0, 384, 3)], [(1, 0, 0)], [(1, 0, 1), (1, 384, 3)],
                    [(0, 0, 2), (1, 256, 2)]]
        KT_COL = [0, 512, 1024, 896]

        def iteration(b, i, jobs, job_a, job_b, extras):
            for pos in range(CHUNKS):
                ja, ca = divmod((i + 1) * CHUNKS + pos + SKEW, CHUNKS)
                for what, rel, at in extras:
                    if at == (pos, 0) and 0 <= i + rel < jobs:
                        what(b, i + rel)
                if 0 <= ja < jobs and job_a:
                    job_a(b, ja, ca)
                if 0 <= i < jobs and job_b:
                    job_b(b, i, pos)
                for what, rel, at in extras:
                    if at == (pos, 1) and 0 <= i + rel < jobs:
                        what(b, i + rel)

        def iterations(eng, base, jobs, job_a, job_b, extras):
            first, last = 2, jobs - 6
            if jobs > JOBS:
                for i in range(-2, first):
                    iteration(base, i, jobs, job_a, job_b, extras)
                with eng.Fori(0, last - first, 4) as at:
                    _plain(eng)
                    for i in range(first + 4, first + 8):
                        iteration(at - 4, i, jobs, job_a, job_b, extras)
                for i in range(last, jobs + 1):
                    iteration(base, i, jobs, job_a, job_b, extras)
            else:
                for i in range(-2, jobs + 1):
                    iteration(base, i, jobs, job_a, job_b, extras)

        ROPE_EACH = 4

        ENC = LAYERS * JOBS

        def ln_init(j):
            return [0, 2, 4, 5, 7, 8, 10, 11][j]

        def ln_index(b, j):
            if isinstance(b, int):
                if b == ENC:
                    return LN_B + j
                if j < 4:
                    return [1, 3, 6, 9][j]
            return b + j + JOBS

        LN_B = JOBS + ENC + 2 * JOBS
        XT_B = ENC + JOBS

        def ln_final(M):
            return JOBS + ENC + 2 * M

        def ln_exp(round_, M):
            return JOBS + ENC + 2 * M + 1 if round_ == 0 else LN_B + M

        def xt_exp(round_, M):
            return ENC + M if round_ == 0 else XT_B + M

        @block.tensor
        def _(pe):
            mm = nc.tensor.matmul

            def transposes(rows_ready, n, made):
                pe.wait_ge(rows_ready, n + 1)
                for t in range(TT):
                    last = nc.tensor.transpose(bankF[:, t * P:(t + 1) * P], xn[:, t, :], ident[:])
                last.then_inc(made, 1)

            def attention(base, jobs, rope_job):
                def xt(b, j):
                    if j >= 2:
                        pe.wait_ge(mT_ready, b + j - 1)
                    elif j == 1:
                        pe.wait_ge(v_ready, b + 1)
                    transposes(xn_ready, ln_index(b, j), xt_ready)

                def project(b, j, k):
                    if k == 0:
                        pe.wait_ge(xnT_ready, b + j + 1)
                        if j % 4 == 0:
                            pe.wait_ge(apack_loaded, 4 * (b + j) + 16)
                    else:
                        pe.wait_ge(qk_ready, 2 * (b + j) + 1)
                    mm(bankF[:], ap_sb[:, k * D:(k + 1) * D], xnT[:], start=True, stop=True).then_inc(proj_ready, 1)

                def project_rope(b, j, k):
                    if k == 0:
                        pe.wait_ge(xnT_ready, XT_B + j + 1)
                    else:
                        pe.wait_ge(rproj_used, ROPE_EACH * j + k)
                    mm(bankF[:], bp_sb[:, k * D:(k + 1) * D], xnT[:], start=True, stop=True).then_inc(rproj_ready, 1)

                def project_v(b, j):
                    if rope_job:
                        pe.wait_ge(rproj_used, ROPE_EACH * (j + 1))
                        wv = bp_sb[:, 4 * D:5 * D]
                    else:
                        pe.wait_ge(qk_ready, 2 * (b + j) + 2)
                        wv = ap_sb[:, 2 * D:3 * D]
                    for t in range(TT):
                        last = mm(bankF[:, t * D:(t + 1) * D], xnT[:, t * P:(t + 1) * P], wv, start=True, stop=True)
                    last.then_inc(proj_ready, 1)

                def pass_a(b, j, c):
                    pair, k = divmod(c, CPP)
                    if c % CPQ == 0:
                        pe.wait_ge(stack_loaded[pair // 2], LOADS * 16 * (b + j + 1))
                    if c == 0:
                        if j > 0:
                            pe.wait_ge(a_used, CHUNKS * (b + j))
                    elif j > 0 or c >= 3:
                        pe.wait_ge(a_used, CHUNKS * (b + j) + c - 2)
                    Q, K, bk = QS[j % 2], KS[j % 2], bankA[c % 3]
                    for n, (h, col, t) in enumerate(A_CHUNKS[k]):
                        hh, w = 2 * pair + h, (t + 1) * P
                        mm(bk[:, col:col + w], Q[0:ROW_MAX, hh, t * P:(t + 1) * P], K[0:ROW_MAX, hh, 0:w],
                           start=True, stop=False)
                        last = mm(bk[:, col + w - P:col + w], ident_b[:], mask_a[:], start=False, stop=True)
                    last.then_inc(a_ready, 1)

                def pass_b(b, j, c):
                    pair, k = divmod(c, CPP)
                    if c == 0:
                        pe.wait_ge(m_loaded, 48 * (b + j + 1))
                    if j > 0 or c >= 2:
                        pe.wait_ge(exp_done, CHUNKS * (b + j) + c - 1)
                    Q, K, bk = QS[j % 2], KS[j % 2], bankB[c % 2]
                    for n, (h, col, t) in enumerate(B_CHUNKS[k]):
                        hh, w = 2 * pair + h, T - t * P
                        mm(bk[:, col:col + w], K[0:ROWS, hh, t * P:(t + 1) * P], Q[0:ROWS, hh, t * P:T],
                           start=True, stop=False)
                        last = mm(bk[:, col:col + P], ident_b[:], mask_b[:], start=False, stop=True)
                    last.then_inc(b_ready, 1)

                def pv(b, j, g, tiles_of_keys):
                    if tiles_of_keys[0] == 0:
                        pe.wait_ge(exp_done, CHUNKS * (b + j) + CPQ * (g + 1))
                        if g == 0:
                            pe.wait_ge(v_ready, b + j + 1)
                        if j > 0 or g > 0:
                            pe.wait_ge(ot_done, QUADS * (b + j) + g)
                    for kt in tiles_of_keys:
                        for h in range(4):
                            last = mm(bankPV[32 * h:32 * h + HD + 1, kt * P:T], V[j % 4][:, kt, 4 * g + h, :],
                                      Pq[g % 2][:, h, KT_COL[kt]:KT_COL[kt] + T - kt * P],
                                      start=(kt == 0), stop=(kt == TT - 1))
                    if kt == TT - 1:
                        last.then_inc(pv_done, 1)

                def ot_transposes(b, j, t):
                    if t == 0:
                        pe.wait_ge(ot_done, QUADS * (b + j + 1))
                        if j > 0:
                            pe.wait_ge(x_added if rope_job else f_added, 2 * (b + j) - 1)
                    else:
                        pe.wait_ge(norm_done, TT * (b + j) + t)
                    for g in range(QUADS):
                        last = nc.tensor.transpose(bankR[:, g * P:(g + 1) * P], OT[:, g, t * P:(t + 1) * P], ident[:])
                    last.then_inc(otT_ready, 1)

                def attn_transposes(b, j):
                    pe.wait_ge(norm_done, TT * (b + j + 1))
                    for t in range(TT):
                        last = nc.tensor.transpose(bankR[:, t * P:(t + 1) * P], attn[:, t, :], ident[:])
                    last.then_inc(attnT_made, 1)

                def out_project(b, j):
                    pe.wait_ge(attnT_ready, b + j + 1)
                    if not rope_job and j % 4 == 0:
                        pe.wait_ge(fpack_loaded, 4 * (b + j) + 16)
                    wo = bp_sb[:, 5 * D:6 * D] if rope_job else fp_sb[:, FP_WO:FP_WO + D]
                    for t in range(TT):
                        last = mm(bankR[:, t * D:(t + 1) * D], attnT[:, t * P:(t + 1) * P], wo, start=True, stop=True)
                    last.then_inc(o_ready, 1)

                def max_transposes(b, j):
                    pe.wait_ge(mparts_ready, b + j + 1)
                    if j >= 2 and not rope_job:
                        pe.wait_ge(gelu_done, FT * (b + j - 1))
                    else:
                        pe.wait_ge(v_ready, b + min(j + 1, jobs - 1) + 1)
                    for t in range(TT):
                        last = nc.tensor.transpose(mT_ps[:, t * P:(t + 1) * P],
                                                   mparts[:, t, :], ident_b[:])
                    last.then_inc(mT_made, 1)

                def ffn_xt(b, j):
                    transposes(fxn_ready, b + j, fxt_ready)

                def ffn_up(b, j, ft):
                    if ft == 0:
                        pe.wait_ge(fxnT_ready, b + j + 1)
                    if ft == 2 and j + 1 < jobs:
                        pe.wait_ge(ot_done, QUADS * (b + j + 1) + 2)
                    if ft == 3:
                        pe.wait_ge(gelu_done, FT * (b + j) + 1)
                    mm(bankG[ft][:], fp_sb[:, FP_W1 + ft * P:FP_W1 + (ft + 1) * P], xnT[:],
                       start=True, stop=True).then_inc(h_ready, 1)

                def ffn_down(b, j, t):
                    if t == 0:
                        pe.wait_ge(gelu_done, FT * (b + j + 1))
                    for ft in range(FT):
                        last = mm(bankR[:, t * D:(t + 1) * D], fhT[:, ft, t * P:(t + 1) * P],
                                  fp_sb[:, FP_W2 + ft * D:FP_W2 + (ft + 1) * D],
                                  start=(ft == 0), stop=(ft == FT - 1))
                    if t == TT - 1:
                        last.then_inc(y_ready, 1)

                extras = [(xt, 2, (0, 1))]
                if rope_job:
                    extras += [(lambda b, j, k=k: project_rope(b, j, k), 2, (3 + 2 * k, 1)) for k in range(4)]
                    extras += [(project_v, 2, (12, 1))]
                else:
                    extras += [(lambda b, j, k=k: project(b, j, k), 2, (4 + 3 * k, 1)) for k in range(2)]
                    extras += [(project_v, 2, (10, 1))]
                for g, rel, at in ((3, -1, (1, 2, 3)), (0, 0, (14, 18, 19)), (1, 0, (22, 23, 25)), (2, 0, (32, 33, 34))):
                    for n, kts in enumerate(((0,), (1,), (2, 3))):
                        extras += [(lambda b, j, g=g, kts=kts: pv(b, j, g, kts), rel, (at[n], 1))]
                extras += [(lambda b, j, t=t: ot_transposes(b, j, t), -1, (7 + 2 * t, 1)) for t in range(TT)]
                extras += [(attn_transposes, -1, (15, 1)), (out_project, -1, (17, 1)), (max_transposes, 1, (31 if rope_job else 34, 1))]
                if not rope_job:
                    extras += [(ffn_xt, -1, (24, 1))]
                    extras += [(lambda b, j, ft=ft: ffn_up(b, j, ft), -1, ((26, 27, 27, 29)[ft], 1)) for ft in range(FT)]
                    extras += [(lambda b, j, t=t: ffn_down(b, j, t), -1, (35 + t, 1)) for t in range(TT)]
                iterations(pe, base, jobs, pass_a, pass_b, extras)

            def experts(round_):
                def xt(M):
                    pe.wait_ge(xnT_ready, xt_exp(round_, M))
                    transposes(xn_ready, ln_exp(round_, M), xt_ready)

                def up(M, xT, e):
                    EI = M * E + e
                    pe.wait_ge(egelu_done, FT * EI)
                    for ft in range(FT):
                        mm(bankH[ft][:], W1[:, e, ft * P:(ft + 1) * P], xT[:],
                           start=True, stop=True).then_inc(eh_ready, 1)

                def down(M, e, first):
                    EI = M * E + e
                    pe.wait_ge(egelu_done, FT * (EI + 1))
                    if not (first and e < 2):
                        pe.wait_ge(ey_used, EI - 1)
                    for t in range(TT):
                        for ft in range(FT):
                            last = mm(bankY[e % 2][:, t * D:(t + 1) * D], hT[e % 2][:, ft, t * P:(t + 1) * P],
                                      W2[:, e, ft, :], start=(ft == 0), stop=(ft == FT - 1))
                    last.then_inc(ey_ready, 1)

                def route(M, xT):
                    pe.wait_ge(b2_added, M)
                    mm(bankR[:], mp_sb[:, MP_WP:MP_WP + D], xT[:], start=True, stop=True).then_inc(xp_ready, 1)

                def route2(M):
                    pe.wait_ge(xpT_ready, 2 * (M + 1))
                    for t in range(TT):
                        mm(bankR[:, t * 16:t * 16 + E], xpT[:, t * P:(t + 1) * P], cproj[:], start=True, stop=True)
                        last = mm(bankR[:, t * 16 + E:t * 16 + E + 1], sqT[:, t * P:(t + 1) * P], ones[:, 0:1],
                                  start=True, stop=True)
                    last.then_inc(r_ready, 1)

                def bias1(M, p):
                    pe.wait_ge(comb_ready, M + 1)
                    for t in range(TT):
                        last = nc.tensor.transpose(bankR[0:E, t * P:(t + 1) * P], comb[p][:, t, :], ident[:])
                    last.then_inc(combT_made, 1)

                def bias2(M):
                    pe.wait_ge(combT_ready, M + 1)
                    for t in range(TT):
                        last = mm(bankR[:, t * D:(t + 1) * D], combT[:, t * P:(t + 1) * P], b2_sb[:],
                                  start=True, stop=True)
                    last.then_inc(b2_ready, 1)

                pe.wait_ge(mw_loaded[0], 16 * (round_ + 1))
                pe.wait_ge(mw_loaded[1], 16 * (round_ + 1))
                M0 = round_ * JOBS
                xt(M0)

                def job(M, p, first, last):
                    xT = [xnT, xnT2][p]
                    pe.wait_ge(xnT_ready, xt_exp(round_, M) + 1)
                    route(M, xT)
                    up(M, xT, 0)
                    route2(M)
                    up(M, xT, 1)
                    down(M, 0, first)
                    up(M, xT, 2)
                    down(M, 1, first)
                    bias1(M, p)
                    up(M, xT, 3)
                    bias2(M)
                    down(M, 2, first)
                    for e in range(4, E):
                        up(M, xT, e)
                        down(M, e - 1, first)
                        if e == 5 and not last:
                            xt(M + 1)
                    down(M, E - 1, first)

                job(M0, 0, round_ == 0, False)
                job(M0 + 1, 1, False, False)
                with pe.Fori(0, 2) as it:
                    _plain(pe)
                    job(M0 + 2 + it * 2, 0, False, False)
                    job(M0 + 3 + it * 2, 1, False, False)
                job(M0 + 6, 0, False, False)
                job(M0 + 7, 1, False, True)

            pe.wait_ge(const_done, N_CONST)
            pe.wait_ge(pv_clear, 1)
            pe.wait_ge(load_const, 16 * 4)
            pe.wait_ge(c_step, 1)
            mm(bankR[:, 0:E], ones[:], cn[:, 0, :], start=True, stop=True).then_inc(c_made, 1)
            attention(0, ENC, False)
            pe.wait_ge(cproj_ready, 1)
            pe.wait_ge(f_added, 2 * ENC - 1)
            experts(0)
            attention(ENC, JOBS, True)
            pe.wait_ge(x_added, 2 * (ENC + JOBS) - 1)
            experts(1)

        @block.scalar
        def _(act):
            A = nc.scalar.activation

            def evac_x(X, dst):
                act.wait_ge(xt_ready, X + 1)
                A(dst[:], bankF[:], ACT.Copy).then_inc(xnT_ready, 1)

            def attention(base, jobs, rope_job):
                def xnt(b, j):
                    act.wait_ge(xt_ready, (XT_B + j if rope_job else b + j) + 1)
                    if not rope_job and j % 4 == 0:
                        act.wait_ge(apack_loaded, 4 * (b + j) + 16)
                    if rope_job:
                        A(xnT[:], bankF[:], ACT.Copy).then_inc(xnT_ready, 1)
                    else:
                        A(xnT[:], bankF[:], ACT.Identity, bias=ap_sb[:, AP_COL + 1:AP_COL + 2],
                          scale=ap_sb[:, AP_COL:AP_COL + 1]).then_inc(xnT_ready, 1)

                def evac_qk(b, j, k):
                    if k == 0 and j % 4 == 0:
                        A(bqs[:], ap_sb[:, AP_COL + 2:AP_COL + 3], ACT.Copy, scale=1.0 / math.sqrt(HD)).then_inc(bqs_ready, 4)
                        act.wait_ge(bqs_ready, b + j + 4)
                    act.wait_ge(proj_ready, 3 * (b + j) + k + 1)
                    if k == 0 and j >= 1:
                        act.wait_ge(p3_ready, 2 * (b + j))
                    if k == 0:
                        A(qk[:, 0, :], bankF[:], ACT.Identity, bias=bqs[:], scale=1.0 / math.sqrt(HD)).then_inc(qk_ready, 1)
                    else:
                        A(qk[:, 1, :], bankF[:], ACT.Identity,
                          bias=ap_sb[:, AP_COL + 3:AP_COL + 4]).then_inc(qk_ready, 1)

                def exps(b, j, c):
                    pair, k = divmod(c, CPP)
                    g = pair // 2
                    if c % CPQ == 0 and (j > 0 or g >= 2):
                        act.wait_ge(pv_done, QUADS * (b + j) + g - 1)
                    act.wait_ge(b_ready, CHUNKS * (b + j) + c + 1)
                    bk = bankB[c % 2]
                    h0 = 2 * (pair % 2)
                    if k < 4:
                        dst = Pq[g % 2][:, h0 + k // 2, (k % 2) * T:(k % 2) * T + T]
                        src = bk[:]
                    else:
                        dst = Pq[g % 2][:, h0:h0 + 2, 2 * T:HCOLS]
                        src = bk[:].rearrange("p (h c) -> p h c", h=2)
                    A(dst, src, ACT.Exp).then_inc(exp_done, 1)

                def evac_ot(b, j, g):
                    act.wait_ge(pv_done, QUADS * (b + j) + g + 1)
                    if g == 0 and j > 0:
                        act.wait_ge(otT_ready, TT * (b + j))
                    A(OT[:, g, :], bankPV[:], ACT.Copy).then_inc(ot_done, 1)

                def evac_attn(b, j):
                    act.wait_ge(attnT_made, b + j + 1)
                    A(attnT[:], bankR[:], ACT.Copy).then_inc(attnT_ready, 1)

                extras = [(xnt, 2, (1, 1))]
                if not rope_job:
                    extras += [(lambda b, j, k=k: evac_qk(b, j, k), 2, (5 + 3 * k, 0)) for k in range(2)]
                extras += [(lambda b, j: evac_ot(b, j, 3), -1, (4, 1))]
                extras += [(lambda b, j, g=g, at=at: evac_ot(b, j, g), 0, (at, 1)) for g, at in enumerate((20, 26, 35))]
                extras += [(evac_attn, -1, (16, 1))]

                def ffn_x(b, j):
                    act.wait_ge(fxt_ready, b + j + 1)
                    A(xnT[:], bankF[:], ACT.Identity, bias=fp_sb[:, FP_COL + 1:FP_COL + 2],
                      scale=fp_sb[:, FP_COL:FP_COL + 1]).then_inc(fxnT_ready, 1)

                def ffn_gelu(b, j):
                    if j >= 1:
                        act.wait_ge(y_ready, b + j)
                    for ft in range(FT):
                        act.wait_ge(h_ready, FT * (b + j) + ft + 1)
                        A(fhT[:, ft, :], bankG[ft][:], ACT.Gelu,
                          bias=fp_sb[:, FP_COL + 2 + ft:FP_COL + 3 + ft]).then_inc(gelu_done, 1)

                if not rope_job:
                    extras += [(ffn_x, -1, (25, 1)), (ffn_gelu, -1, (27, 1))]
                iterations(act, base, jobs, None, exps, extras)

            act.wait_ge(const_done, N_CONST)
            act.wait_ge(load_const, 16 * 4)
            attention(0, ENC, False)

            def experts(round_):
                def job(M, p, first, last):
                    act.wait_ge(xp_ready, M + 1)
                    A(xpT, bankR[:], ACT.Identity, bias=mp_sb[:, MP_BP:MP_BP + 1]).then_inc(xpT_ready, 1)
                    A(sqT, bankR[:], ACT.Square, bias=mp_sb[:, MP_BP:MP_BP + 1]).then_inc(xpT_ready, 1)
                    for e in range(E):
                        EI = M * E + e
                        if not (first and e < 2):
                            act.wait_ge(ey_ready, EI - 1)
                        for ft in range(FT):
                            act.wait_ge(eh_ready, FT * EI + ft + 1)
                            A(hT[e % 2][:, ft, :], bankH[ft][:], ACT.Gelu,
                              bias=mp_sb[:, MP_B1 + e * FT + ft:MP_B1 + e * FT + ft + 1]).then_inc(egelu_done, 1)
                        if e == 2:
                            act.wait_ge(combT_made, M + 1)
                            A(combT[:], bankR[0:E, :], ACT.Copy).then_inc(combT_ready, 1)
                        if e == 5 and not last:
                            evac_x(xt_exp(round_, M) + 1, [xnT2, xnT][p])

                M0 = round_ * JOBS
                evac_x(xt_exp(round_, M0), xnT)
                job(M0, 0, round_ == 0, False)
                job(M0 + 1, 1, False, False)
                with act.Fori(0, 2) as it:
                    _plain(act)
                    job(M0 + 2 + it * 2, 0, False, False)
                    job(M0 + 3 + it * 2, 1, False, False)
                job(M0 + 6, 0, False, False)
                job(M0 + 7, 1, False, True)

            experts(0)
            attention(ENC, JOBS, True)
            experts(1)

        @block.vector
        def _(dve):
            v = nc.vector

            def ln_stats(n, J, steps=ln_step):
                ch = Chain(dve, steps, n, 3)
                for t in range(TT):
                    last = v.bn_stats(stats[:, t, :], tile1(xs, J, t))
                ch.link(last)
                v.tensor_copy(spare[:, 0:1], half[:, 0:1])
                for t in range(TT):
                    last = v.bn_aggr(mv[:, t, :], stats[:, t, :])
                ch.link(last)
                ch.link(v.tensor_scalar(veps[:], mv[:, :, 1], EPS, None, ALU.add), wait=False)
                ch.end()

            def ln_apply(n, J, power=rstd_ready, done=xn_ready, in_place=False):
                dve.wait_ge(power, n + 1)
                for t in range(TT):
                    row = tile1(xs, J, t)
                    last = v.tensor_scalar(row if in_place else xn[:, t, :], row, mv[:, t, 0:1], rstd[:, t:t + 1],
                                           ALU.subtract, ALU.mult)
                last.then_inc(done, 1)

            def expert_ln(round_, M, J, p):
                rows = tiles(xs, J)

                def final_stats():
                    ln_stats(ln_final(M), J)

                def final_apply():
                    ln_apply(ln_final(M), J, in_place=True)
                    dve.wait_ge(xn_ready, ln_final(M) + 1)
                    ch = Chain(dve, fin_step, M, 3)
                    fw = fin_sb[:, 0:D].unsqueeze(1).broadcast_to([P, TT, D])
                    fb = fin_sb[:, D:2 * D].unsqueeze(1).broadcast_to([P, TT, D])
                    ch.link(v.tensor_tensor(rows, rows, fw, ALU.mult))
                    ch.link(v.tensor_tensor(rows, rows, fb, ALU.add))
                    dve.wait_ge(xr_loaded[p], 8 * M + 16 - 8 * p)
                    ch.link(v.tensor_tensor(rows, rows, xload[:, p, :, :], ALU.add))
                    ch.end()

                def expert_stats():
                    ln_stats(ln_exp(round_, M), J)

                def expert_apply():
                    dve.wait_ge(xt_ready, xt_exp(round_, M))
                    if isinstance(M, int) and M == 0:
                        dve.wait_ge(fxt_ready, ENC)
                    ln_apply(ln_exp(round_, M), J)
                return ([final_stats, final_apply] if round_ == 0 else []) + [expert_stats, expert_apply]

            def rope_ln():
                def apply():
                    dve.wait_ge(xt_ready, XT_B)
                    ln_apply(ln_index(ENC, 0), 0)
                return [lambda: ln_stats(ln_index(ENC, 0), 0), apply]

            def first_layernorms():
                dve.wait_ge(x_loaded[0], 16)
                ln_stats(ln_init(0), 0)
                ln_apply(ln_init(0), 0, in_place=True)
                dve.wait_ge(xn_ready, ln_init(0) + 1)
                ln_stats(ln_index(0, 0), 0)
                ln_apply(ln_index(0, 0), 0)

            def attention(base, jobs, rope_job):
                def stream(b, j):
                    if isinstance(b, int):
                        return j % JOBS
                    return (b + j) & (JOBS - 1)

                def lns(b, j):
                    ln_stats(ln_index(b, j), stream(b, j))

                def lna(b, j):
                    if j >= 1:
                        dve.wait_ge(xt_ready, (XT_B if rope_job else b) + j)
                    if j >= 4 and not rope_job:
                        dve.wait_ge(fxt_ready, b + j - 3)
                    ln_apply(ln_index(b, j), stream(b, j))

                def first_ln(b, j, n):
                    k = 2 * j + n
                    if isinstance(b, int) and 0 < k < JOBS:
                        dve.wait_ge(x_loaded[1], 16)
                        ln_stats(ln_init(k), k)
                        ln_apply(ln_init(k), k, in_place=True)
                        dve.wait_ge(xn_ready, ln_init(k) + 1)

                def split1(b, j, k):
                    dve.wait_ge(qk_ready, 2 * (b + j) + k + 1)
                    if j >= 1:
                        dve.wait_ge(parts_stored, 32 * (b + j))
                    v.tensor_copy(parts[:, k, 0, :], qk[:, k, :]).then_inc(p1_ready, 1)

                def split2(b, j, k):
                    dve.wait_ge(r1_ready, 2 * (b + j) + k + 1)
                    v.tensor_copy(parts[:, k, 1, :], resid[:, k, :]).then_inc(p2_ready, 1)

                def rotate(b, j, n):
                    k = n // 2
                    if j == 0 and n == 0:
                        dve.wait_ge(rope_loaded, 16)
                    dve.wait_ge(rproj_ready, ROPE_EACH * j + n + 1)
                    if n % 2 == 0:
                        if k == 0 and j >= 1:
                            dve.wait_ge(p3_ready, 2 * (b + j))
                        v.tensor_tensor(qk[:, k, :], bankF[:], rope_sb[:, 2 * k, :], ALU.mult).then_inc(rproj_used, 1)
                    else:
                        v.tensor_tensor(rtmp[:, k, :], bankF[:], rope_sb[:, 2 * k + 1, :],
                                        ALU.mult).then_inc(rproj_used, 1)
                        dve.wait_ge(rproj_used, ROPE_EACH * j + n + 1)
                        v.tensor_tensor(qk[:, k, :], qk[:, k, :], rtmp[:, k, :], ALU.add).then_inc(qk_ready, 1)
                        split1(b, j, k)

                def take_v(b, j):
                    dve.wait_ge(proj_ready, (3 * ENC + j + 1) if rope_job else 3 * (b + j) + 3)
                    dst = V[j % 4][:, :, :, 0:HD]
                    src = bankF[:].rearrange("p (t h d) -> p t h d", t=TT, h=H)
                    if j >= 4:
                        dve.wait_ge(pv_done, QUADS * (b + j - 3))
                    if rope_job:
                        v.tensor_copy(dst, src).then_inc(v_ready, 1)
                    else:
                        bias = ap_sb[:, AP_BV:AP_BV + D].rearrange("p (h d) -> p h d", h=H)
                        v.tensor_tensor(dst, src, bias.unsqueeze(1).broadcast_to([P, TT, H, HD]),
                                        ALU.add).then_inc(v_ready, 1)

                def maxima(b, j, c):
                    pair, k = divmod(c, CPP)
                    dve.wait_ge(a_ready, CHUNKS * (b + j) + c + 1)
                    bk = bankA[c % 3]
                    if k < 4:
                        h = 2 * pair + k // 2
                        dst = mx[:, h, 4 * (k % 2):4 * (k % 2) + 4]
                        src = bk[:].rearrange("p (n c) -> p n c", n=4)
                    else:
                        dst = mx[:, 2 * pair:2 * pair + 2, 8:10]
                        src = bk[:].rearrange("p (h n c) -> p h n c", h=2, n=2)
                    v.tensor_reduce(dst, src, axis=AX.X, op=ALU.max).then_inc(a_used, 1)

                def negate_split(b, j):
                    ch = Chain(dve, max_step, b + j, 4)
                    dve.wait_ge(a_used, CHUNKS * (b + j + 1))
                    for t, (lo, n) in enumerate([(7, 1), (8, 2), (4, 3), (0, 4)]):
                        last = v.tensor_reduce(mneg[:, t, :], mx[:, :, lo:lo + n], axis=AX.X, op=ALU.max, negate=True)
                    ch.link(last)
                    if j >= 1:
                        dve.wait_ge(mT_made, b + j)
                    ch.link(v.tensor_copy(mparts[:, :, 0 * H:1 * H], mneg[:]))
                    ch.link(v.tensor_tensor(mres[:], mneg[:], mparts[:, :, 0 * H:1 * H], ALU.subtract))
                    ch.link(v.tensor_copy(mparts[:, :, 1 * H:2 * H], mres[:]))
                    ch.end()
                    v.tensor_tensor(mparts[:, :, 2 * H:3 * H], mres[:], mparts[:, :, 1 * H:2 * H],
                                    ALU.subtract).then_inc(mparts_ready, 1)

                def evac_max(b, j):
                    dve.wait_ge(mT_made, b + j + 1)
                    if j >= 1:
                        dve.wait_ge(m_loaded, 48 * (b + j))
                    v.tensor_copy(mT[:], mT_ps[0:NPART * H, :]).then_inc(mT_ready, 1)

                def normalise(b, j, t):
                    dve.wait_ge(otT_ready, TT * (b + j) + t + 1)
                    heads = bankR[:].rearrange("p (h c) -> p h c", h=H)
                    ch = Chain(dve, norm_step, TT * (b + j) + t, 1)
                    ch.link(v.reciprocal(rl[:], heads[:, :, HD]))
                    ch.end()
                    if t == 0 and j > 0:
                        dve.wait_ge(attnT_made, b + j)
                    v.tensor_tensor(attn[:, t, :].rearrange("p (h d) -> p h d", h=H), heads[:, :, 0:HD],
                                    rl[:].unsqueeze(2).broadcast_to([P, H, HD]), ALU.mult).then_inc(norm_done, 1)

                def add_x(b, j):
                    dve.wait_ge(o_ready, b + j + 1)
                    rows = tiles(xs, stream(b, j))
                    o = bankR[:].rearrange("p (t d) -> p t d", t=TT)
                    v.tensor_tensor(rows, rows, o, ALU.add).then_inc(x_added, 1)
                    dve.wait_ge(x_added, 2 * (b + j) + 1)
                    if rope_job:
                        v.tensor_copy(spare[:, 0:1], half[:, 0:1]).then_inc(x_added, 1)
                    else:
                        bo = fp_sb[:, FP_BO:FP_BO + D].unsqueeze(1).broadcast_to([P, TT, D])
                        v.tensor_tensor(rows, rows, bo, ALU.add).then_inc(x_added, 1)

                def ffn_lns(b, j):
                    dve.wait_ge(x_added, 2 * (b + j + 1))
                    ln_stats(b + j, stream(b, j), fln_step)

                def ffn_lna(b, j):
                    ln_apply(b + j, stream(b, j), frstd_ready, fxn_ready)

                def ffn_add(b, j):
                    dve.wait_ge(y_ready, b + j + 1)
                    rows = tiles(xs, stream(b, j))
                    y = bankR[:].rearrange("p (t d) -> p t d", t=TT)
                    v.tensor_tensor(rows, rows, y, ALU.add).then_inc(f_added, 1)
                    dve.wait_ge(f_added, 2 * (b + j) + 1)
                    b2 = fp_sb[:, FP_B2:FP_B2 + D].unsqueeze(1).broadcast_to([P, TT, D])
                    v.tensor_tensor(rows, rows, b2, ALU.add).then_inc(f_added, 1)

                extras = []
                if rope_job:
                    extras += [(lambda b, j, n=n: rotate(b, j, n), 2, (4 + 2 * n, 1)) for n in range(4)]
                    extras += [(lambda b, j: split2(b, j, 0), 2, (11, 1)), (take_v, 2, (13, 1)),
                               (lambda b, j: split2(b, j, 1), 2, (15, 1))]
                else:
                    extras += [(lambda b, j: split1(b, j, 0), 2, (6, 1)), (lambda b, j: split1(b, j, 1), 2, (9, 1)),
                               (lambda b, j: split2(b, j, 0), 2, (9, 1)), (take_v, 2, (11, 1)),
                               (lambda b, j: split2(b, j, 1), 2, (12, 1))]
                extras += [(lambda b, j, t=t: normalise(b, j, t), -1, (8 + 2 * t, 0)) for t in range(TT)]
                extras += [(add_x, -1, (18, 1)), (negate_split, 1, (29, 1)), (evac_max, 1, (31 if rope_job else 34, 1)),
                           (lns, 3, (33, 1)), (lna, 3, (36, 1))]
                if not rope_job:
                    extras += [(ffn_lns, -1, (19, 1)), (ffn_lna, -1, (21, 1)), (ffn_add, -1, (39, 1))]
                    extras += [(lambda b, j, n=n: first_ln(b, j, n), 2, (17 + 8 * n, 1)) for n in range(2)]
                round_ = 1 if rope_job else 0
                steps = expert_ln(round_, round_ * JOBS, 0, 0)
                for n, at in enumerate((25, 27) if rope_job else (2, 5, 25, 27)):
                    extras += [(lambda b, j, n=n: steps[n]() if j == jobs - 1 else None, -1, (at, 1))]
                iterations(dve, base, jobs, maxima, None, extras)

            def experts(round_):
                ROUTE = 22
                cnb = cn[:, 2, :]

                def route(M, p):
                    ch = Chain(dve, route_step, M, ROUTE)
                    n2, nrm, sc, xn2, omx, mn, ws = (s4[:, i, :] for i in range(7))
                    dot, t1, a, ap1, s, root, tt_, w, den, sel = (s8[:, i, :, :] for i in range(10))
                    lt, eq, rk = (s88[:, i, :, :] for i in range(3))

                    def b8(x):
                        return x.unsqueeze(2).broadcast_to([P, TT, E])

                    def row8(x):
                        return x.unsqueeze(1).broadcast_to([P, TT, E])

                    dve.wait_ge(r_ready, M + 1)
                    ch.link(v.tensor_copy(R[:], bankR[:, 0:64].rearrange("p (t c) -> p t c", t=TT)[:, :, 0:E + 1]))
                    ch.link(v.tensor_copy(n2, R[:, :, E]), wait=False)
                    dve.wait_ge(route_pow, 2 * M + 1)
                    ch.link(v.tensor_scalar(nrm, nrm, 1e-7, None, ALU.max))
                    ch.link(v.reciprocal(sc, nrm))
                    ch.link(v.tensor_scalar(sc, sc, 0.95, 1.0, ALU.mult, ALU.min))
                    ch.link(v.tensor_tensor(xn2, n2, sc, ALU.mult))
                    ch.link(v.tensor_tensor(xn2, xn2, sc, ALU.mult))
                    ch.link(v.tensor_scalar(xn2, xn2, 0.99, None, ALU.min))
                    ch.link(v.tensor_tensor(dot, R[:, :, 0:E], b8(sc), ALU.mult))
                    ch.link(v.tensor_scalar(t1, dot, -2.0, None, ALU.mult))
                    ch.link(v.tensor_tensor(t1, t1, row8(cnb), ALU.add))
                    ch.link(v.tensor_tensor(t1, t1, b8(xn2), ALU.add))
                    v.tensor_scalar(omx, xn2, -1.0, 1.0, ALU.mult, ALU.add)
                    ch.link(v.tensor_scalar(t1, t1, 0.0, 2.0, ALU.max, ALU.mult))
                    ch.link(v.tensor_tensor(den, b8(omx), row8(cn[:, 1, :]), ALU.mult))
                    ch.link(v.tensor_scalar(den, den, 1e-7, None, ALU.add))
                    ch.link(v.reciprocal(den, den))
                    ch.link(v.tensor_tensor(a, t1, den, ALU.mult))
                    ch.link(v.tensor_scalar(a, a, 1.0, 1.0 + 1e-7, ALU.add, ALU.max))
                    v.tensor_scalar(ap1, a, 1.0, None, ALU.add)
                    ch.link(v.tensor_scalar(root, a, -1.0, None, ALU.add))
                    ch.link(v.tensor_tensor(s, root, ap1, ALU.mult), wait=False)
                    ae = a.unsqueeze(3).broadcast_to([P, TT, E, E])
                    aj = a.unsqueeze(2).broadcast_to([P, TT, E, E])

                    def e88(x):
                        return x.rearrange("p t (e j) -> p t e j", e=E)

                    v.tensor_tensor(e88(lt), aj, ae, ALU.is_lt)
                    ch.link(v.tensor_tensor(e88(eq), aj, ae, ALU.is_equal))
                    trib = tri[:].rearrange("p e j -> p (e j)").unsqueeze(1).broadcast_to([P, TT, E * E])
                    ch.link(v.tensor_tensor(rk, eq, trib, ALU.mult))
                    ch.end()
                    return lt, eq, rk, sel, a, root, tt_, w, mn, ws

                def route2(M, p, vals):
                    lt, eq, rk, sel, a, root, tt_, w, mn, ws = vals
                    ch = Chain(dve, c_step, M, 11)
                    ch.base = ch.base + 4

                    def b8(x):
                        return x.unsqueeze(2).broadcast_to([P, TT, E])

                    ch.link(v.tensor_tensor(lt, lt, rk, ALU.add))
                    ch.link(v.tensor_reduce(sel, lt.rearrange("p t (e j) -> p t e j", e=E), axis=AX.X, op=ALU.add))
                    ch.link(v.tensor_scalar(sel, sel, 1.5, None, ALU.is_lt))
                    dve.wait_ge(route_pow, 2 * M + 2)
                    ch.link(v.tensor_tensor(tt_, a, root, ALU.add))
                    ch.link(v.tensor_reduce(mn, tt_, axis=AX.X, op=ALU.min))
                    ch.link(v.reciprocal(w, tt_))
                    ch.link(v.tensor_tensor(w, w, b8(mn), ALU.mult))
                    ch.link(v.tensor_tensor(w, w, sel, ALU.mult))
                    ch.link(v.tensor_reduce(ws, w, axis=AX.X, op=ALU.add))
                    ch.link(v.reciprocal(ws, ws))
                    ch.link(v.tensor_tensor(comb[p][:], w, b8(ws), ALU.mult))
                    ch.end()
                    v.tensor_copy(ws, mn).then_inc(comb_ready, 1)

                def job(M, J, p, last):
                    vals = route(M, p)
                    route2(M, p, vals)
                    steps = expert_ln(round_, M + 1, J + 1, 1 - p) if not last else rope_ln() if round_ == 0 else []
                    for e in range(E):
                        EI = M * E + e
                        if e == 1:
                            dve.wait_ge(b2_ready, M + 1)
                            rows = tiles(xs, J)
                            v.tensor_tensor(rows, rows, bankR[:].rearrange("p (t d) -> p t d", t=TT),
                                            ALU.add).then_inc(b2_added, 1)
                            dve.wait_ge(b2_added, M + 1)
                        dve.wait_ge(ey_ready, EI + 1)
                        for t in range(TT):
                            row = tile1(xs, J, t)
                            ins = v.scalar_tensor_tensor(out=row, in0=bankY[e % 2][:, t * D:(t + 1) * D],
                                                         scalar=comb[p][:, t, e:e + 1], in1=row,
                                                         op0=ALU.mult, op1=ALU.add)
                        ins.then_inc(ey_used, 1)
                        dve.wait_ge(ey_used, EI + 1)
                        if e < len(steps):
                            steps[e]()
                    if round_ == 1:
                        v.tensor_copy(spare[:, 0:1], half[:, 0:1]).then_inc(out_ready, 1)

                M0 = round_ * JOBS
                job(M0, 0, 0, False)
                job(M0 + 1, 1, 1, False)
                with dve.Fori(0, 2) as it:
                    _plain(dve)
                    job(M0 + 2 + it * 2, 2 + it * 2, 0, False)
                    job(M0 + 3 + it * 2, 3 + it * 2, 1, False)
                job(M0 + 6, 6, 0, False)
                job(M0 + 7, 7, 1, True)

            v.memset(bankPV[:], 0.0).then_inc(pv_clear, 1)
            dve.wait_ge(const_done, 2)
            first_layernorms()
            dve.wait_ge(const_done, N_CONST)
            dve.wait_ge(load_const, 16 * 4)
            n = [0]

            def step(ins):
                n[0] += 1
                ins.then_inc(cproj_step, 1)
                dve.wait_ge(cproj_step, n[0])
            c = mp_sb[:, MP_C:MP_C + E]
            v.tensor_tensor(cn[:, 0, :], c, c, ALU.mult).then_inc(c_step, 1)
            dve.wait_ge(c_made, 1)
            ch = Chain(dve, c_step, 0, 4)
            ch.k = 1
            ch.link(v.tensor_copy(cn[:, 2, :], bankR[:, 0:E]), wait=False)
            dve.wait_ge(cproj_pow, 1)
            step(v.tensor_scalar(cn[:, 1, :], cn[:, 1, :], 1e-7, None, ALU.max))
            step(v.reciprocal(cn[:, 1, :], cn[:, 1, :]))
            step(v.tensor_scalar(cn[:, 1, :], cn[:, 1, :], 0.95, 1.0, ALU.mult, ALU.min))
            step(v.tensor_tensor(cproj[:], c, cn[:, 1, :], ALU.mult))
            step(v.tensor_tensor(cn[:, 2, :], cn[:, 2, :], cn[:, 1, :], ALU.mult))
            step(v.tensor_tensor(cn[:, 2, :], cn[:, 2, :], cn[:, 1, :], ALU.mult))
            step(v.tensor_scalar(cn[:, 2, :], cn[:, 2, :], 0.99, None, ALU.min))
            ch.link(v.tensor_scalar(cn[:, 1, :], cn[:, 2, :], -1.0, 1.0, ALU.mult, ALU.add))
            ch.link(v.tensor_copy(cn[:, 0, :], cn[:, 2, :]))
            v.tensor_copy(spare[:, 0:1], half[:, 0:1]).then_inc(cproj_ready, 1)
            attention(0, ENC, False)
            dve.wait_ge(f_added, 2 * ENC)
            experts(0)
            attention(ENC, JOBS, True)
            dve.wait_ge(x_added, 2 * (ENC + JOBS))
            experts(1)

        @block.gpsimd
        def _(pool):
            g = nc.gpsimd
            def rsqrt(n, steps=ln_step, done=rstd_ready):
                pool.wait_ge(steps, 3 * n + 3)
                g.tensor_tensor(rstd[:], veps[:], mhalf[:], ALU.pow).then_inc(done, 1)

            g.memset(half[:], 0.5).then_inc(const_done, 1)
            g.memset(mhalf[:], -0.5).then_inc(const_done, 1)
            g.memset(ident[:], 0.0).then_inc(const_zero, 1)
            g.memset(ident_b[:], 0.0).then_inc(const_zero, 1)
            g.memset(mask_a[:], 0.0).then_inc(const_zero, 1)
            g.memset(mask_b[:], 0.0).then_inc(const_zero, 1)
            g.memset(tri[:], 1.0).then_inc(const_zero, 1)
            pool.wait_ge(const_zero, 5)
            for m in (ident, ident_b):
                g.affine_select(out=m[:], in_=m[:], compare_op=ALU.not_equal, fill=1.0, base=0,
                                pattern=[[-1, P]], channel_multiplier=1).then_inc(const_done, 1)
            g.affine_select(out=mask_a[:], in_=mask_a[:], compare_op=ALU.is_ge, fill=NEG, base=0,
                            pattern=[[-1, P]], channel_multiplier=1).then_inc(const_done, 1)
            g.affine_select(out=mask_b[:], in_=mask_b[:], compare_op=ALU.is_ge, fill=NEG, base=0,
                            pattern=[[1, P]], channel_multiplier=-1).then_inc(const_done, 1)
            g.affine_select(out=tri[:], in_=tri[:], compare_op=ALU.is_gt, fill=0.0, base=0,
                            pattern=[[1, E], [-1, E]], channel_multiplier=0).then_inc(const_done, 1)
            g.memset(ones[:], 1.0).then_inc(const_done, 1)
            rsqrt(ln_init(0))
            g.memset(mparts[:], 0.0).then_inc(const_done, 1)
            for i in range(len(V)):
                g.memset(V[i][:], 1.0).then_inc(const_done, 1)
            pool.wait_ge(const_done, N_CONST)

            def init_stack(i):
                q4, k4 = (S[i][:].rearrange("p h t -> p (h t)").bitcast(F32) for S in (QS, KS))
                g.memset(q4[64:ROW_MAX, :], 0.0).then_inc(const_zero, 1)
                g.memset(k4[64:ROW_MAX, :], 0.0).then_inc(const_zero, 1)
                pool.wait_ge(const_zero, 7 + 3 * i)
                g.memset(k4[ROW_MAX:ROWS, :], ONES_PAIR).then_inc(const_zero, 1)
                pool.wait_ge(const_zero, 8 + 3 * i)
                for S, rows in ((QS, alibi[0]), (KS, alibi[1])):
                    g.dma_start(S[i][ROW_ALIBI:ROW_ALIBI + N_ALIBI, :, :], rows).then_inc(alibi_loaded[i], 16)

            def first_ln(b, j, n):
                k = 2 * j + n
                if isinstance(b, int) and 0 < k < JOBS:
                    rsqrt(ln_init(k))

            def attention(base, jobs, rope_job):
                def split(b, j, k):
                    n = 2 * (b + j) + k
                    pool.wait_ge(p1_ready, n + 1)
                    g.tensor_tensor(resid[:, k, :], qk[:, k, :], parts[:, k, 0, :], ALU.subtract).then_inc(r1_ready, 1)

                def split3(b, j, k):
                    n = 2 * (b + j) + k
                    pool.wait_ge(p2_ready, n + 1)
                    g.tensor_tensor(parts[:, k, 2, :], resid[:, k, :], parts[:, k, 1, :],
                                    ALU.subtract).then_inc(p3_ready, 1)

                extras = [(lambda b, j: split(b, j, 0), 2, (5, 1)), (lambda b, j: split(b, j, 1), 2, (8, 1)),
                          (lambda b, j: split3(b, j, 0), 2, (10, 1)), (lambda b, j: split3(b, j, 1), 2, (13, 1)),
                          (lambda b, j: rsqrt(ln_index(b, j)), 3, (34, 1))]
                def second_stack(b, j):
                    if isinstance(b, int) and b + j == 0:
                        pool.wait_ge(p3_ready, 2)
                        init_stack(1)

                if not rope_job:
                    extras += [(second_stack, 2, (14, 1))]
                    extras += [(lambda b, j: rsqrt(b + j, fln_step, frstd_ready), -1, (20, 1))]
                    extras += [(lambda b, j, n=n: first_ln(b, j, n), 2, (17 + 8 * n, 1)) for n in range(2)]
                else:
                    rsqrt(ln_index(base, 0))
                round_ = 1 if rope_job else 0

                def expert_rows(b, j, n):
                    if j == jobs - 1:
                        rsqrt(ln_exp(round_, round_ * JOBS) if n else ln_final(0))
                for n in range(round_, 2):
                    extras += [(lambda b, j, n=n: expert_rows(b, j, n), -1, (26 if n else 3, 1))]
                iterations(pool, base, jobs, None, None, extras)

            def experts(round_):
                def rows(M):
                    if round_ == 0:
                        rsqrt(ln_final(M))
                    rsqrt(ln_exp(round_, M))

                def job(M, last):
                    pool.wait_ge(route_step, 22 * M + 2)
                    g.tensor_tensor(s4[:, 1, :], s4[:, 0, :], half[:], ALU.pow).then_inc(route_pow, 1)
                    pool.wait_ge(route_step, 22 * M + 20)
                    g.tensor_tensor(s8[:, 5, :, :], s8[:, 4, :, :],
                                    half[:].unsqueeze(2).broadcast_to([P, TT, E]), ALU.pow).then_inc(route_pow, 1)
                    if not last:
                        rows(M + 1)
                M0 = round_ * JOBS
                job(M0, False)
                job(M0 + 1, False)
                with pool.Fori(0, 2) as it:
                    _plain(pool)
                    job(M0 + 2 + it * 2, False)
                    job(M0 + 3 + it * 2, False)
                job(M0 + 6, False)
                job(M0 + 7, True)

            rsqrt(ln_index(0, 0))
            pool.wait_ge(c_step, 2)
            g.tensor_tensor(cn[:, 1, :], cn[:, 2, :], half[:, 0:1].broadcast_to([P, E]),
                            ALU.pow).then_inc(cproj_pow, 1)
            pool.wait_ge(rstd_ready, 2)
            pool.wait_ge(cproj_pow, 1)
            init_stack(0)
            attention(0, ENC, False)
            pool.wait_ge(x_added, 2 * ENC)
            for i in range(2):
                g.dma_start(QS[i][ROW_ALIBI:ROW_ALIBI + N_ALIBI, :, :], alibi[2]).then_inc(alibi_cleared, 16)
            experts(0)
            attention(ENC, JOBS, True)
            experts(1)

        @block.sync
        def _(sp):
            xv = x.rearrange("b (t p) d -> p (b t) d", p=P)
            ov = out.rearrange("b (t p) d -> p (b t) d", p=P)
            sp.dma_start(xs[:, 0:TT, :], xv[:, 0:TT, :]).then_inc(x_loaded[0], 16)
            for dst, src in ((ap_sb, apack[0]), (fp_sb, fpack[0])):
                sp.dma_start(dst[:], src).then_inc(apack_loaded if dst is ap_sb else fpack_loaded, 16)
            for dst, src in ((fin_sb, final), (bp_sb, bpack), (mp_sb, mpack), (b2_sb, b2e)):
                sp.dma_start(dst[:], src).then_inc(load_const, 16)
            sp.dma_start(xs[:, TT:, :], xv[:, TT:, :]).then_inc(x_loaded[1], 16)

            def attention(base, jobs, rope_job):
                def layer(b, j):
                    return (b + j) // JOBS if isinstance(b, int) else ((b + j) >> 3) & (LAYERS - 1)

                def load_front(b, j):
                    if j % 4 == 0:
                        sp.wait_ge(v_ready, b + j)
                        src = apack[bass.ds(layer(b, j), 1)].rearrange("a p n -> p (a n)")
                        sp.dma_start(ap_sb[:], src).then_inc(apack_loaded, 16)

                def load_rear(b, j):
                    if j % 4 == 0 and j > 0:
                        sp.wait_ge(f_added, 2 * (b + j))
                        src = fpack[bass.ds(layer(b, j), 1)].rearrange("a p n -> p (a n)")
                        sp.dma_start(fp_sb[:], src).then_inc(fpack_loaded, 16)

                def store(b, j):
                    for k in range(2):
                        sp.wait_ge(p3_ready, 2 * (b + j) + k + 1)
                        sp.dma_start(part_scr[j % 2, k].rearrange("a p t -> p a t"),
                                     parts[:, k, :, :]).then_inc(parts_stored, 16)

                def load(b, j, q):
                    if q == 0:
                        sp.wait_ge(parts_stored, 32 * (b + j + 1))
                        if isinstance(b, int) and b == 0 and j < 2:
                            sp.wait_ge(alibi_loaded[j], 32)
                    if j >= 2:
                        sp.wait_ge(b_ready, CHUNKS * (b + j - 2) + CPQ * (q + 1))
                    heads = slice(q * 4 * T, (q + 1) * 4 * T)
                    for n in range(NPART):
                        src = part_scr[j % 2, 0, n].rearrange("(d h) t -> d (h t)", d=HD)[:, heads]
                        sp.dma_start(QS[j % 2][n * 24:(n + 1) * 24, 4 * q:4 * q + 4, :],
                                     src.unsqueeze(0).broadcast_to([NPART, HD, 4 * T])).then_inc(stack_loaded[q], 16)
                        src = part_scr[j % 2, 1].rearrange("a (d h) t -> (a d) (h t)", d=HD)[:, heads]
                        sp.dma_start(KS[j % 2][n * 24:(n + 1) * 24, 4 * q:4 * q + 4, :],
                                     src).then_inc(stack_loaded[q], 16)

                def load_max(b, j):
                    sp.wait_ge(mT_ready, b + j + 1)
                    for a in range(NPART):
                        sp.dma_start(QS[j % 2][ROW_MAX + a:ROW_MAX + a + 1, :, :],
                                     mT[a * H:(a + 1) * H, :]).then_inc(m_loaded, 16)

                extras = [(store, 2, (14, 1)), (lambda b, j: load(b, j, 0), 2, (15, 1)),
                          (lambda b, j: load(b, j, 1), 2, (20, 1)), (load_max, 1, (33 if rope_job else 35, 1)),
                          (lambda b, j: load(b, j, 2), 2, (36, 1)), (lambda b, j: load(b, j, 3), 2, (39, 1))]
                if not rope_job:
                    extras += [(load_front, 3, (16, 1)), (load_rear, -1, (2, 1))]
                iterations(sp, base, jobs, None, None, extras)

            attention(0, ENC, False)
            def load_experts(jobs):
                sp.wait_ge(pv_done, QUADS * jobs - 1)
                sp.dma_start(big[:, 0:4096], w1e).then_inc(mw_loaded[0], 16)
                sp.wait_ge(pv_done, QUADS * jobs)
                sp.dma_start(big[:, 4096:8192], w2e).then_inc(mw_loaded[1], 16)

            sp.wait_ge(p3_ready, 2 * ENC)
            for j in range(JOBS):
                if j == 2:
                    load_experts(ENC)
                if j >= 2:
                    sp.wait_ge(fin_step, 3 * (j - 1))
                sp.dma_start(xload[:, j % 2, :, :], xv[:, j * TT:(j + 1) * TT, :]).then_inc(xr_loaded[j % 2], 16)
            sp.wait_ge(ey_used, E * JOBS)
            sp.dma_start(rope_sb, rope).then_inc(rope_loaded, 16)
            sp.wait_ge(alibi_cleared, 32)
            attention(ENC, JOBS, True)
            load_experts(ENC + JOBS)
            for j in range(JOBS):
                sp.wait_ge(out_ready, j + 1)
                sp.dma_start(ov[:, j * TT:(j + 1) * TT, :], xs[:, j * TT:(j + 1) * TT, :]).then_inc(stored, 16)
            sp.wait_ge(stored, 16 * JOBS)


def kernel(**inputs):
    import concourse.bacc as _bacc
    from concourse.bass_utils import run_bass_kernel_spmd as _run

    a = {k[3:] if k.startswith("L0_") else k: np.asarray(v) for k, v in inputs.items()}
    f = np.float32
    dh = np.arange(D).reshape(H, HD).T.reshape(-1)
    swap = (np.arange(D) ^ 1)[dh]

    def rep(v):
        return np.broadcast_to(v[..., None, :], (*v.shape[:-1], P, v.shape[-1]))

    wi = a["attn_a_in_proj_w"].reshape(LAYERS, 3, D, D)
    bi = a["attn_a_in_proj_b"].reshape(LAYERS, 3, D)
    T21 = (0, 2, 1)
    apack = np.concatenate([
        wi[:, 0][:, dh].transpose(T21), wi[:, 1][:, dh].transpose(T21), wi[:, 2].transpose(T21),
        rep(bi[:, 2]), a["attn_a_ln1_w"][:, :, None], a["attn_a_ln1_b"][:, :, None],
        bi[:, 0][:, dh][:, :, None], bi[:, 1][:, dh][:, :, None]], axis=2)
    fpack = np.concatenate([
        a["attn_a_ffn1_w"].transpose(T21),
        a["attn_a_ffn2_w"].reshape(LAYERS, D, FT, P).transpose(0, 3, 2, 1).reshape(LAYERS, P, FT * D),
        rep(a["attn_a_ffn2_b"]), a["attn_a_out_proj_w"].transpose(T21), rep(a["attn_a_out_proj_b"]),
        a["attn_a_ln2_w"][:, :, None], a["attn_a_ln2_b"][:, :, None],
        a["attn_a_ffn1_b"].reshape(LAYERS, FT, P).transpose(T21)], axis=2)
    final = np.concatenate([rep(a["attn_a_final_w"]), rep(a["attn_a_final_b"])], axis=1)
    wq, wk = a["attn_b_W_q"], a["attn_b_W_k"]
    bpack = np.concatenate([wq[dh].T, wq[swap].T, wk[dh].T, wk[swap].T, a["attn_b_W_v"].T, a["attn_b_W_o"].T], axis=1)
    mpack = np.concatenate([a["ffn_centroids"].T, a["ffn_Wp"], a["ffn_bp"][:, None],
                            a["ffn_b1"].reshape(E, FT, P).transpose(2, 0, 1).reshape(P, E * FT)], axis=1)
    w1e = a["ffn_W1"].transpose(1, 0, 2).reshape(P, E * T)
    w2e = a["ffn_W2"].reshape(E, FT, P, D).transpose(2, 0, 1, 3).reshape(P, E * FT * D)

    def part(v):
        return (v.view(np.uint32) & np.uint32(0xFFFF0000)).view(f)
    slopes = ((2.0 ** -0.5) ** np.arange(1, H + 1)).astype(f)
    s1 = part(slopes)
    s2 = part(slopes - s1)
    s3 = slopes - s1 - s2
    pos = np.arange(T)
    hi, lo = (pos // 8 * 8).astype(f), (pos % 8).astype(f)
    alibi = np.zeros((3, N_ALIBI, H, T), f)
    for n, s in enumerate((s1, s2, s3)):
        for m, p in enumerate((hi, lo)):
            r = 2 * n + m
            alibi[0, r], alibi[1, r] = s[:, None], p[None]
            alibi[0, 6 + r], alibi[1, 6 + r] = p[None], -s[:, None]
    at = np.minimum(pos, 255).astype(f)
    theta = (10000.0 ** (-2.0 * np.arange(HD // 2, dtype=f) / HD)).astype(f)
    ang = at[None, :] * theta[:, None]
    cos, sin = np.cos(ang).astype(f), np.sin(ang).astype(f)
    dim = np.repeat(np.arange(HD), H)
    C, S = cos[dim // 2], sin[dim // 2] * np.where(dim % 2 == 0, -1, 1)[:, None].astype(f)
    r8 = f(1.0 / math.sqrt(HD))
    rope = np.stack([C * r8, S * r8, C, S], axis=1).astype(f)

    arrays = dict(x=a["attn_a_x"], apack=apack, fpack=fpack, final=final, bpack=bpack, mpack=mpack,
                  b2e=a["ffn_b2"], w1e=w1e, w2e=w2e, alibi=alibi, rope=rope)
    arrays = {f"in_{k}": np.ascontiguousarray(v) for k, v in arrays.items()}
    nc = _bacc.Bacc("TRN2", target_bir_lowering=False, num_devices=1)
    args = [nc.dram_tensor(k, v.shape, F32, kind="ExternalInput").ap() for k, v in arrays.items()]
    out = nc.dram_tensor("out_x", [JOBS, T, D], F32, kind="ExternalOutput").ap()
    part_scr = nc.dram_tensor("part_scr", [2, 2, NPART, P, T], BF16, kind="Internal").ap()
    hybrid_kernel(nc, *args, out, part_scr)
    r = _run(nc, [arrays], core_ids=[0])
    return r.results[0]["out_x"]
```
